# Optimizing a Trainium2 kernel written in Bass

```python
import numpy as np
import jax
import jax.numpy as jnp

def _softmax(x, axis=-1):
    return jax.nn.softmax(x, axis=axis)

def _gelu(x):
    return jax.nn.gelu(x, approximate=True)

def _silu(x):
    return jax.nn.silu(x)

def _sigmoid(x):
    return jax.nn.sigmoid(x)

def _layernorm(x, axis=-1, eps=1e-05):
    m = jnp.mean(x, axis=axis, keepdims=True)
    v = jnp.var(x, axis=axis, keepdims=True)
    return (x - m) / jnp.sqrt(v + eps)

def _scatter_add(tgt, idx, src, axis=0):
    return tgt.at[idx].add(src)

def _segment_sum(src, seg, n):
    return jax.ops.segment_sum(src, seg, n)
kernel_name = 'mk_flamingo_gated_d2_seqx_r4_b24d50'

def setup_inputs(seed: int=0):
    np.random.seed(seed)
    _w = jnp.asarray

    def _rec_inputs():
        import jax
        import jax.numpy as jnp
        _rk = jax.random.key(seed)
        x = -0.0005207 + 1.001 * jax.random.normal(jax.random.fold_in(_rk, 1), (8, 112, 1024), jnp.float32)
        _lenS = 112 - jax.random.randint(jax.random.fold_in(_rk, 7), (8,), 0, max(1, 112 // 4) + 1, jnp.int32)
        _lenS2 = 375 - jax.random.randint(jax.random.fold_in(_rk, 8), (8,), 0, max(1, 375 // 4) + 1, jnp.int32)
        _ctx_4096P = jax.random.normal(jax.random.fold_in(_rk, 11), (8, 16, 1024), jnp.float32)
        _ctx_4096c = jax.random.dirichlet(jax.random.fold_in(_rk, 511), 0.3 * jnp.ones((16,), jnp.float32), (8, 375))
        _ctx_4096t = jnp.einsum('bsk,bkd->bsd', _ctx_4096c, _ctx_4096P)
        _ctx_4096t = _ctx_4096t * jax.lax.rsqrt(jnp.mean(jnp.square(_ctx_4096t)) + 1e-12) * 0.953939
        ctx_4096 = -0.00010331 + 0.999899 * (_ctx_4096t + 0.3 * jax.random.normal(jax.random.fold_in(_rk, 611), (8, 375, 1024), jnp.float32))
        _g = jax.random.normal(jax.random.fold_in(_rk, 9001), (2, 2), jnp.float32)
        _g = jnp.sign(_g) * jnp.maximum(jnp.abs(_g), 1.0) + (_g == 0) * 1.0
        g_xattn = _g[0]
        g_ffn = _g[1]
        return (x, ctx_4096, g_xattn, g_ffn)
    x, ctx_4096, g_xattn, g_ffn = _rec_inputs()

    def _L0_xattn_setup():
        import jax, jax.numpy as jnp
        import numpy as np
        HEADS = 32
        KV_HEADS = 8
        HEAD_DIM = 128
        EPS = 1e-06

        def rms_norm(x, w):
            var = jnp.mean(jnp.square(x.astype(jnp.float32)), axis=-1, keepdims=True)
            return (x.astype(jnp.float32) * jax.lax.rsqrt(var + EPS)).astype(x.dtype) * w
        key = jax.random.key(seed)
        ks = jax.random.split(key, 6)
        bsz, n_lat, seq, hidden = (8, 64, 1024, 1024)
        return {'latents': jax.random.normal(ks[0], (bsz, n_lat, hidden), jnp.float32), 'context': jax.random.normal(ks[1], (bsz, seq, hidden), jnp.float32), 'Wq': jax.random.normal(ks[2], (hidden, HEADS * HEAD_DIM), jnp.float32) * 0.02, 'Wk': jax.random.normal(ks[3], (hidden, KV_HEADS * HEAD_DIM), jnp.float32) * 0.02, 'Wv': jax.random.normal(ks[4], (hidden, KV_HEADS * HEAD_DIM), jnp.float32) * 0.02, 'Wo': jax.random.normal(ks[5], (HEADS * HEAD_DIM, hidden), jnp.float32) * 0.02, 'q_norm_w': jnp.ones((HEAD_DIM,), jnp.float32), 'k_norm_w': jnp.ones((HEAD_DIM,), jnp.float32)}
    _L0_xattn_all = _L0_xattn_setup()
    _L0_xattn_in = {k: v for k, v in _L0_xattn_all.items() if k in ('Wq', 'Wk', 'Wv', 'Wo', 'q_norm_w', 'k_norm_w')}
    del _L0_xattn_all

    def _L0_ffn_setup():
        import jax, jax.numpy as jnp
        import numpy as np
        FP8_MAX = 448.0
        EPS = 1e-12
        key = jax.random.key(seed)
        kx, kw = jax.random.split(key)
        x = jax.random.normal(kx, (8, 512, 1024), dtype=jnp.float32)
        weight = jax.random.normal(kw, (1024, 1024), dtype=jnp.float32) * 0.02
        return {'x': x, 'weight': weight}
    _L0_ffn_all = _L0_ffn_setup()
    _L0_ffn_in = {k: v for k, v in _L0_ffn_all.items() if k in ('weight',)}
    del _L0_ffn_all

    def _L1_xattn_setup():
        import jax, jax.numpy as jnp
        import numpy as np
        B, Q, D = (8, 64, 1024)
        CTX = 1024
        H, KV, HD = (16, 4, 96)
        G = H // KV
        key = jax.random.key(seed)
        ks = jax.random.split(key, 6)
        s = 0.02
        return {'latents': jax.random.normal(ks[0], (B, Q, D), jnp.float32), 'context': jax.random.normal(ks[1], (B, CTX, D), jnp.float32), 'Wq': jax.random.normal(ks[2], (H * HD, D), jnp.float32) * s, 'Wk': jax.random.normal(ks[3], (KV * HD, D), jnp.float32) * s, 'Wv': jax.random.normal(ks[4], (KV * HD, D), jnp.float32) * s, 'Wo': jax.random.normal(ks[5], (D, H * HD), jnp.float32) * s}
    _L1_xattn_all = _L1_xattn_setup()
    _L1_xattn_in = {k: v for k, v in _L1_xattn_all.items() if k in ('Wq', 'Wk', 'Wv', 'Wo')}
    del _L1_xattn_all

    def _L1_ffn_setup():
        import jax, jax.numpy as jnp
        import numpy as np
        ALPHA = 32
        R = 16
        SCALING = ALPHA / R
        key = jax.random.key(seed)
        k1, k2, k3, k4 = jax.random.split(key, 4)
        B_, S, D = (4, 512, 1024)
        H, r, O = (8, R, 1024)
        x = jax.random.normal(k1, (B_, S, D), dtype=jnp.float32)
        A = jax.random.normal(k2, (H, r, D), dtype=jnp.float32) * 0.02
        Bm = jax.random.normal(k3, (H, O, r), dtype=jnp.float32) * 0.02
        Wr = jax.random.normal(k4, (H, D), dtype=jnp.float32) * 0.02
        br = jnp.zeros((H,), dtype=jnp.float32)
        return {'x': x, 'A': A, 'B': Bm, 'Wr': Wr, 'br': br}
    _L1_ffn_all = _L1_ffn_setup()
    _L1_ffn_in = {k: v for k, v in _L1_ffn_all.items() if k in ('A', 'B', 'Wr', 'br')}
    del _L1_ffn_all
    return {'x': x, 'ctx_4096': ctx_4096, 'g_xattn': g_xattn, 'g_ffn': g_ffn, 'L0_xattn_Wq': _L0_xattn_in['Wq'], 'L0_xattn_Wk': _L0_xattn_in['Wk'], 'L0_xattn_Wv': _L0_xattn_in['Wv'], 'L0_xattn_Wo': _L0_xattn_in['Wo'], 'L0_xattn_q_norm_w': _L0_xattn_in['q_norm_w'], 'L0_xattn_k_norm_w': _L0_xattn_in['k_norm_w'], 'L0_ffn_weight': _L0_ffn_in['weight'], 'L1_xattn_Wq': _L1_xattn_in['Wq'], 'L1_xattn_Wk': _L1_xattn_in['Wk'], 'L1_xattn_Wv': _L1_xattn_in['Wv'], 'L1_xattn_Wo': _L1_xattn_in['Wo'], 'L1_ffn_A': _L1_ffn_in['A'], 'L1_ffn_B': _L1_ffn_in['B'], 'L1_ffn_Wr': _L1_ffn_in['Wr'], 'L1_ffn_br': _L1_ffn_in['br']}

def reference(x, ctx_4096, g_xattn, g_ffn, L0_xattn_Wq, L0_xattn_Wk, L0_xattn_Wv, L0_xattn_Wo, L0_xattn_q_norm_w, L0_xattn_k_norm_w, L0_ffn_weight, L1_xattn_Wq, L1_xattn_Wk, L1_xattn_Wv, L1_xattn_Wo, L1_ffn_A, L1_ffn_B, L1_ffn_Wr, L1_ffn_br):
    import jax
    import jax.numpy as jnp

    def _L0_xattn_ref(latents, context, Wq, Wk, Wv, Wo, q_norm_w, k_norm_w):
        import jax, jax.numpy as jnp
        import numpy as np
        HEADS = 32
        KV_HEADS = 8
        HEAD_DIM = 128
        EPS = 1e-06

        def rms_norm(x, w):
            var = jnp.mean(jnp.square(x.astype(jnp.float32)), axis=-1, keepdims=True)
            return (x.astype(jnp.float32) * jax.lax.rsqrt(var + EPS)).astype(x.dtype) * w
        bsz, q_len, hidden = latents.shape
        kv = jnp.concatenate([context, latents], axis=1)
        kv_len = kv.shape[1]
        groups = HEADS // KV_HEADS
        q = (latents @ Wq).reshape(bsz, q_len, HEADS, HEAD_DIM).transpose(0, 2, 1, 3)
        k = (kv @ Wk).reshape(bsz, kv_len, KV_HEADS, HEAD_DIM).transpose(0, 2, 1, 3)
        v = (kv @ Wv).reshape(bsz, kv_len, KV_HEADS, HEAD_DIM).transpose(0, 2, 1, 3)
        q = rms_norm(q, q_norm_w)
        k = rms_norm(k, k_norm_w)
        qg = q.reshape(bsz, KV_HEADS, groups, q_len, HEAD_DIM)
        scale = 1.0 / np.sqrt(HEAD_DIM)
        scores = jnp.einsum('bhgqd,bhkd->bhgqk', qg, k) * scale
        probs = jax.nn.softmax(scores.astype(jnp.float32), axis=-1).astype(q.dtype)
        out = jnp.einsum('bhgqk,bhkd->bhgqd', probs, v)
        out = out.reshape(bsz, HEADS, q_len, HEAD_DIM).transpose(0, 2, 1, 3)
        out = out.reshape(bsz, q_len, HEADS * HEAD_DIM)
        return out @ Wo

    def _L0_ffn_ref(x, weight):
        import jax, jax.numpy as jnp
        import numpy as np
        FP8_MAX = 448.0
        EPS = 1e-12
        B, S, K = x.shape
        N = weight.shape[1]
        x2 = x.reshape(-1, K)
        x_scale = FP8_MAX / jnp.maximum(jnp.max(jnp.abs(x2)), EPS)
        w_scale = FP8_MAX / jnp.maximum(jnp.max(jnp.abs(weight)), EPS)
        x_sim = jnp.clip(x2 * x_scale, -FP8_MAX, FP8_MAX)
        w_sim = jnp.clip(weight * w_scale, -FP8_MAX, FP8_MAX)
        out = x_sim @ w_sim * (1.0 / (x_scale * w_scale))
        return out.reshape(B, S, N)

    def _L1_xattn_ref(latents, context, Wq, Wk, Wv, Wo):
        import jax, jax.numpy as jnp
        import numpy as np
        B, Q, D = (8, 64, 1024)
        CTX = 1024
        H, KV, HD = (16, 4, 96)
        G = H // KV
        b, q_len, _ = latents.shape
        hidden = jnp.concatenate([context, latents], axis=1)
        s_len = hidden.shape[1]
        q = (latents @ Wq.T).reshape(b, q_len, H, HD)
        k = (hidden @ Wk.T).reshape(b, s_len, KV, HD)
        v = (hidden @ Wv.T).reshape(b, s_len, KV, HD)
        q = q.transpose(0, 2, 1, 3).reshape(b, KV, G, q_len, HD)
        k = k.transpose(0, 2, 1, 3)
        v = v.transpose(0, 2, 1, 3)
        scale = 1.0 / jnp.sqrt(jnp.asarray(HD, q.dtype))
        scores = jnp.einsum('bkgqd,bksd->bkgqs', q, k) * scale
        attn = jax.nn.softmax(scores.astype(jnp.float32), axis=-1).astype(q.dtype)
        out = jnp.einsum('bkgqs,bksd->bkgqd', attn, v)
        out = out.reshape(b, H, q_len, HD).transpose(0, 2, 1, 3).reshape(b, q_len, H * HD)
        return out @ Wo.T

    def _L1_ffn_ref(x, A, B, Wr, br):
        import jax, jax.numpy as jnp
        import numpy as np
        ALPHA = 32
        R = 16
        SCALING = ALPHA / R
        H = A.shape[0]
        router_logits = jnp.einsum('bsd,hd->bsh', x, Wr) + br
        scores = H * jax.nn.softmax(router_logits, axis=-1)
        low = jnp.einsum('bsd,hrd->bshr', x, A)
        out = jnp.einsum('bshr,hor,bsh->bso', low, B, scores)
        return SCALING * out
    x = x + jnp.tanh(g_xattn[0]) * _L0_xattn_ref(_layernorm(x, axis=-1), ctx_4096, L0_xattn_Wq, L0_xattn_Wk, L0_xattn_Wv, L0_xattn_Wo, L0_xattn_q_norm_w, L0_xattn_k_norm_w)
    x = x + jnp.tanh(g_ffn[0]) * _L0_ffn_ref(_layernorm(x, axis=-1), L0_ffn_weight)
    x = x + jnp.tanh(g_xattn[1]) * _L1_xattn_ref(_layernorm(x, axis=-1), ctx_4096, L1_xattn_Wq, L1_xattn_Wk, L1_xattn_Wv, L1_xattn_Wo)
    x = x + jnp.tanh(g_ffn[1]) * _L1_ffn_ref(_layernorm(x, axis=-1), L1_ffn_A, L1_ffn_B, L1_ffn_Wr, L1_ffn_br)
    return x

_drawn_inputs = setup_inputs


def setup_inputs(seed=0):
    import zlib

    import numpy as np

    out = dict(_drawn_inputs(seed))
    spreads = {'g_ffn': (-1.0, 0.6),
     'L0_xattn_q_norm_w': (1.0, 0.6),
     'L0_xattn_k_norm_w': (1.0, 0.6),
     'L1_ffn_br': (0.0, 0.376)}
    factors = {}
    for name, (base, spread) in spreads.items():
        noise = np.random.default_rng([zlib.crc32(name.encode()), seed]).standard_normal(out[name].shape)
        drawn = base * np.exp(spread * noise) if base else spread * noise
        out[name] = jnp.asarray(drawn.astype(out[name].dtype))
    for name, factor in factors.items():
        out[name] = (out[name] * factor).astype(out[name].dtype)
    return out
```

```python
from contextlib import ExitStack

import numpy as np

import concourse.bass as bass
from concourse import mybir

F32 = mybir.dt.float32
F32R = mybir.dt.float32r
ACT = mybir.ActivationFunctionType
ALU = mybir.AluOpType
AX = mybir.AxisListType

BATCH, QLEN, HID = 8, 112, 1024
CTX = 375
KVLEN = CTX + QLEN
KVPAD = KVLEN + 1
TOKENS = BATCH * QLEN
P = 128
TT = TOKENS // P
KS = HID // P
CT = 3
CR = CTX // CT
ROWS = [CR] * CT + [QLEN]
KVT = len(ROWS)
BANK = 512
G = 4



def f32(ap):
    return ap.bitcast(F32)


def product(pe, out, stat_hi, stat_lo, mov_hi, mov_lo, start, stop):
    pe.matmul(out, stat_hi, mov_hi, start=start, stop=False)
    pe.matmul(out, stat_hi, mov_lo, start=False, stop=False)
    return pe.matmul(out, stat_lo, mov_hi, start=False, stop=stop)


class Layer:

    def __init__(self, heads, kv_heads, dim, normed):
        self.heads, self.kvh, self.d, self.normed = heads, kv_heads, dim, normed
        self.cw = G * dim
        self.nkc = kv_heads // G
        self.units = BATCH * kv_heads
        self.scale = float(dim) ** -0.5


L0 = Layer(32, 8, 128, True)
L1 = Layer(16, 4, 96, False)


def flamingo(nc, x, ctx4096, g_xattn, g_ffn, wq0, wk0, wv0, wo0, qw0, kw0, wffn0,
             wq1, wk1, wv1, wo1, a1, b1, wr1, br1, out):
    stack = ExitStack()

    in_use = []

    def sem(name):
        in_use.append(nc.alloc_semaphore(name=name))
        return in_use[-1]

    def next_stage():
        nc.clear_and_free_semaphores(in_use)
        in_use.clear()
        nc.all_engine_barrier()

    def sb(st, name, shape, dt=F32):
        return st.enter_context(nc.sbuf_tensor(name, shape, dt))

    def ps(st, name, shape):
        return st.enter_context(nc.psum_tensor(name, shape, F32))

    def dram(name, shape, dt=F32):
        return nc.dram_tensor(name, shape, dt, kind="Internal").ap()

    x_rows = x.rearrange("b q h -> (b q) h")
    out_rows = out.rearrange("b q h -> (b q) h")
    ctx_rows = ctx4096.rearrange("b s h -> (b s) h")

    xn_d = dram("xn_d", (TOKENS, HID))
    scratch = {}
    for n, L in enumerate((L0, L1)):
        scratch[L] = (dram(f"qT{n}_d", (L.heads // G, L.d, 2, G, TOKENS)),
                      dram(f"kT{n}_d", (L.units, L.d, 2, KVLEN)),
                      dram(f"v{n}_d", (BATCH * KVLEN, 2, L.kvh * L.d)))
    wqT1, wkT1, wvT1 = (dram(f"{n}T1_d", (HID, w.shape[0])) for n, w in (("wq", wq1), ("wk", wk1), ("wv", wv1)))
    woT1 = dram("woT1_d", (L1.heads * L1.d, HID))
    aT1 = dram("aT1_d", (HID, P))
    bT1 = dram("bT1_d", (P, HID))
    wrT1 = dram("wrT1_d", (HID, 8))

    with stack:
        ident = sb(stack, "ident", [P, P])
        gates = sb(stack, "gates", [P, 4])
        eps5 = sb(stack, "eps5", [P, 1])
        eps6 = sb(stack, "eps6", [P, 1])
        qw = sb(stack, "qw", [P, 1])
        kw = sb(stack, "kw", [P, 1])
        brb = sb(stack, "brb", [P, 8])

        def constants():
            loaded, zeroed, diag, gated = sem("c_loaded"), sem("c_zeroed"), sem("c_diag"), sem("c_gated")
            with nc.Block() as block:
                @block.sync
                def _(sp):
                    sp.dma_start(gates[:, 0:2], g_xattn.rearrange("(a n) -> a n", a=1).broadcast_to([P, 2])).then_inc(loaded, 16)
                    sp.dma_start(gates[:, 2:4], g_ffn.rearrange("(a n) -> a n", a=1).broadcast_to([P, 2])).then_inc(loaded, 16)
                    sp.dma_start(qw[:], qw0.rearrange("(n a) -> n a", a=1)).then_inc(loaded, 16)
                    sp.dma_start(kw[:], kw0.rearrange("(n a) -> n a", a=1)).then_inc(loaded, 16)
                    sp.dma_start(brb[:], br1.rearrange("(a n) -> a n", a=1).broadcast_to([P, 8])).then_inc(loaded, 16)
                    sp.wait_ge(loaded, 80)

                @block.gpsimd
                def _(pool):
                    pool.memset(ident[:], 0.0).then_inc(zeroed, 1)
                    pool.memset(eps5[:], 1e-5)
                    pool.memset(eps6[:], 1e-6)
                    pool.wait_ge(zeroed, 1)
                    pool.affine_select(out=ident[:], in_=ident[:], compare_op=ALU.not_equal, fill=1.0,
                                       base=0, pattern=[[-1, P]], channel_multiplier=1).then_inc(diag, 1)
                    pool.wait_ge(diag, 1)

                @block.scalar
                def _(act):
                    act.wait_ge(loaded, 80)
                    act.activation(gates[:], gates[:], ACT.Tanh).then_inc(gated, 1)

                @block.vector
                def _(dve):
                    dve.wait_ge(loaded, 80)
                    dve.tensor_scalar(qw[:], qw[:], L0.scale, None, ALU.mult).then_inc(gated, 1)

        def transpose_weights():
            with ExitStack() as st:
                rows = sb(st, "tw_rows", [P, 2, 12 * P])
                cols = sb(st, "tw_cols", [P, 2, 12, P])
                banks = [ps(st, f"tw_ps{i}", [P, G, P]) for i in range(6)]
                loaded = [sem(f"tw_loaded{p}") for p in range(2)]
                turned, copied = sem("tw_turned"), sem("tw_copied")
                stored = [sem(f"tw_stored{p}") for p in range(2)]
                b1_rows = b1.rearrange("h o r -> o h r")
                jobs = [(wq1, wqT1, 12, P, 8), (wk1, wkT1, 3, P, 8), (wv1, wvT1, 3, P, 8),
                        (wo1, woT1, 8, P, 12), (b1_rows, bT1, 8, P, 1),
                        (a1.rearrange("h r d -> (h r) d"), aT1, 1, P, 8), (wr1, wrT1, 1, 8, 8)]

                def walk(eng, step):
                    done = [0, 0]
                    parts = 0
                    for job in jobs:
                        tiles, nb = job[2], job[4]
                        per = -(-nb // G)
                        pairs = tiles // 2
                        if pairs:
                            with eng.Fori(0, pairs) as i:
                                for p in range(2):
                                    step(job, 2 * i + p, p, i + done[p], parts + (2 * i + p) * per)
                            done = [done[0] + pairs, done[1] + pairs]
                            parts += 2 * pairs * per
                        if tiles % 2:
                            step(job, tiles - 1, 0, done[0], parts)
                            done[0] += 1
                            parts += per
                    return done

                with nc.Block() as block:
                    @block.sync
                    def _(sp):
                        def load(job, n, p, k, parts):
                            src, dst, tiles, r, nb = job
                            sp.wait_ge(stored[p], 16 * k)
                            if len(src.shape) == 3:
                                sp.dma_start(rows[0:r, p, 0:P].rearrange("p (h r) -> p h r", h=8),
                                             src[bass.ds(n * P, r), :, :]).then_inc(loaded[p], 16)
                            else:
                                sp.dma_start(rows[0:r, p, 0:nb * P], src[bass.ds(n * P, r), :] if tiles > 1 else src).then_inc(loaded[p], 16)
                        walk(sp, load)

                    @block.gpsimd
                    def _(pool):
                        def store(job, n, p, k, parts):
                            src, dst, tiles, r, nb = job
                            pool.wait_ge(copied, parts + -(-nb // G))
                            view = dst.rearrange("(b p) n -> p b n", p=P)
                            pool.dma_start(view[:, :, bass.ds(n * P, r)] if tiles > 1 else view,
                                           cols[:, p, 0:nb, 0:r]).then_inc(stored[p], 16)
                        done = walk(pool, store)
                        for p in range(2):
                            pool.wait_ge(stored[p], 16 * done[p])

                    @block.tensor
                    def _(pe):
                        def turn(job, n, p, k, parts):
                            r, nb = job[3], job[4]
                            pe.wait_ge(loaded[p], 16 * (k + 1))
                            for q in range(-(-nb // G)):
                                if q == 0:
                                    pe.wait_ge(stored[p], 16 * k)
                                for j in range(G * q, min(G * q + G, nb)):
                                    last = pe.transpose(banks[3 * p + q][:, j - G * q, 0:r],
                                                        rows[0:r, p, j * P:(j + 1) * P], ident[0:r, 0:r])
                                last.then_inc(turned, 1)
                        walk(pe, turn)

                    @block.scalar
                    def _(act):
                        def copy(job, n, p, k, parts):
                            r, nb = job[3], job[4]
                            for q in range(-(-nb // G)):
                                act.wait_ge(turned, parts + q + 1)
                                if q == 0:
                                    act.wait_ge(stored[p], 16 * k)
                                m = min(G, nb - G * q)
                                act.activation(cols[:, p, G * q:G * q + m, 0:r], banks[3 * p + q][:, 0:m, 0:r],
                                               ACT.Copy).then_inc(copied, 1)
                        walk(act, copy)

        def layer_norm(tag, x_sb, xn, source=None, to_dram=False):
            with ExitStack() as st:
                stats = sb(st, f"{tag}_stats", [P, TT, 2, 6])
                mv = sb(st, f"{tag}_mv", [P, TT, 2])
                rstd = sb(st, f"{tag}_rstd", [P, TT])
                loaded = [sem(f"{tag}_loaded{t}") for t in range(TT)]
                s_stats, s_mv, s_sd, s_rstd = (sem(f"{tag}_{n}") for n in ("s_stats", "s_mv", "s_sd", "s_rstd"))
                s_xn, stored = sem(f"{tag}_s_xn"), sem(f"{tag}_stored")
                with nc.Block() as block:
                    @block.sync
                    def _(sp):
                        if source is not None:
                            for t in range(TT):
                                sp.dma_start(x_sb[:, t, :], source[t * P:(t + 1) * P, :]).then_inc(loaded[t], 16)
                        if to_dram:
                            for t in range(TT):
                                sp.wait_ge(s_xn, t + 1)
                                sp.dma_start(xn_d[t * P:(t + 1) * P, :], xn[:, t, :]).then_inc(stored, 16)
                            sp.wait_ge(stored, 16 * TT)

                    @block.vector
                    def _(dve):
                        for t in range(TT):
                            if source is not None:
                                dve.wait_ge(loaded[t], 16)
                            for h in range(2):
                                dve.bn_stats(stats[:, t, h, :], x_sb[:, t, h * BANK:(h + 1) * BANK]).then_inc(s_stats, 1)
                        for t in range(TT):
                            dve.wait_ge(s_stats, 2 * t + 2)
                            dve.bn_aggr(mv[:, t, :], stats[:, t, :, :]).then_inc(s_mv, 1)
                        dve.wait_ge(s_sd, 1)
                        dve.reciprocal(rstd[:], rstd[:]).then_inc(s_rstd, 1)
                        dve.wait_ge(s_rstd, 1)
                        for t in range(TT):
                            dve.tensor_scalar(xn[:, t, :], x_sb[:, t, :], mv[:, t, 0:1], rstd[:, t:t + 1],
                                              ALU.subtract, ALU.mult).then_inc(s_xn, 1)

                    @block.scalar
                    def _(act):
                        act.wait_ge(s_mv, TT)
                        act.activation(rstd[:], mv[:, :, 1], ACT.Sqrt, bias=eps5[:]).then_inc(s_sd, 1)

        def transpose_rows(tag, xn, xt_hi, xt_lo):
            with ExitStack() as st:
                banks = [ps(st, f"{tag}_ps{i}", [P, G, P]) for i in range(4)]
                turned, hi_done, lo_done = (sem(f"{tag}_{n}") for n in ("turned", "hi", "lo"))
                parts = [(t, q) for t in range(TT) for q in range(KS // G)]
                with nc.Block() as block:
                    @block.tensor
                    def _(pe):
                        for n, (t, q) in enumerate(parts):
                            if n >= 4:
                                pe.wait_ge(lo_done, n - 3)
                            for j in range(G):
                                last = pe.transpose(banks[n % 4][:, j, :],
                                                    xn[:, t, (G * q + j) * P:(G * q + j + 1) * P], ident[:])
                            last.then_inc(turned, 1)

                    @block.scalar
                    def _(act):
                        for n, (t, q) in enumerate(parts):
                            act.wait_ge(turned, n + 1)
                            act.activation(xt_hi[:, G * q:G * q + G, t * P:(t + 1) * P], banks[n % 4][:],
                                           ACT.Copy).then_inc(hi_done, 1)

                    @block.vector
                    def _(dve):
                        for n, (t, q) in enumerate(parts):
                            dve.wait_ge(hi_done, n + 1)
                            cut = xt_hi[:, G * q:G * q + G, t * P:(t + 1) * P]
                            dve.tensor_tensor(xt_lo[:, G * q:G * q + G, t * P:(t + 1) * P], banks[n % 4][:],
                                              f32(cut), ALU.subtract).then_inc(lo_done, 1)

        def project(tag, L, w_cols, kinds, body, iters, tail, source, target):
            CW, D, C, T = L.cw, L.d, len(kinds), len(body)
            HK = KS // 2
            weight = qw if tag.startswith("q") else kw
            unit_scale = L.scale if tag.startswith("q") else 1.0
            order = []
            for c in range(C):
                order.append(("Y", c))
                if c == 0:
                    order.append(("X", 0))
                if c >= 2 and kinds[c - 2] == "T":
                    order.append(("K", c - 2))
            order += [("K", c) for c in range(max(C - 2, 0), C) if kinds[c] == "T"]
            n_turn = kinds.count("T")
            with ExitStack() as st:
                raw = sb(st, f"{tag}_raw", [P, 2, HK, CW])
                w_hi = sb(st, f"{tag}_whi", [P, C, KS, CW], F32R)
                w_lo = sb(st, f"{tag}_wlo", [P, C, KS, CW], F32R)
                xin = sb(st, f"{tag}_xin", [P, 2, HID])
                xt_hi = sb(st, f"{tag}_xthi", [P, 2, KS, P], F32R)
                xt_lo = sb(st, f"{tag}_xtlo", [P, 2, KS, P], F32R)
                sq = sb(st, f"{tag}_sq", [P, CW])
                inv = sb(st, f"{tag}_inv", [P, C, G])
                yn = sb(st, f"{tag}_yn", [P, 2, CW])
                stage = sb(st, f"{tag}_stage", [P, C, 2, BANK], F32R)
                y = [ps(st, f"{tag}_y{c}", [P, BANK]) for c in range(C)]
                xb = [ps(st, f"{tag}_xb{q}", [P, G, P]) for q in range(2)]
                tb = [ps(st, f"{tag}_tb{q}", [P, G, P]) for q in range(2)]

                raw_loaded = [sem(f"{tag}_rawl{h}") for h in range(2)]
                w_hi_done, w_lo_dve, w_lo_pool = (sem(f"{tag}_{n}") for n in ("whi_s", "wlo_dve", "wlo_pool"))
                x_loaded = [sem(f"{tag}_xl{p}") for p in range(2)]
                x_turned, x_hi_done, x_lo_done = (sem(f"{tag}_{n}") for n in ("xturn", "xhi_s", "xlo_s"))
                y_ready = sem(f"{tag}_yready")
                squared, summed, rooted, inverted = (sem(f"{tag}_{n}") for n in ("sq_s", "sum_s", "root_s", "inv_s"))
                normed = [sem(f"{tag}_norm{c}") for c in range(n_turn)]
                turned = [sem(f"{tag}_turned{c}") for c in range(n_turn)]
                s_hi_done = sem(f"{tag}_shi_s")
                staged = [sem(f"{tag}_staged{c}") for c in range(C)]
                stored = [sem(f"{tag}_stored{c}") for c in range(C)]
                y_read = [normed[c] if kinds[c] == "T" else staged[c] for c in range(C)]
                tail_of = [max((x for x in range(n_turn) if x % 2 == b), default=0) for b in range(2)]
                total = iters * T + len(tail)

                def walk(eng, step):
                    if iters:
                        with eng.Fori(0, iters) as i:
                            for j in range(T):
                                step(i, j, body[j], (body + tail)[j + 1])
                    for j in range(len(tail)):
                        step(iters, j, tail[j], tail[j + 1] if j + 1 < len(tail) else None)

                def stage_out(c, r):
                    if kinds[c] == "V":
                        return stage[0:r, c, :, 0:CW]
                    return stage[0:D, c, :, :].rearrange("p l (g s) -> p l g s", g=G)[:, :, :, 0:r]

                def t_index(n, c):
                    return n_turn * n + c

                with nc.Block() as block:
                    @block.sync
                    def _(sp):
                        sp.dma_start(xin[0:body[0], 0, :], source(0, 0)).then_inc(x_loaded[0], 16)
                        for c in range(C):
                            for h in range(2):
                                if c:
                                    sp.wait_ge(w_hi_done, KS * (c - 1) + HK * (h + 1))
                                    sp.wait_ge(w_lo_pool if h else w_lo_dve, HK * c)
                                sp.dma_start(raw[:, h, :, :], w_cols(c)[:, h * HK:(h + 1) * HK, :]).then_inc(raw_loaded[h], 16)

                        def step(i, j, r, r_next):
                            n = i * T + j
                            if r_next:
                                sp.wait_ge(x_turned, 2 * n)
                                jn = (i, j + 1) if j + 1 < T else (i + 1, 0)
                                sp.dma_start(xin[0:r_next, (j + 1) % 2, :], source(*jn)).then_inc(x_loaded[(j + 1) % 2], 16)
                            for kind, c in order:
                                if (kind == "K") or (kind == "Y" and kinds[c] == "V"):
                                    sp.wait_ge(staged[c], n + 1)
                                    for dst, src in target(c, i, j, stage_out(c, r)):
                                        sp.dma_start(dst, f32(src)).then_inc(stored[c], 16)
                        walk(sp, step)
                        for c in range(C):
                            sp.wait_ge(stored[c], 32 * total)

                    @block.gpsimd
                    def _(pool):
                        for c in range(C):
                            for k in range(HK, KS):
                                pool.wait_ge(w_hi_done, KS * c + k + 1)
                                pool.tensor_tensor(w_lo[:, c, k, :], raw[:, 1, k - HK, :], f32(w_hi[:, c, k, :]),
                                                   ALU.subtract).then_inc(w_lo_pool, 1)

                    @block.tensor
                    def _(pe):
                        def step(i, j, r, r_next):
                            n = i * T + j
                            p = j % 2
                            for kind, c in order:
                                if kind == "Y":
                                    pe.wait_ge(w_lo_dve, HK * (c + 1))
                                    pe.wait_ge(w_lo_pool, HK * (c + 1))
                                    pe.wait_ge(x_lo_done, 2 * n + 2)
                                    pe.wait_ge(y_read[c], n)
                                    for k in range(KS):
                                        last = product(pe, y[c][0:r, 0:CW], xt_hi[:, p, k, 0:r], xt_lo[:, p, k, 0:r],
                                                       w_hi[:, c, k, :], w_lo[:, c, k, :], k == 0, k == KS - 1)
                                    last.then_inc(y_ready, 1)
                                elif kind == "X" and r_next:
                                    pn = (j + 1) % 2
                                    pe.wait_ge(x_loaded[pn], 16 * (i * (T // 2) + (j + 1) // 2 + 1))
                                    for q in range(2):
                                        for m in range(G):
                                            k = G * q + m
                                            last = pe.transpose(xb[q][:, m, 0:r_next], xin[0:r_next, pn, k * P:(k + 1) * P], ident[0:r_next, 0:r_next])
                                        last.then_inc(x_turned, 1)
                                elif kind == "K":
                                    b = c % 2
                                    pe.wait_ge(normed[c], n + 1)
                                    if c >= 2:
                                        pe.wait_ge(staged[c - 2], n + 1)
                                    else:
                                        pe.wait_ge(staged[tail_of[b]], n)
                                    for m in range(G):
                                        last = pe.transpose(tb[b][0:D, m, 0:r], yn[0:r, c % 2, m * D:(m + 1) * D], ident[0:r, 0:r])
                                    last.then_inc(turned[c], 1)

                        pe.wait_ge(x_loaded[0], 16)
                        r = body[0]
                        for q in range(2):
                            for m in range(G):
                                k = G * q + m
                                last = pe.transpose(xb[q][:, m, 0:r], xin[0:r, 0, k * P:(k + 1) * P], ident[0:r, 0:r])
                            last.then_inc(x_turned, 1)
                        walk(pe, step)

                    @block.scalar
                    def _(act):
                        def x_highs(n, p, r):
                            for q in range(2):
                                act.wait_ge(x_turned, 2 * n + q + 1)
                                act.activation(xt_hi[:, p, G * q:G * q + G, 0:r], xb[q][:, :, 0:r], ACT.Copy).then_inc(x_hi_done, 1)

                        x_highs(0, 0, body[0])
                        for c in range(C):
                            for k in range(KS):
                                if k % HK == 0:
                                    act.wait_ge(raw_loaded[k // HK], 16 * (c + 1))
                                act.activation(w_hi[:, c, k, :], raw[:, k // HK, k % HK, :], ACT.Copy).then_inc(w_hi_done, 1)

                        def step(i, j, r, r_next):
                            n = i * T + j
                            for kind, c in order:
                                if kind == "Y":
                                    act.wait_ge(y_ready, C * n + c + 1)
                                    if kinds[c] == "V":
                                        act.wait_ge(stored[c], 32 * n)
                                        act.activation(stage[0:r, c, 0, 0:CW], y[c][0:r, 0:CW], ACT.Copy).then_inc(s_hi_done, 1)
                                    elif L.normed:
                                        act.wait_ge(summed, t_index(n, c))
                                        act.activation(sq[0:r, :], y[c][0:r, 0:CW], ACT.Square).then_inc(squared, 1)
                                        act.wait_ge(summed, t_index(n, c) + 1)
                                        act.activation(inv[0:r, c, :], inv[0:r, c, :], ACT.Sqrt, scale=1.0 / D, bias=eps6[0:r, :]).then_inc(rooted, 1)
                                    else:
                                        act.wait_ge(turned[c - 2 if c >= 2 else tail_of[c % 2]], n + 1 if c >= 2 else n)
                                        act.activation(yn[0:r, c % 2, :], y[c][0:r, 0:CW], ACT.Copy).then_inc(normed[c], 1)
                                elif kind == "X" and r_next:
                                    x_highs(n + 1, (j + 1) % 2, r_next)
                                elif kind == "K":
                                    b = c % 2
                                    act.wait_ge(turned[c], n + 1)
                                    act.wait_ge(stored[c], 32 * n)
                                    act.activation(stage_out(c, r)[:, 0, :, :], tb[b][0:D, :, 0:r], ACT.Copy,
                                                   scale=weight[0:D, :] if L.normed else unit_scale).then_inc(s_hi_done, 1)
                        walk(act, step)

                    hi_turn = {c: x for x, c in enumerate([c for kind, c in order if kind == "K" or (kind == "Y" and kinds[c] == "V")])}

                    @block.vector
                    def _(dve):
                        def x_lows(n, p, r):
                            for q in range(2):
                                dve.wait_ge(x_hi_done, 2 * n + q + 1)
                                dve.tensor_tensor(xt_lo[:, p, G * q:G * q + G, 0:r], xb[q][:, :, 0:r],
                                                  f32(xt_hi[:, p, G * q:G * q + G, 0:r]), ALU.subtract).then_inc(x_lo_done, 1)

                        x_lows(0, 0, body[0])
                        for c in range(C):
                            for k in range(HK):
                                dve.wait_ge(w_hi_done, KS * c + k + 1)
                                dve.tensor_tensor(w_lo[:, c, k, :], raw[:, 0, k, :], f32(w_hi[:, c, k, :]),
                                                  ALU.subtract).then_inc(w_lo_dve, 1)

                        def step(i, j, r, r_next):
                            n = i * T + j
                            for kind, c in order:
                                if kind == "Y" and kinds[c] == "V":
                                    dve.wait_ge(s_hi_done, C * n + hi_turn[c] + 1)
                                    dve.tensor_tensor(stage[0:r, c, 1, 0:CW], y[c][0:r, 0:CW], f32(stage[0:r, c, 0, 0:CW]),
                                                      ALU.subtract).then_inc(staged[c], 1)
                                elif kind == "Y" and L.normed:
                                    dve.wait_ge(squared, t_index(n, c) + 1)
                                    dve.tensor_reduce(inv[0:r, c, :], sq[0:r, :].rearrange("p (g d) -> p g d", g=G),
                                                      AX.X, ALU.add).then_inc(summed, 1)
                                    dve.wait_ge(rooted, t_index(n, c) + 1)
                                    dve.reciprocal(inv[0:r, c, :], inv[0:r, c, :]).then_inc(inverted, 1)
                                    dve.wait_ge(inverted, t_index(n, c) + 1)
                                    dve.wait_ge(turned[c - 2 if c >= 2 else tail_of[c % 2]], n + 1 if c >= 2 else n)
                                    dve.tensor_tensor(yn[0:r, c % 2, :].rearrange("p (g d) -> p g d", g=G),
                                                      y[c][0:r, 0:CW].rearrange("p (g d) -> p g d", g=G),
                                                      inv[0:r, c, :].unsqueeze(2).broadcast_to([r, G, D]), ALU.mult).then_inc(normed[c], 1)
                                elif kind == "X" and r_next:
                                    x_lows(n + 1, (j + 1) % 2, r_next)
                                elif kind == "K":
                                    b = c % 2
                                    dve.wait_ge(s_hi_done, C * n + hi_turn[c] + 1)
                                    dve.scalar_tensor_tensor(out=stage_out(c, r)[:, 1, :, :], in0=tb[b][0:D, :, 0:r],
                                                             scalar=weight[0:D, :] if L.normed else unit_scale,
                                                             in1=f32(stage_out(c, r)[:, 0, :, :]), op0=ALU.mult, op1=ALU.subtract).then_inc(staged[c], 1)
                        walk(dve, step)

        def attention(tag, L, oT):
            D, U = L.d, L.units
            qT_d, kT_d, v_d = scratch[L]
            GP = L.kvh // 2
            with ExitStack() as st:
                qs = sb(st, f"{tag}_q", [D, 2, 2, G * QLEN], F32R)
                ks = sb(st, f"{tag}_k", [D, 2, 2, KVPAD], F32R)
                vs = sb(st, f"{tag}_v", [P, 2, 2, KVT, D], F32R)
                pr = sb(st, f"{tag}_p", [QLEN, 2, G, KVPAD])
                nmax = sb(st, f"{tag}_nmax", [QLEN, 2, G])
                rsum = sb(st, f"{tag}_rsum", [QLEN, 2, G])
                rinv = sb(st, f"{tag}_rinv", [QLEN, 2, G])
                pt_hi = sb(st, f"{tag}_pthi", [P, KVT, G * QLEN], F32R)
                pt_lo = sb(st, f"{tag}_ptlo", [P, KVT, G * QLEN], F32R)
                s = [ps(st, f"{tag}_s{h}", [QLEN, BANK]) for h in range(G)]
                tb = [ps(st, f"{tag}_tb{b}", [P, G * QLEN]) for b in range(2)]
                o = [ps(st, f"{tag}_o{p}", [P, G * QLEN]) for p in range(2)]
                padded = sem(f"{tag}_padded")
                qk_loaded = [sem(f"{tag}_qkl{p}") for p in range(2)]
                v_loaded = [sem(f"{tag}_vl{p}") for p in range(2)]
                scored = [sem(f"{tag}_scored{h}") for h in range(G - 1)]
                qk_used = [sem(f"{tag}_qku{p}") for p in range(2)]
                exped = [sem(f"{tag}_exped{h}") for h in range(G)]
                maxed, inverted, normed = (sem(f"{tag}_{n}") for n in ("maxed", "inverted", "normed"))
                turned = [sem(f"{tag}_turned{x}") for x in range(KVT)]
                hi_done, lo_done = sem(f"{tag}_hi_s"), sem(f"{tag}_lo_s")
                multiplied = [sem(f"{tag}_mult{x}") for x in range(KVT - 1)]
                v_used = [sem(f"{tag}_vu{p}") for p in range(2)]
                o_read = [sem(f"{tag}_oread{p}") for p in range(2)]

                def walk(eng, step):
                    with eng.Fori(0, U // 2 - 1) as i:
                        step(i, 0, True)
                        step(i, 1, True)
                    step(U // 2 - 1, 0, True)
                    step(U // 2 - 1, 1, False)

                ORDER = ["S0", "S1", "T0", "S2", "T1", "V0", "S3", "T2", "V1", "T3", "V2", "V3"]

                with nc.Block() as block:
                    @block.sync
                    def _(sp):
                        with sp.Fori(0, BATCH) as b:
                            with sp.Fori(0, GP) as gp:
                                for p in range(2):
                                    half = b * GP + gp
                                    u = half * 2 + p
                                    sp.wait_ge(qk_used[p], half)
                                    for l in range(2):
                                        sp.dma_start(f32(qs[:, p, l, :]).rearrange("d (g s) -> d g s", g=G),
                                                     qT_d[gp * 2 + p, :, l, :, bass.ds(b * QLEN, QLEN)]).then_inc(qk_loaded[p], 16)
                                    sp.dma_start(f32(ks[:, p, :, 0:KVLEN]), kT_d[u, :, :, :]).then_inc(qk_loaded[p], 16)
                                    sp.wait_ge(v_used[p], half)
                                    for l in range(2):
                                        cols = bass.ds((gp * 2 + p) * D, D)
                                        sp.dma_start(f32(vs[0:CR, p, l, 0:CT, :]), v_d[bass.ds(b * KVLEN, CTX), l, cols].rearrange("(j r) d -> r j d", r=CR)).then_inc(v_loaded[p], 16)
                                        sp.dma_start(f32(vs[0:QLEN, p, l, CT, :]), v_d[bass.ds(b * KVLEN + CTX, QLEN), l, cols]).then_inc(v_loaded[p], 16)

                    @block.gpsimd
                    def _(pool):
                        pool.memset(f32(ks[:, :, :, KVLEN:KVPAD]), 0.0).then_inc(padded, 1)

                        def norm(p, h, u):
                            pool.wait_ge(inverted, 4 * u + h + 1)
                            pool.tensor_tensor(pr[:, p, h, 0:KVLEN], pr[:, p, h, 0:KVLEN],
                                               rinv[:, p, h:h + 1].broadcast_to([QLEN, KVLEN]), ALU.mult).then_inc(normed, 1)

                        with pool.Fori(0, U // 2) as i:
                            for p in range(2):
                                for h in range(G):
                                    norm(p, h, 2 * i + p)

                    @block.tensor
                    def _(pe):
                        def scores(p, h, half, u):
                            if h == 0:
                                pe.wait_ge(qk_loaded[p], 48 * (half + 1))
                            pe.wait_ge(exped[h], u)
                            last = product(pe, s[h][:, 0:KVPAD], qs[:, p, 0, h * QLEN:(h + 1) * QLEN], qs[:, p, 1, h * QLEN:(h + 1) * QLEN],
                                           ks[:, p, 0, :], ks[:, p, 1, :], True, True)
                            last.then_inc(scored[h] if h < G - 1 else qk_used[p], 1)

                        def step(i, p, more):
                            u = 2 * i + p
                            for what in ORDER:
                                x = int(what[1])
                                if what[0] == "S" and more:
                                    scores(1 - p, x, i + p, u + 1)
                                elif what[0] == "T":
                                    if x == 0:
                                        pe.wait_ge(normed, G * u + G)
                                    r = ROWS[x]
                                    for h in range(G):
                                        last = pe.transpose(tb[x % 2][0:r, h * QLEN:(h + 1) * QLEN], pr[:, p, h, x * CR:x * CR + r], ident[0:QLEN, 0:QLEN])
                                    last.then_inc(turned[x], 1)
                                elif what[0] == "V":
                                    r = ROWS[x]
                                    if x == 0:
                                        pe.wait_ge(v_loaded[p], 64 * (i + 1))
                                        pe.wait_ge(o_read[p], i)
                                    pe.wait_ge(lo_done, KVT * u + x + 1)
                                    last = product(pe, o[p][0:D, :], vs[0:r, p, 0, x, :], vs[0:r, p, 1, x, :],
                                                   pt_hi[0:r, x, :], pt_lo[0:r, x, :], x == 0, x == KVT - 1)
                                    last.then_inc(multiplied[x] if x < KVT - 1 else v_used[p], 1)

                        pe.wait_ge(padded, 1)
                        for h in range(G):
                            scores(0, h, 0, 0)
                        walk(pe, step)

                    @block.scalar
                    def _(act):
                        def exp(p, h, u, transposed):
                            act.wait_ge(maxed, G * u + h + 1)
                            if h == 0:
                                act.wait_ge(turned[KVT - 1], transposed)
                            act.activation(pr[:, p, h, 0:KVLEN], s[h][:, 0:KVLEN], ACT.Exp, bias=nmax[:, p, h:h + 1],
                                           accum_out=rsum[:, p, h:h + 1]).then_inc(exped[h], 1)

                        def step(i, p, more):
                            u = 2 * i + p
                            for what in ORDER:
                                x = int(what[1])
                                if what[0] == "S" and more:
                                    exp(1 - p, x, u + 1, u)
                                elif what[0] == "T":
                                    act.wait_ge(turned[x], u + 1)
                                    if x < KVT - 1:
                                        act.wait_ge(multiplied[x], u)
                                    else:
                                        act.wait_ge(v_used[1 - p], i + p)
                                    act.activation(pt_hi[0:ROWS[x], x, :], tb[x % 2][0:ROWS[x], :], ACT.Copy).then_inc(hi_done, 1)
                            if p == 0:
                                act.wait_ge(v_used[0], i + 1)
                                act.activation(oT[:, bass.ds(u, 1), :], o[0][0:D, :].unsqueeze(1), ACT.Copy).then_inc(o_read[0], 1)

                        for h in range(G):
                            exp(0, h, 0, 0)
                        walk(act, step)

                    @block.vector
                    def _(dve):
                        def neg_max(p, h, half, u):
                            if h < G - 1:
                                dve.wait_ge(scored[h], u + 1)
                            else:
                                dve.wait_ge(qk_used[p], half + 1)
                            dve.tensor_reduce(nmax[:, p, h:h + 1], s[h][:, 0:KVLEN], AX.X, ALU.max, negate=True).then_inc(maxed, 1)

                        def invert(p, h, u):
                            dve.wait_ge(exped[h], u + 1)
                            dve.reciprocal(rinv[:, p, h:h + 1], rsum[:, p, h:h + 1]).then_inc(inverted, 1)

                        def step(i, p, more):
                            u = 2 * i + p
                            for what in ORDER:
                                x = int(what[1])
                                if what[0] == "S" and more:
                                    neg_max(1 - p, x, i + p, u + 1)
                                    if x:
                                        invert(1 - p, x - 1, u + 1)
                                elif what[0] == "T":
                                    dve.wait_ge(hi_done, KVT * u + x + 1)
                                    dve.tensor_tensor(pt_lo[0:ROWS[x], x, :], tb[x % 2][0:ROWS[x], :], f32(pt_hi[0:ROWS[x], x, :]),
                                                      ALU.subtract).then_inc(lo_done, 1)
                                    if x == 2 and more:
                                        invert(1 - p, G - 1, u + 1)
                            if p == 1:
                                dve.wait_ge(v_used[1], i + 1)
                                dve.tensor_copy(oT[:, bass.ds(u, 1), :], o[1][0:D, :].unsqueeze(1)).then_inc(o_read[1], 1)

                        for h in range(G):
                            neg_max(0, h, 0, 0)
                            if h:
                                invert(0, h - 1, 0)
                        invert(0, G - 1, 0)
                        walk(dve, step)

        def out_project(tag, L, oT, wo, x_sb, gate, source=None):
            D, H = L.d, L.heads
            wo_v = wo.rearrange("(h d) n -> d h n", d=D)
            o_v = oT.rearrange("d (b g) (h s) -> d b g h s", b=BATCH, h=G)
            with ExitStack() as st:
                raw = sb(st, f"{tag}_raw", [D, 2, BANK])
                w_hi = sb(st, f"{tag}_whi", [D, 2, BANK], F32R)
                w_lo = sb(st, f"{tag}_wlo", [D, 2, BANK], F32R)
                o_hi = sb(st, f"{tag}_ohi", [D, 2, TOKENS], F32R)
                o_lo = sb(st, f"{tag}_olo", [D, 2, TOKENS], F32R)
                y = [ps(st, f"{tag}_y{t}", [P, BANK]) for t in range(TT)]
                x_loaded = sem(f"{tag}_xl")
                raw_loaded, wh_done, wl_done, oh_done, ol_done, used = (
                    [sem(f"{tag}_{n}{p}") for p in range(2)] for n in ("rawl", "wh", "wl", "oh", "ol", "used"))
                y_ready, y_read = sem(f"{tag}_yready"), sem(f"{tag}_yread")

                def walk(eng, step):
                    for half in range(2):
                        def group(g, first, last):
                            for h in range(G):
                                step(half, g, h, half * (H // 2) + 2 * g + h // 2, first and h == 0, last and h == G - 1)
                        group(0, True, False)
                        if L.kvh > 2:
                            with eng.Fori(1, L.kvh - 1) as g:
                                group(g, False, False)
                        group(L.kvh - 1, False, True)

                with nc.Block() as block:
                    @block.sync
                    def _(sp):
                        if source is not None:
                            sp.dma_start(x_sb[:], source.rearrange("(t p) n -> p t n", p=P)).then_inc(x_loaded, 16)

                        def step(half, g, h, m, first, last):
                            sp.wait_ge(wl_done[h % 2], m)
                            sp.dma_start(raw[:, h % 2, :], wo_v[:, g * G + h, half * BANK:(half + 1) * BANK]).then_inc(raw_loaded[h % 2], 16)
                        walk(sp, step)

                    @block.gpsimd
                    def _(pool):
                        def step(half, g, h, m, first, last):
                            p = h % 2
                            pool.wait_ge(wh_done[p], m + 1)
                            pool.tensor_tensor(w_lo[:, p, :], raw[:, p, :], f32(w_hi[:, p, :]), ALU.subtract).then_inc(wl_done[p], 1)
                        walk(pool, step)

                    @block.scalar
                    def _(act):
                        def step(half, g, h, m, first, last):
                            p = h % 2
                            act.wait_ge(used[p], m)
                            act.activation(o_hi[:, p, :].rearrange("d (b s) -> d b s", b=BATCH), o_v[:, :, g, h, :], ACT.Copy).then_inc(oh_done[p], 1)
                            act.wait_ge(raw_loaded[p], 16 * (m + 1))
                            act.activation(w_hi[:, p, :], raw[:, p, :], ACT.Copy).then_inc(wh_done[p], 1)
                        walk(act, step)

                    @block.tensor
                    def _(pe):
                        def step(half, g, h, m, first, last):
                            p = h % 2
                            pe.wait_ge(ol_done[p], m + 1)
                            pe.wait_ge(wl_done[p], m + 1)
                            for t in range(TT):
                                if first and half:
                                    pe.wait_ge(y_read, t + 1)
                                mm = product(pe, y[t][:], o_hi[:, p, t * P:(t + 1) * P], o_lo[:, p, t * P:(t + 1) * P],
                                             w_hi[:, p, :], w_lo[:, p, :], first, last)
                                if last and t < TT - 1:
                                    mm.then_inc(y_ready, 1)
                            mm.then_inc(used[p], 1)
                        walk(pe, step)

                    @block.vector
                    def _(dve):
                        if source is not None:
                            dve.wait_ge(x_loaded, 16)

                        def step(half, g, h, m, first, last):
                            p = h % 2
                            dve.wait_ge(oh_done[p], m + 1)
                            dve.tensor_tensor(o_lo[:, p, :].rearrange("d (b s) -> d b s", b=BATCH), o_v[:, :, g, h, :],
                                              f32(o_hi[:, p, :]).rearrange("d (b s) -> d b s", b=BATCH), ALU.subtract).then_inc(ol_done[p], 1)
                            if last:
                                for t in range(TT):
                                    if t < TT - 1:
                                        dve.wait_ge(y_ready, half * (TT - 1) + t + 1)
                                    else:
                                        dve.wait_ge(used[p], m + 1)
                                    cols = x_sb[:, t, half * BANK:(half + 1) * BANK]
                                    dve.scalar_tensor_tensor(out=cols, in0=y[t][:], scalar=gates[:, gate:gate + 1], in1=cols,
                                                             op0=ALU.mult, op1=ALU.add).then_inc(y_read, 1)
                        walk(dve, step)

        def scaled_ffn(x_sb):
            LIMIT = 448.0
            with ExitStack() as st:
                xt_hi = sb(st, "f0_xthi", [P, KS, TOKENS], F32R)
                xt_lo = sb(st, "f0_xtlo", [P, KS, TOKENS], F32R)
                w = sb(st, "f0_w", [P, KS, HID])
                most = sb(st, "f0_most", [P, 2])
                scl = sb(st, "f0_scl", [P, 3])
                with ExitStack() as st2:
                    xn = sb(st2, "f0_xn", [P, TT, HID])
                    loaded, maxed, reduced = sem("f0_loaded"), sem("f0_maxed"), sem("f0_reduced")
                    scaled, clipped, chain = sem("f0_scaled"), sem("f0_clipped"), sem("f0_chain")
                    layer_norm("f0_ln", x_sb, xn)
                    with nc.Block() as block:
                        @block.sync
                        def _(sp):
                            sp.dma_start(w[:], wffn0.rearrange("(k p) n -> p k n", p=P)).then_inc(loaded, 16)

                        @block.gpsimd
                        def _(pool):
                            pool.wait_ge(maxed, 2)
                            pool.partition_all_reduce(most[:], most[:], P, bass.bass_isa.ReduceOp.max).then_inc(reduced, 1)
                            pool.wait_ge(chain, 4)
                            for k in range(KS):
                                pool.tensor_scalar(w[:, k, :], w[:, k, :], scl[:, 1:2], LIMIT, ALU.mult, ALU.min).then_inc(scaled, 1)
                                pool.wait_ge(scaled, k + 1)
                                pool.tensor_scalar(w[:, k, :], w[:, k, :], -LIMIT, None, ALU.max).then_inc(clipped, 1)

                        @block.vector
                        def _(dve):
                            dve.tensor_reduce(most[:, 0:1], xn[:].rearrange("p t n -> p (t n)"), AX.X, ALU.max, apply_absolute_value=True).then_inc(maxed, 1)
                            dve.wait_ge(loaded, 16)
                            dve.tensor_reduce(most[:, 1:2], w[:].rearrange("p t n -> p (t n)"), AX.X, ALU.max, apply_absolute_value=True).then_inc(maxed, 1)
                            dve.wait_ge(reduced, 1)
                            dve.tensor_scalar(scl[:, 0:2], most[:], 1e-12, None, ALU.max).then_inc(chain, 1)
                            dve.wait_ge(chain, 1)
                            dve.reciprocal(scl[:, 0:2], scl[:, 0:2]).then_inc(chain, 1)
                            dve.wait_ge(chain, 2)
                            dve.tensor_scalar(scl[:, 0:2], scl[:, 0:2], LIMIT, None, ALU.mult).then_inc(chain, 1)
                            dve.wait_ge(chain, 3)
                            dve.tensor_tensor(scl[:, 2:3], scl[:, 0:1], scl[:, 1:2], ALU.mult).then_inc(chain, 1)
                            dve.wait_ge(chain, 4)
                            dve.reciprocal(scl[:, 2:3], scl[:, 2:3]).then_inc(chain, 1)
                            dve.wait_ge(chain, 5)
                            dve.tensor_tensor(scl[:, 2:3], scl[:, 2:3], gates[:, 2:3], ALU.mult).then_inc(chain, 1)
                            x_scaled = sem("f0_xscaled")
                            for t in range(TT):
                                dve.tensor_scalar(xn[:, t, :], xn[:, t, :], scl[:, 0:1], LIMIT, ALU.mult, ALU.min).then_inc(x_scaled, 1)
                            for t in range(TT):
                                dve.wait_ge(x_scaled, t + 1)
                                dve.tensor_scalar(xn[:, t, :], xn[:, t, :], -LIMIT, None, ALU.max)
                    transpose_rows("f0_tr", xn, xt_hi, xt_lo)

                w_hi = sb(st, "f0_whi", [P, KS, HID], F32R)
                w_lo = sb(st, "f0_wlo", [P, KS, HID], F32R)
                y = [ps(st, f"f0_y{n}", [P, BANK]) for n in range(4)]
                hi_done, lo_dve, lo_pool = sem("f0_hi"), sem("f0_lod"), sem("f0_lop")
                y_ready, y_read = sem("f0_yready"), sem("f0_yread")
                slabs = [(half, k) for half in range(2) for k in range(KS)]
                outs = [(half, t) for half in range(2) for t in range(TT)]

                def cut(ap, half, k):
                    return ap[:, k, half * BANK:(half + 1) * BANK]

                with nc.Block() as block:
                    @block.scalar
                    def _(act):
                        for half, k in slabs:
                            act.activation(cut(w_hi, half, k), cut(w, half, k), ACT.Copy).then_inc(hi_done, 1)

                    @block.gpsimd
                    def _(pool):
                        for n, (half, k) in enumerate(slabs):
                            if k % 2:
                                pool.wait_ge(hi_done, n + 1)
                                pool.tensor_tensor(cut(w_lo, half, k), cut(w, half, k), f32(cut(w_hi, half, k)), ALU.subtract).then_inc(lo_pool, 1)

                    @block.vector
                    def _(dve):
                        for n, (half, k) in enumerate(slabs):
                            if k % 2 == 0:
                                dve.wait_ge(hi_done, n + 1)
                                dve.tensor_tensor(cut(w_lo, half, k), cut(w, half, k), f32(cut(w_hi, half, k)), ALU.subtract).then_inc(lo_dve, 1)
                        for n, (half, t) in enumerate(outs):
                            dve.wait_ge(y_ready, n + 1)
                            cols = x_sb[:, t, half * BANK:(half + 1) * BANK]
                            dve.scalar_tensor_tensor(out=cols, in0=y[n % 4][:], scalar=scl[:, 2:3], in1=cols,
                                                     op0=ALU.mult, op1=ALU.add).then_inc(y_read, 1)

                    @block.tensor
                    def _(pe):
                        for n, (half, t) in enumerate(outs):
                            if n >= 4:
                                pe.wait_ge(y_read, n - 3)
                            for k in range(KS):
                                if t == 0:
                                    done = half * KS // 2 + k // 2 + 1
                                    pe.wait_ge(lo_pool if k % 2 else lo_dve, done)
                                mm = product(pe, y[n % 4][:], xt_hi[:, k, t * P:(t + 1) * P], xt_lo[:, k, t * P:(t + 1) * P],
                                             cut(w_hi, half, k), cut(w_lo, half, k), k == 0, k == KS - 1)
                            mm.then_inc(y_ready, 1)

        def routed_lora(x_sb):
            EX, RANK = 8, 16
            ER = EX * RANK
            NW = EX + ER
            FACTOR = 2.0 * EX
            with ExitStack() as st:
                xt_hi = sb(st, "f1_xthi", [P, KS, TOKENS], F32R)
                xt_lo = sb(st, "f1_xtlo", [P, KS, TOKENS], F32R)
                with ExitStack() as st2:
                    xn = sb(st2, "f1_xn", [P, TT, HID])
                    layer_norm("f1_ln", x_sb, xn)
                    transpose_rows("f1_tr", xn, xt_hi, xt_lo)
                wra = sb(st, "f1_wra", [P, KS, NW])
                wra_hi = sb(st, "f1_wrahi", [P, KS, NW], F32R)
                wra_lo = sb(st, "f1_wralo", [P, KS, NW], F32R)
                wb = sb(st, "f1_wb", [P, HID])
                wb_hi = sb(st, "f1_wbhi", [P, HID], F32R)
                wb_lo = sb(st, "f1_wblo", [P, HID], F32R)
                logit = sb(st, "f1_logit", [P, TT, EX])
                nmax = sb(st, "f1_nmax", [P, TT])
                tot = sb(st, "f1_tot", [P, TT])
                score = sb(st, "f1_score", [P, TT, EX])
                low = sb(st, "f1_low", [P, TT, ER])
                lt_hi = sb(st, "f1_lthi", [P, TT, P], F32R)
                lt_lo = sb(st, "f1_ltlo", [P, TT, P], F32R)
                ya = [ps(st, f"f1_ya{n}", [P, BANK]) for n in range(2)]
                tb = [ps(st, f"f1_tb{n}", [P, P]) for n in range(2)]
                yo = [ps(st, f"f1_yo{n}", [P, BANK]) for n in range(4)]
                names = ("loaded", "whi", "wlo", "aready", "chain", "exped", "low_s", "turned", "lthi_s", "ltlo_s", "oready", "added", "stored")
                loaded, whi, wlo, a_ready, chain, exped, lowed, turned, lt_hi_s, lt_lo_s, o_ready, added, stored = (sem("f1_" + n) for n in names)

                with nc.Block() as block:
                    @block.sync
                    def _(sp):
                        sp.dma_start(wra[:, :, 0:EX], wrT1.rearrange("(k p) n -> p k n", p=P)).then_inc(loaded, 16)
                        sp.dma_start(wra[:, :, EX:NW], aT1.rearrange("(k p) n -> p k n", p=P)).then_inc(loaded, 16)
                        sp.dma_start(wb[:], bT1).then_inc(loaded, 16)
                        for t in range(TT):
                            sp.wait_ge(added, 2 * t + 2)
                            sp.dma_start(out_rows[t * P:(t + 1) * P, :], x_sb[:, t, :]).then_inc(stored, 16)
                        sp.wait_ge(stored, 16 * TT)

                    @block.tensor
                    def _(pe):
                        pe.wait_ge(wlo, 2)

                        def up(t):
                            if t >= 2:
                                pe.wait_ge(lowed, t - 1)
                            for k in range(KS):
                                mm = product(pe, ya[t % 2][:, 0:NW], xt_hi[:, k, t * P:(t + 1) * P], xt_lo[:, k, t * P:(t + 1) * P],
                                             wra_hi[:, k, :], wra_lo[:, k, :], k == 0, k == KS - 1)
                            mm.then_inc(a_ready, 1)

                        def down(t):
                            pe.wait_ge(lowed, t + 1)
                            if t >= 2:
                                pe.wait_ge(lt_lo_s, t - 1)
                            pe.transpose(tb[t % 2][:], low[:, t, :], ident[:]).then_inc(turned, 1)
                            pe.wait_ge(lt_lo_s, t + 1)
                            for c in range(2):
                                n = 2 * t + c
                                if n >= 4:
                                    pe.wait_ge(added, n - 3)
                                product(pe, yo[n % 4][:], lt_hi[:, t, :], lt_lo[:, t, :], wb_hi[:, c * BANK:(c + 1) * BANK],
                                        wb_lo[:, c * BANK:(c + 1) * BANK], True, True).then_inc(o_ready, 1)
                        up(0)
                        for t in range(1, TT):
                            up(t)
                            down(t - 1)
                        down(TT - 1)

                    @block.scalar
                    def _(act):
                        act.wait_ge(loaded, 48)
                        act.activation(wra_hi[:], wra[:], ACT.Copy).then_inc(whi, 1)
                        act.activation(wb_hi[:], wb[:], ACT.Copy).then_inc(whi, 1)
                        for t in range(TT):
                            act.wait_ge(chain, 2 * t + 2)
                            act.activation(score[:, t, :], logit[:, t, :], ACT.Exp, bias=nmax[:, t:t + 1], accum_out=tot[:, t:t + 1]).then_inc(exped, 1)
                            act.wait_ge(turned, t + 1)
                            act.activation(lt_hi[:, t, :], tb[t % 2][:], ACT.Copy).then_inc(lt_hi_s, 1)

                    @block.vector
                    def _(dve):
                        dve.wait_ge(whi, 1)
                        dve.tensor_tensor(wra_lo[:], wra[:], f32(wra_hi[:]), ALU.subtract).then_inc(wlo, 1)
                        dve.wait_ge(whi, 2)
                        dve.tensor_tensor(wb_lo[:], wb[:], f32(wb_hi[:]), ALU.subtract).then_inc(wlo, 1)
                        scores_s = sem("f1_scores_s")
                        for t in range(TT):
                            dve.wait_ge(a_ready, t + 1)
                            dve.tensor_tensor(logit[:, t, :], ya[t % 2][:, 0:EX], brb[:], ALU.add).then_inc(chain, 1)
                            dve.wait_ge(chain, 2 * t + 1)
                            dve.tensor_reduce(nmax[:, t:t + 1], logit[:, t, :], AX.X, ALU.max, negate=True).then_inc(chain, 1)
                            dve.wait_ge(exped, t + 1)
                            dve.reciprocal(tot[:, t:t + 1], tot[:, t:t + 1]).then_inc(scores_s, 1)
                            dve.wait_ge(scores_s, 2 * t + 1)
                            dve.tensor_scalar(score[:, t, :], score[:, t, :], tot[:, t:t + 1], FACTOR, ALU.mult, ALU.mult).then_inc(scores_s, 1)
                            dve.wait_ge(scores_s, 2 * t + 2)
                            dve.tensor_tensor(low[:, t, :].rearrange("p (e r) -> p e r", e=EX), ya[t % 2][:, EX:NW].rearrange("p (e r) -> p e r", e=EX),
                                              score[:, t, :].unsqueeze(2).broadcast_to([P, EX, RANK]), ALU.mult).then_inc(lowed, 1)
                            dve.wait_ge(lt_hi_s, t + 1)
                            dve.tensor_tensor(lt_lo[:, t, :], tb[t % 2][:], f32(lt_hi[:, t, :]), ALU.subtract).then_inc(lt_lo_s, 1)
                            for c in range(2):
                                dve.wait_ge(o_ready, 2 * t + c + 1)
                                cols = x_sb[:, t, c * BANK:(c + 1) * BANK]
                                dve.scalar_tensor_tensor(out=cols, in0=yo[(2 * t + c) % 4][:], scalar=gates[:, 3:4], in1=cols,
                                                         op0=ALU.mult, op1=ALU.add).then_inc(added, 1)

        def columns(w, L):
            v = w.rearrange("(k p) n -> p k n", p=P)
            return [v[:, :, c * L.cw:(c + 1) * L.cw] for c in range(w.shape[1] // L.cw)]

        def project_queries(tag, L, wq, first):
            chunks = columns(wq, L)[first:first + 4]
            qT_d = scratch[L][0]

            def target(c, i, j, src):
                tok = bass.ds(i * (2 * P) + j * P, P)
                return [(qT_d[first + c, :, l, :, tok], src[:, l, :, :]) for l in range(2)]

            project(tag, L, lambda c: chunks[c], ["T"] * 4, [P, P], TT // 2, [P] * (TT % 2),
                    lambda i, j: xn_d[bass.ds((2 * i + j) * P, P), :], target)

        def project_keys_values(tag, L, wk, wv):
            chunks = columns(wk, L) + columns(wv, L)
            _, kT_d, v_d = scratch[L]

            def source(i, j):
                if j < CT:
                    return ctx_rows[bass.ds(i * CTX + j * CR, CR), :]
                return xn_d[bass.ds(i * QLEN, QLEN), :]

            def target(c, i, j, src):
                if c < L.nkc:
                    view = kT_d[bass.ds(i * L.kvh + c * G, G), :, :, j * CR:j * CR + ROWS[j]].rearrange("u d l s -> d l u s")
                    return [(view[:, l, :, :], src[:, l, :, :]) for l in range(2)]
                view = v_d[bass.ds(i * KVLEN + j * CR, ROWS[j]), :, (c - L.nkc) * L.cw:(c - L.nkc + 1) * L.cw]
                return [(view[:, l, :], src[:, l, :]) for l in range(2)]

            project(tag, L, lambda c: chunks[c], ["T"] * L.nkc + ["V"] * L.nkc, ROWS, BATCH - 1, ROWS, source, target)

        constants()
        transpose_weights()
        next_stage()
        with ExitStack() as st:
            x_tmp, xn = sb(st, "x_tmp", [P, TT, HID]), sb(st, "xn0", [P, TT, HID])
            layer_norm("a0_ln", x_tmp, xn, source=x_rows, to_dram=True)
        for n in range(L0.heads // G // 4):
            next_stage()
            project_queries(f"q0{n}", L0, wq0, 4 * n)
        next_stage()
        project_keys_values("kv0", L0, wk0, wv0)
        next_stage()
        x_sb = sb(stack, "x_sb", [P, TT, HID])
        with ExitStack() as st:
            oT = sb(st, "oT0", [L0.d, L0.units, G * QLEN])
            attention("at0", L0, oT)
            next_stage()
            out_project("o0", L0, oT, wo0, x_sb, 0, source=x_rows)
        next_stage()
        scaled_ffn(x_sb)
        next_stage()
        with ExitStack() as st:
            xn = sb(st, "xn1", [P, TT, HID])
            layer_norm("a1_ln", x_sb, xn, to_dram=True)
        project_queries("q1", L1, wqT1, 0)
        next_stage()
        project_keys_values("kv1", L1, wkT1, wvT1)
        next_stage()
        with ExitStack() as st:
            oT = sb(st, "oT1", [L1.d, L1.units, G * QLEN])
            attention("at1", L1, oT)
            next_stage()
            out_project("o1", L1, oT, woT1, x_sb, 1)
        next_stage()
        routed_lora(x_sb)


_INS = ["x", "ctx_4096", "g_xattn", "g_ffn", "L0_xattn_Wq", "L0_xattn_Wk", "L0_xattn_Wv", "L0_xattn_Wo",
        "L0_xattn_q_norm_w", "L0_xattn_k_norm_w", "L0_ffn_weight", "L1_xattn_Wq", "L1_xattn_Wk", "L1_xattn_Wv",
        "L1_xattn_Wo", "L1_ffn_A", "L1_ffn_B", "L1_ffn_Wr", "L1_ffn_br"]


def kernel(**inputs):
    import numpy as _np
    import concourse.bacc as _bacc
    from concourse import mybir as _mybir
    from concourse.bass_utils import run_bass_kernel_spmd as _run

    nc = _bacc.Bacc("TRN2", target_bir_lowering=False, num_devices=1)
    arrays, args = {}, []
    for name in _INS:
        a = _np.ascontiguousarray(inputs[name])
        arrays[f"in_{name}_dram"] = a
        args.append(nc.dram_tensor(f"in_{name}_dram", a.shape, _mybir.dt.from_np(a.dtype), kind="ExternalInput").ap())
    args.append(nc.dram_tensor("out_0_dram", (BATCH, QLEN, HID), _mybir.dt.float32, kind="ExternalOutput").ap())
    flamingo(nc, *args)
    r = _run(nc, [arrays], core_ids=[0])
    return r.results[0]["out_0_dram"]
```

```python
from contextlib import ExitStack

import numpy as np

import concourse.bass as bass
from concourse import mybir

F32 = mybir.dt.float32
F32R = mybir.dt.float32r
ACT = mybir.ActivationFunctionType
ALU = mybir.AluOpType
AX = mybir.AxisListType

BATCH, QLEN, HID = 8, 112, 1024
CTX = 375
KVLEN = CTX + QLEN
KVPAD = KVLEN + 1
TOKENS = BATCH * QLEN
P = 128
TT = TOKENS // P
KS = HID // P
CT = 3
CR = CTX // CT
ROWS = [CR] * CT + [QLEN]
KVT = len(ROWS)
BANK = 512
G = 4



def f32(ap):
    return ap.bitcast(F32)


def product(pe, out, stat_hi, stat_lo, mov_hi, mov_lo, start, stop):
    pe.matmul(out, stat_hi, mov_hi, start=start, stop=False)
    pe.matmul(out, stat_hi, mov_lo, start=False, stop=False)
    return pe.matmul(out, stat_lo, mov_hi, start=False, stop=stop)


class Layer:

    def __init__(self, heads, kv_heads, dim, normed):
        self.heads, self.kvh, self.d, self.normed = heads, kv_heads, dim, normed
        self.cw = G * dim
        self.nkc = kv_heads // G
        self.units = BATCH * kv_heads
        self.scale = float(dim) ** -0.5


L0 = Layer(32, 8, 128, True)
L1 = Layer(16, 4, 96, False)


def flamingo(nc, x, ctx4096, g_xattn, g_ffn, wq0, wk0, wv0, wo0, qw0, kw0, wffn0,
             wq1, wk1, wv1, wo1, a1, b1, wr1, br1, out):
    stack = ExitStack()

    in_use = []

    def sem(name):
        in_use.append(nc.alloc_semaphore(name=name))
        return in_use[-1]

    def next_stage():
        nc.clear_and_free_semaphores(in_use)
        in_use.clear()
        nc.all_engine_barrier()

    def sb(st, name, shape, dt=F32):
        return st.enter_context(nc.sbuf_tensor(name, shape, dt))

    def ps(st, name, shape):
        return st.enter_context(nc.psum_tensor(name, shape, F32))

    def dram(name, shape, dt=F32):
        return nc.dram_tensor(name, shape, dt, kind="Internal").ap()

    x_rows = x.rearrange("b q h -> (b q) h")
    out_rows = out.rearrange("b q h -> (b q) h")
    ctx_rows = ctx4096.rearrange("b s h -> (b s) h")

    xn_d = dram("xn_d", (TOKENS, HID))
    scratch = {}
    for n, L in enumerate((L0, L1)):
        scratch[L] = (dram(f"qT{n}_d", (L.kvh, L.d, G, TOKENS)),
                      dram(f"kT{n}_d", (L.units, L.d, KVLEN)),
                      dram(f"v{n}_d", (BATCH * KVLEN, L.kvh * L.d)),
                      dram(f"rT{n}_d", (BATCH, L.heads, QLEN)))

    with stack:
        ident = sb(stack, "ident", [P, P])
        gates = sb(stack, "gates", [P, 4])
        eps5 = sb(stack, "eps5", [P, 1])
        eps6 = sb(stack, "eps6", [P, 1])
        qw = sb(stack, "qw", [P, 1])
        kw = sb(stack, "kw", [P, 1])
        brb = sb(stack, "brb", [P, 8])

        def constants():
            loaded, zeroed, diag, gated = sem("c_loaded"), sem("c_zeroed"), sem("c_diag"), sem("c_gated")
            with nc.Block() as block:
                @block.sync
                def _(sp):
                    sp.dma_start(gates[:, 0:2], g_xattn.rearrange("(a n) -> a n", a=1).broadcast_to([P, 2])).then_inc(loaded, 16)
                    sp.dma_start(gates[:, 2:4], g_ffn.rearrange("(a n) -> a n", a=1).broadcast_to([P, 2])).then_inc(loaded, 16)
                    sp.dma_start(qw[:], qw0.rearrange("(n a) -> n a", a=1)).then_inc(loaded, 16)
                    sp.dma_start(kw[:], kw0.rearrange("(n a) -> n a", a=1)).then_inc(loaded, 16)
                    sp.dma_start(brb[:], br1.rearrange("(a n) -> a n", a=1).broadcast_to([P, 8])).then_inc(loaded, 16)
                    sp.wait_ge(loaded, 80)

                @block.gpsimd
                def _(pool):
                    pool.memset(ident[:], 0.0).then_inc(zeroed, 1)
                    pool.memset(eps5[:], 1e-5)
                    pool.memset(eps6[:], 1e-6)
                    pool.wait_ge(zeroed, 1)
                    pool.affine_select(out=ident[:], in_=ident[:], compare_op=ALU.not_equal, fill=1.0,
                                       base=0, pattern=[[-1, P]], channel_multiplier=1).then_inc(diag, 1)
                    pool.wait_ge(diag, 1)

                @block.scalar
                def _(act):
                    act.wait_ge(loaded, 80)
                    act.activation(gates[:], gates[:], ACT.Tanh).then_inc(gated, 1)

                @block.vector
                def _(dve):
                    dve.wait_ge(loaded, 80)
                    dve.tensor_scalar(qw[:], qw[:], L0.scale, None, ALU.mult).then_inc(gated, 1)

        def layer_norm(tag, x_sb, xn, xt_hi=None, xt_lo=None, source=None, to_dram=False, preload=()):
            turn = xt_hi is not None
            with ExitStack() as st:
                stats = sb(st, f"{tag}_stats", [P, TT, 2, 6])
                mv = sb(st, f"{tag}_mv", [P, TT, 2])
                rstd = sb(st, f"{tag}_rstd", [P, TT])
                shift = sb(st, f"{tag}_shift", [P, TT])
                banks = [ps(st, f"{tag}_ps{i}", [P, G, P]) for i in range(4)]
                loaded = [sem(f"{tag}_loaded{t}") for t in range(TT)]
                s_stats, s_mv, s_sd, s_rstd, s_shift, s_xn, stored, turned, hi_done, lo_done = (
                    sem(f"{tag}_{n}") for n in ("stats_s", "mv_s", "sd_s", "rstd_s", "shift_s", "xn_s", "stored", "turned", "hi_s", "lo_s"))
                with nc.Block() as block:
                    @block.sync
                    def _(sp):
                        if source is not None:
                            for t in range(TT):
                                sp.dma_start(x_sb[:, t, :], source[t * P:(t + 1) * P, :]).then_inc(loaded[t], 16)
                        for dst, src, arrived in preload:
                            sp.dma_start(dst, src).then_inc(arrived, 16)
                        if to_dram:
                            for t in range(TT):
                                sp.wait_ge(s_xn, t + 1)
                                sp.dma_start(xn_d[t * P:(t + 1) * P, :], xn[:, t, :]).then_inc(stored, 16)
                            sp.wait_ge(stored, 16 * TT)

                    @block.vector
                    def _(dve):
                        for step in range(TT + 3):
                            if step < TT:
                                t = step
                                if source is not None:
                                    dve.wait_ge(loaded[t], 16)
                                for h in range(2):
                                    dve.bn_stats(stats[:, t, h, :], x_sb[:, t, h * BANK:(h + 1) * BANK]).then_inc(s_stats, 1)
                                dve.wait_ge(s_stats, 2 * t + 2)
                                dve.bn_aggr(mv[:, t, :], stats[:, t, :, :]).then_inc(s_mv, 1)
                            if 1 <= step <= TT:
                                dve.wait_ge(s_sd, step)
                                dve.reciprocal(rstd[:, step - 1:step], rstd[:, step - 1:step]).then_inc(s_rstd, 1)
                                dve.wait_ge(s_rstd, step)
                                dve.scalar_tensor_tensor(out=shift[:, step - 1:step], in0=mv[:, step - 1, 0:1], scalar=-1.0,
                                                         in1=rstd[:, step - 1:step], op0=ALU.mult, op1=ALU.mult).then_inc(s_shift, 1)
                            if turn and step >= 3:
                                for q in range(KS // G):
                                    t, n = step - 3, 2 * (step - 3) + q
                                    dve.wait_ge(hi_done, n + 1)
                                    dve.tensor_tensor(xt_lo[:, G * q:G * q + G, t * P:(t + 1) * P], banks[n % 4][:],
                                                      f32(xt_hi[:, G * q:G * q + G, t * P:(t + 1) * P]), ALU.subtract).then_inc(lo_done, 1)

                    @block.tensor
                    def _(pe):
                        for n in range(2 * TT if turn else 0):
                            t, q = n // 2, n % 2
                            pe.wait_ge(s_xn, t + 1)
                            if n >= 4:
                                pe.wait_ge(lo_done, n - 3)
                            for j in range(G):
                                last = pe.transpose(banks[n % 4][:, j, :],
                                                    xn[:, t, (G * q + j) * P:(G * q + j + 1) * P], ident[:])
                            last.then_inc(turned, 1)

                    @block.scalar
                    def _(act):
                        for step in range(TT + 2):
                            if step < TT:
                                act.wait_ge(s_mv, step + 1)
                                act.activation(rstd[:, step:step + 1], mv[:, step, 1:2], ACT.Sqrt, bias=eps5[:]).then_inc(s_sd, 1)
                            if 1 <= step <= TT:
                                t = step - 1
                                act.wait_ge(s_shift, step)
                                act.activation(xn[:, t, :], x_sb[:, t, :], ACT.Identity, scale=rstd[:, t:t + 1],
                                               bias=shift[:, t:t + 1]).then_inc(s_xn, 1)
                            if turn and step >= 2:
                                for q in range(KS // G):
                                    t, n = step - 2, 2 * (step - 2) + q
                                    act.wait_ge(turned, n + 1)
                                    act.activation(xt_hi[:, G * q:G * q + G, t * P:(t + 1) * P], banks[n % 4][:],
                                                   ACT.Copy).then_inc(hi_done, 1)

        class Weights:

            def __init__(self, tag, st, L, hi, lo, fetch, turned_first, banks=None, bufs=1):
                self.bufs = bufs
                self.L, self.hi, self.lo, self.fetch, self.flip, self.banks = L, hi, lo, fetch, turned_first, banks
                self.nr = L.cw // P
                shape = [P, bufs, self.nr, HID] if self.flip else [P, bufs, KS, L.cw]
                self.raw = sb(st, f"{tag}_raw", shape)
                self.loaded = [sem(f"{tag}_w_loaded{b}") for b in range(bufs)]
                self.turned, self.hi_done, self.lo_dve, self.lo_pool = (
                    sem(f"{tag}_{n}") for n in ("w_turned", "w_hi", "w_lodve", "w_lopool"))

            def buffer(self, c):
                return c % self.bufs if self.bufs > 1 else 0

            def load(self, sp, c):
                b = self.buffer(c)
                sp.dma_start(self.raw[:, b], self.fetch(c)).then_inc(self.loaded[b], 16)

            def wait_loaded(self, eng, c):
                eng.wait_ge(self.loaded[self.buffer(c)], 16 * (c // self.bufs if self.bufs > 1 else c) + 16)

            def turn(self, pe, c, k):
                if self.flip:
                    if k == 0:
                        self.wait_loaded(pe, c)
                    if k >= 2:
                        pe.wait_ge(self.lo_dve, KS * c + k - 1)
                    for m in range(self.nr):
                        last = pe.transpose(self.banks[k % 2][:, m * P:(m + 1) * P], self.raw[:, self.buffer(c), m, k * P:(k + 1) * P], ident[:])
                    last.then_inc(self.turned, 1)

            def slab(self, c, k):
                return self.banks[k % 2][:, 0:self.L.cw] if self.flip else self.raw[:, self.buffer(c), k, :]

            def cut_hi(self, act, b, c, k):
                if self.flip:
                    act.wait_ge(self.turned, KS * c + k + 1)
                elif k == 0:
                    self.wait_loaded(act, c)
                act.activation(self.hi[:, b, k, :], self.slab(c, k), ACT.Copy).then_inc(self.hi_done, 1)

            def on_dve(self, k):
                return self.flip or k % 2 == 0

            def cut_lo(self, eng, b, c, k):
                eng.wait_ge(self.hi_done, KS * c + k + 1)
                eng.tensor_tensor(self.lo[:, b, k, :], self.slab(c, k), f32(self.hi[:, b, k, :]),
                                  ALU.subtract).then_inc(self.lo_dve if self.on_dve(k) else self.lo_pool, 1)

            def wait(self, eng, chunks):
                if self.flip:
                    eng.wait_ge(self.lo_dve, KS * chunks)
                else:
                    eng.wait_ge(self.lo_dve, KS // 2 * chunks)
                    eng.wait_ge(self.lo_pool, KS // 2 * chunks)

        def chunk_of(w, L, turned_first):
            if turned_first:
                return lambda c: w[bass.ds(c * L.cw, L.cw), :].rearrange("(m p) k -> p m k", p=P)
            v = w.rearrange("(k p) n -> p k n", p=P)
            return lambda c: v[:, :, bass.ds(c * L.cw, L.cw)]

        def queries(tag, L, xt_hi, xt_lo, wq, turned_first):
            CW, D = L.cw, L.d
            chunks = L.kvh
            qT_d = scratch[L][0]
            PAIR = 2 * TT
            with ExitStack() as st:
                w_hi = sb(st, f"{tag}_whi", [P, 2, KS, CW], F32R)
                w_lo = sb(st, f"{tag}_wlo", [P, 2, KS, CW], F32R)
                sq = sb(st, f"{tag}_sq", [P, CW])
                inv = sb(st, f"{tag}_inv", [P, 2, G])
                qn = sb(st, f"{tag}_qn", [P, 2, CW])
                stage = sb(st, f"{tag}_stage", [P, 2, G, P])
                y = [ps(st, f"{tag}_y{i}", [P, BANK]) for i in range(2)]
                qt = [ps(st, f"{tag}_qt{i}", [P, G, P]) for i in range(2)]
                wt = [ps(st, f"{tag}_wt{i}", [P, BANK]) for i in range(2)]
                W = Weights(tag, st, L, w_hi, w_lo, chunk_of(wq, L, turned_first), turned_first, wt)
                squared, summed, rooted, inverted = (sem(f"{tag}_{n}") for n in ("sq_s", "sum_s", "root_s", "inv_s"))
                y_ready = sem(f"{tag}_yready")
                normed, turned, staged = ([sem(f"{tag}_{n}{p}") for p in range(2)] for n in ("norm", "turned", "staged"))
                stored = [sem(f"{tag}_stored{p}") for p in range(2)]
                primed = sem(f"{tag}_primed")

                def slabs(t):
                    return [0, 1] if t == 0 else [t + 1]

                def walk(eng, pair):
                    if chunks > 2:
                        with eng.Fori(0, chunks // 2 - 1) as i:
                            pair(i, True)
                    pair(chunks // 2 - 1, False)

                with nc.Block() as block:
                    @block.sync
                    def _(sp):
                        W.load(sp, 0)
                        W.wait(sp, 1)
                        W.load(sp, 1)

                        def pair(i, more):
                            for n in range(PAIR):
                                c, t = n // TT, n % TT
                                if t == TT - 1 and more:
                                    W.wait(sp, 2 * i + c + 2)
                                    W.load(sp, 2 * i + c + 2)
                                sp.wait_ge(staged[n % 2], TT * i + n // 2 + 2)
                                sp.dma_start(qT_d[2 * i + c, :, :, t * P:(t + 1) * P], stage[0:D, n % 2, :, :]).then_inc(stored[n % 2], 16)
                        walk(sp, pair)
                        for p in range(2):
                            sp.wait_ge(stored[p], 16 * TT * (chunks // 2) + 1)

                    @block.gpsimd
                    def _(pool):
                        for p in range(2):
                            pool.sem_inc(stored[p], 1)
                        if not W.flip:
                            for k in range(1, KS, 2):
                                W.cut_lo(pool, 0, 0, k)

                            def pair(i, more):
                                for n in range(PAIR):
                                    c, t = n // TT, n % TT
                                    if more or c == 0:
                                        for k in slabs(t):
                                            if not W.on_dve(k):
                                                W.cut_lo(pool, 1 - c, 2 * i + c + 1, k)
                            walk(pool, pair)

                    @block.tensor
                    def _(pe):
                        def turn(i, n):
                            p = n % 2
                            pe.wait_ge(normed[p], TT * i + n // 2 + 2)
                            pe.wait_ge(staged[p], TT * i + n // 2 + 1)
                            for h in range(G):
                                last = pe.transpose(qt[p][0:D, h, :], qn[:, p, h * D:(h + 1) * D], ident[:])
                            last.then_inc(turned[p], 1)

                        def pair(i, more):
                            for n in range(PAIR):
                                c, t, p = n // TT, n % TT, n % 2
                                if t == 0:
                                    W.wait(pe, 2 * i + c + 1)
                                pe.wait_ge(normed[p], TT * i + n // 2 + 1)
                                for k in range(KS):
                                    last = product(pe, y[p][:, 0:CW], xt_hi[:, k, t * P:(t + 1) * P], xt_lo[:, k, t * P:(t + 1) * P],
                                                   w_hi[:, c, k, :], w_lo[:, c, k, :], k == 0, k == KS - 1)
                                last.then_inc(y_ready, 1)
                                if n:
                                    turn(i, n - 1)
                                if more or c == 0:
                                    for k in slabs(t):
                                        W.turn(pe, 2 * i + c + 1, k)
                            turn(i, PAIR - 1)

                        for p in range(2):
                            pe.sem_inc(turned[p], 1)
                        for k in range(KS):
                            W.turn(pe, 0, k)
                        walk(pe, pair)

                    @block.scalar
                    def _(act):
                        def put(i, n):
                            p = n % 2
                            act.wait_ge(turned[p], TT * i + n // 2 + 2)
                            act.wait_ge(stored[p], 16 * (TT * i + n // 2) + 1)
                            act.activation(stage[0:D, p, :, :], qt[p][0:D, :, :], ACT.Copy,
                                           scale=qw[0:D, :] if L.normed else L.scale).then_inc(staged[p], 1)

                        def pair(i, more):
                            for n in range(PAIR):
                                c, t, p = n // TT, n % TT, n % 2
                                m = PAIR * i + n
                                act.wait_ge(y_ready, m + 1)
                                if L.normed:
                                    act.wait_ge(summed, m + 1)
                                    act.activation(sq[:], y[p][:, 0:CW], ACT.Square).then_inc(squared, 1)
                                    act.wait_ge(summed, m + 2)
                                    act.activation(inv[:, p, :], inv[:, p, :], ACT.Sqrt, scale=1.0 / D, bias=eps6[:]).then_inc(rooted, 1)
                                else:
                                    act.wait_ge(turned[p], TT * i + n // 2 + 1)
                                    act.activation(qn[:, p, :], y[p][:, 0:CW], ACT.Copy).then_inc(normed[p], 1)
                                if more or c == 0:
                                    for k in slabs(t):
                                        W.cut_hi(act, 1 - c, 2 * i + c + 1, k)
                                if n:
                                    put(i, n - 1)
                            put(i, PAIR - 1)

                        for p in range(2):
                            act.sem_inc(staged[p], 1)
                            if not L.normed:
                                act.sem_inc(normed[p], 1)
                        for k in range(KS):
                            W.cut_hi(act, 0, 0, k)
                        walk(act, pair)

                    @block.vector
                    def _(dve):
                        def pair(i, more):
                            for n in range(PAIR):
                                c, t, p = n // TT, n % TT, n % 2
                                m = PAIR * i + n
                                if L.normed:
                                    dve.wait_ge(squared, m + 1)
                                    dve.tensor_reduce(inv[:, p, :], sq[:].rearrange("p (g d) -> p g d", g=G), AX.X, ALU.add).then_inc(summed, 1)
                                    dve.wait_ge(rooted, m + 1)
                                    dve.reciprocal(inv[:, p, :], inv[:, p, :]).then_inc(inverted, 1)
                                    dve.wait_ge(inverted, m + 1)
                                    dve.wait_ge(turned[p], TT * i + n // 2 + 1)
                                    dve.tensor_tensor(qn[:, p, :].rearrange("p (g d) -> p g d", g=G),
                                                      y[p][:, 0:CW].rearrange("p (g d) -> p g d", g=G),
                                                      inv[:, p, :].unsqueeze(2).broadcast_to([P, G, D]), ALU.mult).then_inc(normed[p], 1)
                                if more or c == 0:
                                    for k in slabs(t):
                                        if W.on_dve(k):
                                            W.cut_lo(dve, 1 - c, 2 * i + c + 1, k)

                        if L.normed:
                            dve.sem_inc(summed, 1)
                            for p in range(2):
                                dve.sem_inc(normed[p], 1)
                        for k in range(KS):
                            if W.on_dve(k):
                                W.cut_lo(dve, 0, 0, k)
                        walk(dve, pair)

        def keys_values(tag, L, wk, wv, turned_first):
            CW, D, NK, T = L.cw, L.d, L.nkc, KVT
            C = 2 * NK
            _, kT_d, v_d, _ = scratch[L]
            order = {4: ["Y0", "Y1", "X0", "Y2", "K0", "Y3", "K1"], 2: ["Y0", "X0", "Y1", "K0"]}[C]
            sources = [chunk_of(wk, L, turned_first), chunk_of(wv, L, turned_first)]
            with ExitStack() as st:
                w_hi = sb(st, f"{tag}_whi", [P, C, KS, CW], F32R)
                w_lo = sb(st, f"{tag}_wlo", [P, C, KS, CW], F32R)
                xin = sb(st, f"{tag}_xin", [P, 2, HID])
                xt_hi = sb(st, f"{tag}_xthi", [P, 2, KS, P], F32R)
                xt_lo = sb(st, f"{tag}_xtlo", [P, 2, KS, P], F32R)
                sq = sb(st, f"{tag}_sq", [P, CW])
                inv = sb(st, f"{tag}_inv", [P, NK, G])
                yn = sb(st, f"{tag}_yn", [P, NK, CW])
                stage = sb(st, f"{tag}_stage", [P, C, BANK])
                y = [ps(st, f"{tag}_y{c}", [P, BANK]) for c in range(C)]
                xb = [ps(st, f"{tag}_xb{q}", [P, G, P]) for q in range(2)]
                tb = [ps(st, f"{tag}_tb{c}", [P, G, P]) for c in range(2)]
                W = Weights(tag, st, L, w_hi, w_lo, lambda c: sources[c // NK](c % NK), turned_first,
                            [b.ap().rearrange("p g s -> p (g s)") for b in tb] if turned_first else None, bufs=2)

                x_loaded = [sem(f"{tag}_xl{p}") for p in range(2)]
                x_turned, x_hi_done, x_lo_done, y_ready = (sem(f"{tag}_{n}") for n in ("xturn", "xhi_s", "xlo_s", "yready"))
                squared, summed, rooted, inverted = (sem(f"{tag}_{n}") for n in ("sq_s", "sum_s", "root_s", "inv_s"))
                normed = [sem(f"{tag}_norm{c}") for c in range(NK)]
                turned = [sem(f"{tag}_turned{c}") for c in range(NK)]
                staged = [sem(f"{tag}_staged{c}") for c in range(C)]
                stored = [sem(f"{tag}_stored{c}") for c in range(C)]
                y_read = normed + staged[NK:]

                def source(i, j):
                    if j < 0 or j >= T:
                        i, j = i + j // T, j % T
                    if j < CT:
                        return ctx_rows[bass.ds(i * CTX + j * CR, CR), :]
                    return xn_d[bass.ds(i * QLEN, QLEN), :]

                def target(c, i, j):
                    if c < NK:
                        return kT_d[bass.ds(i * L.kvh + c * G, G), :, j * CR:j * CR + ROWS[j]].rearrange("u d s -> d u s")
                    return v_d[bass.ds(i * KVLEN + j * CR, ROWS[j]), (c - NK) * CW:(c - NK + 1) * CW]

                def staging(c, r):
                    if c < NK:
                        return stage[0:D, c, :].rearrange("p (g s) -> p g s", g=G)[:, :, 0:r]
                    return stage[0:r, c, 0:CW]

                def walk(eng, step):
                    with eng.Fori(0, BATCH - 1) as i:
                        for j in range(T):
                            step(i, j, ROWS[j], 2)
                    for j in range(T):
                        step(BATCH - 1, j, ROWS[j], min(T - 1 - j, 2))

                with nc.Block() as block:
                    @block.sync
                    def _(sp):
                        for j in range(2):
                            sp.dma_start(xin[0:ROWS[j], j, :], source(0, j)).then_inc(x_loaded[j], 16)
                        for c in range(C):
                            if c >= 2:
                                W.wait(sp, c - 1)
                            W.load(sp, c)

                        def step(i, j, r, left):
                            n = i * T + j
                            if left == 2:
                                sp.wait_ge(x_turned, 2 * n + 2)
                                sp.dma_start(xin[0:ROWS[(j + 2) % T], j % 2, :], source(i, j + 2)).then_inc(x_loaded[j % 2], 16)
                            for what in order:
                                c = int(what[1])
                                if what[0] == "K" or (what[0] == "Y" and c >= NK):
                                    sp.wait_ge(staged[c], n + 2)
                                    sp.dma_start(target(c, i, j), staging(c, r)).then_inc(stored[c], 16)
                        walk(sp, step)
                        for c in range(C):
                            sp.wait_ge(stored[c], 16 * BATCH * T + 1)

                    @block.gpsimd
                    def _(pool):
                        for c in range(C):
                            pool.sem_inc(stored[c], 1)
                        if not W.flip:
                            for c in range(C):
                                for k in range(1, KS, 2):
                                    W.cut_lo(pool, c, c, k)

                    @block.tensor
                    def _(pe):
                        def turn_rows(r, p):
                            for q in range(2):
                                for m in range(G):
                                    k = G * q + m
                                    last = pe.transpose(xb[q][:, m, 0:r], xin[0:r, p, k * P:(k + 1) * P], ident[0:r, 0:r])
                                last.then_inc(x_turned, 1)

                        def step(i, j, r, left):
                            n, p = i * T + j, j % 2
                            for what in order:
                                c = int(what[1])
                                if what[0] == "Y":
                                    if not W.flip:
                                        W.wait(pe, c + 1)
                                    pe.wait_ge(x_lo_done, 2 * n + 2)
                                    pe.wait_ge(y_read[c], n + 1)
                                    for k in range(KS):
                                        last = product(pe, y[c][0:r, 0:CW], xt_hi[:, p, k, 0:r], xt_lo[:, p, k, 0:r],
                                                       w_hi[:, c, k, :], w_lo[:, c, k, :], k == 0, k == KS - 1)
                                    last.then_inc(y_ready, 1)
                                elif what[0] == "X" and left:
                                    pe.wait_ge(x_loaded[1 - p], 16 * (i * (T // 2) + (j + 1) // 2 + 1))
                                    turn_rows(ROWS[(j + 1) % T], 1 - p)
                                elif what[0] == "K":
                                    pe.wait_ge(normed[c], n + 2)
                                    pe.wait_ge(staged[c], n + 1)
                                    for m in range(G):
                                        last = pe.transpose(tb[c][0:D, m, 0:r], yn[0:r, c, m * D:(m + 1) * D], ident[0:r, 0:r])
                                    last.then_inc(turned[c], 1)

                        for c in range(NK):
                            pe.sem_inc(turned[c], 1)
                        pe.wait_ge(x_loaded[0], 16)
                        turn_rows(ROWS[0], 0)
                        if W.flip:
                            for c in range(C):
                                for k in range(KS):
                                    if k < 2 and c:
                                        W.wait(pe, c)
                                    W.turn(pe, c, k)
                            W.wait(pe, C)
                        walk(pe, step)

                    @block.scalar
                    def _(act):
                        def x_highs(n, p, r):
                            for q in range(2):
                                act.wait_ge(x_turned, 2 * n + q + 1)
                                act.activation(xt_hi[:, p, G * q:G * q + G, 0:r], xb[q][:, :, 0:r], ACT.Copy).then_inc(x_hi_done, 1)

                        for c in range(C):
                            act.sem_inc(staged[c], 1)
                        if not L.normed:
                            for c in range(NK):
                                act.sem_inc(normed[c], 1)
                        x_highs(0, 0, ROWS[0])
                        for c in range(C):
                            for k in range(KS):
                                W.cut_hi(act, c, c, k)

                        def step(i, j, r, left):
                            n = i * T + j
                            for what in order:
                                c = int(what[1])
                                if what[0] == "Y":
                                    act.wait_ge(y_ready, C * n + c + 1)
                                    if c >= NK:
                                        act.wait_ge(stored[c], 16 * n + 1)
                                        act.activation(staging(c, r), y[c][0:r, 0:CW], ACT.Copy).then_inc(staged[c], 1)
                                    elif L.normed:
                                        act.wait_ge(summed, NK * n + c + 1)
                                        act.activation(sq[0:r, :], y[c][0:r, 0:CW], ACT.Square).then_inc(squared, 1)
                                        act.wait_ge(summed, NK * n + c + 2)
                                        act.activation(inv[0:r, c, :], inv[0:r, c, :], ACT.Sqrt, scale=1.0 / D, bias=eps6[0:r, :]).then_inc(rooted, 1)
                                    else:
                                        act.wait_ge(turned[c], n + 1)
                                        act.activation(yn[0:r, c, :], y[c][0:r, 0:CW], ACT.Copy).then_inc(normed[c], 1)
                                elif what[0] == "X" and left:
                                    x_highs(n + 1, 1 - j % 2, ROWS[(j + 1) % T])
                                elif what[0] == "K":
                                    act.wait_ge(turned[c], n + 2)
                                    act.wait_ge(stored[c], 16 * n + 1)
                                    act.activation(staging(c, r), tb[c][0:D, :, 0:r], ACT.Copy,
                                                   scale=kw[0:D, :] if L.normed else 1.0).then_inc(staged[c], 1)
                        walk(act, step)

                    @block.vector
                    def _(dve):
                        def x_lows(n, p, r):
                            for q in range(2):
                                dve.wait_ge(x_hi_done, 2 * n + q + 1)
                                dve.tensor_tensor(xt_lo[:, p, G * q:G * q + G, 0:r], xb[q][:, :, 0:r],
                                                  f32(xt_hi[:, p, G * q:G * q + G, 0:r]), ALU.subtract).then_inc(x_lo_done, 1)

                        if L.normed:
                            dve.sem_inc(summed, 1)
                            for c in range(NK):
                                dve.sem_inc(normed[c], 1)
                        x_lows(0, 0, ROWS[0])
                        for c in range(C):
                            for k in range(KS):
                                if W.on_dve(k):
                                    W.cut_lo(dve, c, c, k)

                        def step(i, j, r, left):
                            n = i * T + j
                            for what in order:
                                c = int(what[1])
                                if what[0] == "Y" and c < NK and L.normed:
                                    dve.wait_ge(squared, NK * n + c + 1)
                                    dve.tensor_reduce(inv[0:r, c, :], sq[0:r, :].rearrange("p (g d) -> p g d", g=G),
                                                      AX.X, ALU.add).then_inc(summed, 1)
                                    dve.wait_ge(rooted, NK * n + c + 1)
                                    dve.reciprocal(inv[0:r, c, :], inv[0:r, c, :]).then_inc(inverted, 1)
                                    dve.wait_ge(inverted, NK * n + c + 1)
                                    dve.wait_ge(turned[c], n + 1)
                                    dve.tensor_tensor(yn[0:r, c, :].rearrange("p (g d) -> p g d", g=G),
                                                      y[c][0:r, 0:CW].rearrange("p (g d) -> p g d", g=G),
                                                      inv[0:r, c, :].unsqueeze(2).broadcast_to([r, G, D]), ALU.mult).then_inc(normed[c], 1)
                                elif what[0] == "X" and left:
                                    x_lows(n + 1, 1 - j % 2, ROWS[(j + 1) % T])
                        walk(dve, step)

        def attention(tag, L, oT, rinv):
            D, U = L.d, L.units
            qT_d, kT_d, v_d, _ = scratch[L]
            GP = L.kvh // 2
            with ExitStack() as st:
                qr = sb(st, f"{tag}_qr", [D, 2, G * QLEN])
                kr = sb(st, f"{tag}_kr", [D, 2, KVPAD])
                vr = sb(st, f"{tag}_vr", [P, 2, KVT, D])
                qs = sb(st, f"{tag}_q", [D, 2, 2, G * QLEN], F32R)
                ks = sb(st, f"{tag}_k", [D, 2, 2, KVPAD], F32R)
                vs = sb(st, f"{tag}_v", [P, 2, 2, KVT, D], F32R)
                pr = sb(st, f"{tag}_p", [QLEN, 2, G, KVPAD])
                nmax = sb(st, f"{tag}_nmax", [QLEN, 2, G])
                rsum = sb(st, f"{tag}_rsum", [QLEN, 2, G])
                pt_hi = sb(st, f"{tag}_pthi", [P, KVT, G * QLEN], F32R)
                pt_lo = sb(st, f"{tag}_ptlo", [P, KVT, G * QLEN], F32R)
                s = [ps(st, f"{tag}_s{h}", [QLEN, BANK]) for h in range(G)]
                tb = [ps(st, f"{tag}_tb{b}", [P, G * QLEN]) for b in range(2)]
                o = [ps(st, f"{tag}_o{p}", [P, G * QLEN]) for p in range(2)]
                padded = sem(f"{tag}_padded")
                qk_loaded = [sem(f"{tag}_qkl{p}") for p in range(2)]
                v_loaded = [sem(f"{tag}_vl{p}") for p in range(2)]
                k_hi, q_hi = ([sem(f"{tag}_{n}hi{p}") for p in range(2)] for n in "kq")
                v_hi, arrived = sem(f"{tag}_vhi"), sem(f"{tag}_arrived")
                qk_cut = [sem(f"{tag}_qkc{p}") for p in range(2)]
                v_cut = [sem(f"{tag}_vc{p}") for p in range(2)]
                scored = [sem(f"{tag}_scored{h}") for h in range(G - 1)]
                qk_used = [sem(f"{tag}_qku{p}") for p in range(2)]
                exped = [sem(f"{tag}_exped{h}") for h in range(G)]
                maxed, inverted = sem(f"{tag}_maxed"), sem(f"{tag}_inverted")
                turned = [sem(f"{tag}_turned{x}") for x in range(KVT)]
                hi_done, lo_done = sem(f"{tag}_hi_s"), sem(f"{tag}_lo_s")
                multiplied = [sem(f"{tag}_mult{x}") for x in range(KVT - 1)]
                v_used = [sem(f"{tag}_vu{p}") for p in range(2)]
                o_read = [sem(f"{tag}_oread{p}") for p in range(2)]

                def walk(eng, step):
                    step(0, 0, 2, True)
                    step(0, 1, 2)
                    with eng.Fori(1, U // 2 - 1) as i:
                        step(i, 0, 2)
                        step(i, 1, 2)
                    step(U // 2 - 1, 0, 1)
                    step(U // 2 - 1, 1, 0)

                ORDER = ["S0", "T0", "S1", "T1", "S2", "S3", "v2", "T2", "v3", "V0", "T3", "V1"]
                ACT_ORDER = ["T0", "q", "T1", "S0", "S1", "T2", "S2", "S3", "T3", "o"]
                DVE_ORDER = ["k", "S0", "T0", "S1", "T1", "S2", "S3", "T2", "T3", "o"]

                with nc.Block() as block:
                    @block.sync
                    def _(sp):
                        sp.wait_ge(padded, 2)
                        with sp.Fori(0, BATCH) as b:
                            with sp.Fori(0, GP) as gp:
                                for p in range(2):
                                    half = b * GP + gp
                                    u = half * 2 + p
                                    sp.wait_ge(qk_cut[p], half + 1)
                                    sp.dma_start(qr[:, p, :].rearrange("d (g s) -> d g s", g=G),
                                                 qT_d[gp * 2 + p, :, :, bass.ds(b * QLEN, QLEN)]).then_inc(qk_loaded[p], 16)
                                    sp.dma_start(kr[:, p, 0:KVLEN], kT_d[u, :, :]).then_inc(qk_loaded[p], 16)
                                    sp.wait_ge(v_cut[p], half + 1)
                                    cols = bass.ds((gp * 2 + p) * D, D)
                                    sp.dma_start(vr[0:CR, p, 0:CT, :], v_d[bass.ds(b * KVLEN, CTX), cols].rearrange("(j r) d -> r j d", r=CR)).then_inc(v_loaded[p], 16)
                                    sp.dma_start(vr[0:QLEN, p, CT, :], v_d[bass.ds(b * KVLEN + CTX, QLEN), cols]).then_inc(v_loaded[p], 16)

                    @block.gpsimd
                    def _(pool):
                        pool.memset(kr[:, :, KVLEN:KVPAD], 0.0).then_inc(padded, 1)
                        pool.memset(vr[:, :, CT, :], 0.0).then_inc(padded, 1)
                        for p in range(2):
                            pool.sem_inc(qk_cut[p], 1)
                            pool.sem_inc(v_cut[p], 1)

                        def cut_qk(p, half):
                            pool.wait_ge(k_hi[p], half + 1)
                            pool.tensor_tensor(ks[:, p, 1, :], kr[:, p, :], f32(ks[:, p, 0, :]), ALU.subtract)
                            pool.wait_ge(q_hi[p], half + 1)
                            pool.tensor_tensor(qs[:, p, 1, :], qr[:, p, :], f32(qs[:, p, 0, :]), ALU.subtract).then_inc(qk_cut[p], 1)

                        def cut_v(p, half):
                            pool.wait_ge(v_used[p], half + 1)
                            pool.wait_ge(v_loaded[p], 32 * half + 32)
                            pool.sem_inc(arrived, 1)
                            pool.tensor_copy(vs[0:CR, p, 0, :, :], vr[0:CR, p, :, :]).then_inc(v_hi, 1)
                            pool.wait_ge(v_hi, 2 * half + p + 1)
                            pool.tensor_tensor(vs[0:CR, p, 1, :, :], vr[0:CR, p, :, :], f32(vs[0:CR, p, 0, :, :]), ALU.subtract).then_inc(v_cut[p], 1)

                        def step(i, p, more, first=False):
                            if more == 2:
                                cut_qk(p, i + 1)
                            if more:
                                cut_v(1 - p, i + p)
                        cut_qk(0, 0)
                        cut_v(0, 0)
                        cut_qk(1, 0)
                        walk(pool, step)

                    @block.tensor
                    def _(pe):
                        def scores(p, h, half, u):
                            if h == 0:
                                pe.wait_ge(qk_cut[p], half + 2)
                            if not (isinstance(u, int) and u == 0):
                                pe.wait_ge(exped[h], u)
                            last = product(pe, s[h][:, 0:KVPAD], qs[:, p, 0, h * QLEN:(h + 1) * QLEN], qs[:, p, 1, h * QLEN:(h + 1) * QLEN],
                                           ks[:, p, 0, :], ks[:, p, 1, :], True, True)
                            last.then_inc(scored[h] if h < G - 1 else qk_used[p], 1)

                        def multiply(p, x, i, u):
                            r = ROWS[x]
                            if x == 0:
                                pe.wait_ge(v_cut[p], i + 2)
                                pe.wait_ge(o_read[p], i + 1)
                            pe.wait_ge(lo_done, KVT * u + x + 1)
                            last = product(pe, o[p][0:D, :], vs[0:r, p, 0, x, :], vs[0:r, p, 1, x, :],
                                           pt_hi[0:r, x, :], pt_lo[0:r, x, :], x == 0, x == KVT - 1)
                            last.then_inc(multiplied[x] if x < KVT - 1 else v_used[p], 1)

                        def step(i, p, more, first=False):
                            u = 2 * i + p
                            for what in ORDER:
                                x = int(what[1])
                                if what[0] == "S" and more:
                                    scores(1 - p, x, i + p, u + 1)
                                elif what[0] == "T":
                                    if x == 0:
                                        pe.wait_ge(exped[G - 1], u + 1)
                                    if not first or x >= 2:
                                        pe.wait_ge(lo_done, KVT * u + x - 1)
                                    r = ROWS[x]
                                    for h in range(G):
                                        last = pe.transpose(tb[x % 2][0:r, h * QLEN:(h + 1) * QLEN], pr[:, p, h, x * CR:x * CR + r], ident[0:QLEN, 0:QLEN])
                                    last.then_inc(turned[x], 1)
                                elif what[0] == "V":
                                    multiply(p, x, i, u)
                                elif what[0] == "v" and not first:
                                    multiply(1 - p, x, i + p - 1, u - 1)

                        for one in qk_used + v_used + multiplied + turned:
                            pe.sem_inc(one, 1)
                        for h in range(G):
                            scores(0, h, 0, 0)
                        walk(pe, step)
                        for x in (2, 3):
                            multiply(1, x, U // 2 - 1, U - 1)

                    @block.scalar
                    def _(act):
                        def exp(p, h, u, transposed):
                            act.wait_ge(maxed, G * u + h + 1)
                            if h == 0:
                                act.wait_ge(turned[KVT - 1], transposed + 1)
                            act.activation(pr[:, p, h, 0:KVLEN], s[h][:, 0:KVLEN], ACT.Exp, bias=nmax[:, p, h:h + 1],
                                           accum_out=rsum[:, p, h:h + 1]).then_inc(exped[h], 1)

                        def cut_q(p, half):
                            act.wait_ge(qk_used[p], half + 1)
                            act.wait_ge(qk_loaded[p], 32 * half + 32)
                            act.activation(qs[:, p, 0, :], qr[:, p, :], ACT.Copy).then_inc(q_hi[p], 1)

                        def step(i, p, more, first=False):
                            u = 2 * i + p
                            for what in ACT_ORDER:
                                x = int(what[1:] or 0)
                                if what[0] == "S" and more:
                                    exp(1 - p, x, u + 1, u)
                                elif what[0] == "T":
                                    act.wait_ge(turned[x], u + 2)
                                    if x < KVT - 1:
                                        act.wait_ge(multiplied[x], u + 1)
                                    else:
                                        act.wait_ge(v_used[1 - p], i + p + 1)
                                    act.activation(pt_hi[0:ROWS[x], x, :], tb[x % 2][0:ROWS[x], :], ACT.Copy).then_inc(hi_done, 1)
                                elif what == "q" and more == 2:
                                    cut_q(p, i + 1)
                                elif what == "o" and p == 1:
                                    act.wait_ge(v_used[0], i + 2)
                                    act.activation(oT[:, bass.ds(u - 1, 1), :], o[0][0:D, :].unsqueeze(1), ACT.Copy).then_inc(o_read[0], 1)

                        act.sem_inc(o_read[0], 1)
                        cut_q(0, 0)
                        cut_q(1, 0)
                        for h in range(G):
                            exp(0, h, 0, 0)
                        walk(act, step)

                    @block.vector
                    def _(dve):
                        def neg_max(p, h, half, u):
                            if h < G - 1:
                                dve.wait_ge(scored[h], u + 1)
                            else:
                                dve.wait_ge(qk_used[p], half + 2)
                            dve.tensor_reduce(nmax[:, p, h:h + 1], s[h][:, 0:KVLEN], AX.X, ALU.max, negate=True).then_inc(maxed, 1)

                        def invert(p, u):
                            dve.wait_ge(exped[G - 1], u + 1)
                            dve.reciprocal(rinv[:, bass.ds(u, 1), :], rsum[:, p:p + 1, :]).then_inc(inverted, 1)

                        def cut_k(p, half):
                            dve.wait_ge(qk_used[p], half + 1)
                            dve.wait_ge(qk_loaded[p], 32 * half + 32)
                            dve.tensor_copy(ks[:, p, 0, :], kr[:, p, :]).then_inc(k_hi[p], 1)

                        def keep_sums(i, u):
                            dve.wait_ge(v_used[1], i + 2)
                            dve.tensor_copy(oT[:, bass.ds(u, 1), :], o[1][0:D, :].unsqueeze(1)).then_inc(o_read[1], 1)

                        def step(i, p, more, first=False):
                            u = 2 * i + p
                            for what in DVE_ORDER:
                                x = int(what[1:] or 0)
                                if what[0] == "S" and more:
                                    neg_max(1 - p, x, i + p, u + 1)
                                elif what[0] == "T":
                                    dve.wait_ge(hi_done, KVT * u + x + 1)
                                    dve.tensor_tensor(pt_lo[0:ROWS[x], x, :], tb[x % 2][0:ROWS[x], :], f32(pt_hi[0:ROWS[x], x, :]),
                                                      ALU.subtract).then_inc(lo_done, 1)
                                    if x == 0:
                                        invert(p, u)
                                elif what == "k" and more == 2:
                                    cut_k(p, i + 1)
                                elif what == "o" and p == 0 and not first:
                                    keep_sums(i - 1, u - 1)

                        dve.sem_inc(o_read[1], 1)
                        cut_k(0, 0)
                        cut_k(1, 0)
                        for h in range(G):
                            neg_max(0, h, 0, 0)
                        walk(dve, step)
                        keep_sums(U // 2 - 1, U - 1)

        def out_project(tag, L, oT, rinv, wo, x_sb, gate, source=None):
            D, H = L.d, L.heads
            flip = not L.normed
            rT_d = scratch[L][3]
            NR = L.units * G // P
            NM = BANK // P
            o_v = oT[:].rearrange("d (b g) (h s) -> d b g h s", b=BATCH, h=G)
            with ExitStack() as st:
                rt = sb(st, f"{tag}_rt", [P, NR, QLEN])
                rb = sb(st, f"{tag}_rb", [D, 2, BATCH, QLEN])
                raw = sb(st, f"{tag}_raw", [P, 2, NM, D] if flip else [D, 2, BANK])
                w_hi = sb(st, f"{tag}_whi", [D, 2, BANK], F32R)
                w_lo = sb(st, f"{tag}_wlo", [D, 2, BANK], F32R)
                o_hi = sb(st, f"{tag}_ohi", [D, 2, TOKENS], F32R)
                o_lo = sb(st, f"{tag}_olo", [D, 2, TOKENS], F32R)
                y = [ps(st, f"{tag}_y{t}", [P, BANK]) for t in range(TT)]
                tb = ps(st, f"{tag}_tb", [P, BANK])
                x_loaded, r_turned, r_copied, r_stored = (sem(f"{tag}_{n}") for n in ("xl", "rturned", "rcopied", "rstored"))
                raw_loaded, r_loaded, o_normed, wt_done, wh_done, wl_done, oh_done, ol_done, used = (
                    [sem(f"{tag}_{n}{p}") for p in range(2)] for n in ("rawl", "rl", "on", "wt", "wh", "wl", "oh", "ol", "used"))
                y_ready, y_read = sem(f"{tag}_yready"), sem(f"{tag}_yread")

                def walk(eng, step):
                    for half in range(2):
                        def group(g, first, last):
                            for h in range(G):
                                step(half, g, h, half * (H // 2) + g * 2 + h // 2, first and h == 0, last and h == G - 1)
                        group(0, True, False)
                        if L.kvh > 2:
                            with eng.Fori(1, L.kvh - 1) as g:
                                group(g, False, False)
                        group(L.kvh - 1, False, True)

                with nc.Block() as block:
                    @block.sync
                    def _(sp):
                        if source is not None:
                            sp.dma_start(x_sb[:], source.rearrange("(t p) n -> p t n", p=P)).then_inc(x_loaded, 16)
                        sp.wait_ge(r_copied, NR)
                        sp.dma_start(rT_d.rearrange("b h s -> (b h) s").rearrange("(n p) s -> p n s", p=P), rt[:]).then_inc(r_stored, 16)
                        sp.wait_ge(r_stored, 16)

                        def step(half, g, h, m, first, last):
                            p = h % 2
                            if half == 0:
                                sp.wait_ge(o_normed[p], m)
                                sp.dma_start(rb[:, p, :, :], rT_d[:, bass.ds(g * G + h, 1), :].rearrange("b o s -> o b s")
                                             .broadcast_to([D, BATCH, QLEN])).then_inc(r_loaded[p], 16)
                            sp.wait_ge(wl_done[p], m)
                            if flip:
                                src = wo[half * BANK:(half + 1) * BANK, bass.ds((g * G + h) * D, D)].rearrange("(m p) d -> p m d", p=P)
                                sp.dma_start(raw[:, p, :, :], src).then_inc(raw_loaded[p], 16)
                            else:
                                sp.dma_start(raw[:, p, :], wo[bass.ds((g * G + h) * D, D), half * BANK:(half + 1) * BANK]).then_inc(raw_loaded[p], 16)
                        walk(sp, step)

                    @block.gpsimd
                    def _(pool):
                        def step(half, g, h, m, first, last):
                            p = h % 2
                            if not flip:
                                pool.wait_ge(wh_done[p], m + 1)
                                pool.tensor_tensor(w_lo[:, p, :], raw[:, p, :], f32(w_hi[:, p, :]), ALU.subtract).then_inc(wl_done[p], 1)
                            if half == 0:
                                pool.wait_ge(oh_done[p], m + 1)
                                pool.tensor_tensor(o_lo[:, p, :].rearrange("d (b s) -> d b s", b=BATCH), o_v[:, :, g, h, :],
                                                   f32(o_hi[:, p, :]).rearrange("d (b s) -> d b s", b=BATCH), ALU.subtract).then_inc(ol_done[p], 1)
                        walk(pool, step)

                    @block.scalar
                    def _(act):
                        act.wait_ge(r_turned, NR)
                        for n in range(NR):
                            act.activation(rt[:, n, :], tb[:, n * P:n * P + QLEN], ACT.Copy).then_inc(r_copied, 1)

                        def step(half, g, h, m, first, last):
                            p = h % 2
                            act.wait_ge(used[p], m)
                            if flip:
                                act.wait_ge(wt_done[p], m + 1)
                                act.activation(w_hi[:, p, :], tb[0:D, :], ACT.Copy).then_inc(wh_done[p], 1)
                            else:
                                act.wait_ge(raw_loaded[p], 16 * m + 16)
                                act.activation(w_hi[:, p, :], raw[:, p, :], ACT.Copy).then_inc(wh_done[p], 1)
                            if half == 0:
                                act.wait_ge(o_normed[p], m + 1)
                            act.activation(o_hi[:, p, :].rearrange("d (b s) -> d b s", b=BATCH), o_v[:, :, g, h, :], ACT.Copy).then_inc(oh_done[p], 1)
                        walk(act, step)

                    @block.tensor
                    def _(pe):
                        for n in range(NR):
                            pe.transpose(tb[:, n * P:n * P + QLEN], rinv[:].rearrange("q u h -> q (u h)")[:, n * P:(n + 1) * P],
                                         ident[0:QLEN, 0:QLEN]).then_inc(r_turned, 1)
                        pe.wait_ge(r_copied, NR)

                        def turn(p, m):
                            pe.wait_ge(raw_loaded[p], 16 * m + 16)
                            for n in range(NM):
                                last = pe.transpose(tb[0:D, n * P:(n + 1) * P], raw[:, p, n, :], ident[:])
                            last.then_inc(wt_done[p], 1)

                        if flip:
                            turn(0, 0)

                        def step(half, g, h, m, first, last):
                            p = h % 2
                            pe.wait_ge(wl_done[p], m + 1)
                            if flip and not (half and last):
                                turn(1 - p, m + p)
                            pe.wait_ge(ol_done[p], m + 1)
                            for t in range(TT):
                                if first and half:
                                    pe.wait_ge(y_read, t + 1)
                                mm = product(pe, y[t][:], o_hi[:, p, t * P:(t + 1) * P], o_lo[:, p, t * P:(t + 1) * P],
                                             w_hi[:, p, :], w_lo[:, p, :], first, last)
                                if last and t < TT - 1:
                                    mm.then_inc(y_ready, 1)
                            mm.then_inc(used[p], 1)
                        walk(pe, step)

                    @block.vector
                    def _(dve):
                        if source is not None:
                            dve.wait_ge(x_loaded, 16)

                        def step(half, g, h, m, first, last):
                            p = h % 2
                            if half == 0:
                                dve.wait_ge(r_loaded[p], 16 * m + 16)
                                dve.tensor_tensor(o_v[:, :, g, h, :], o_v[:, :, g, h, :], rb[:, p, :, :], ALU.mult).then_inc(o_normed[p], 1)
                            if flip:
                                dve.wait_ge(wh_done[p], m + 1)
                                dve.tensor_tensor(w_lo[:, p, :], tb[0:D, :], f32(w_hi[:, p, :]), ALU.subtract).then_inc(wl_done[p], 1)
                            if half:
                                dve.wait_ge(oh_done[p], m + 1)
                                dve.tensor_tensor(o_lo[:, p, :].rearrange("d (b s) -> d b s", b=BATCH), o_v[:, :, g, h, :],
                                                  f32(o_hi[:, p, :]).rearrange("d (b s) -> d b s", b=BATCH), ALU.subtract).then_inc(ol_done[p], 1)
                            if last:
                                for t in range(TT):
                                    if t < TT - 1:
                                        dve.wait_ge(y_ready, half * (TT - 1) + t + 1)
                                    else:
                                        dve.wait_ge(used[p], m + 1)
                                    cols = x_sb[:, t, half * BANK:(half + 1) * BANK]
                                    dve.scalar_tensor_tensor(out=cols, in0=y[t][:], scalar=gates[:, gate:gate + 1], in1=cols,
                                                             op0=ALU.mult, op1=ALU.add).then_inc(y_read, 1)
                        walk(dve, step)

        def scaled_ffn(x_sb):
            LIMIT = 448.0
            with ExitStack() as st:
                xt_hi = sb(st, "f0_xthi", [P, KS, TOKENS], F32R)
                xt_lo = sb(st, "f0_xtlo", [P, KS, TOKENS], F32R)
                w = sb(st, "f0_w", [P, KS, HID])
                most = sb(st, "f0_most", [P, 2])
                scl = sb(st, "f0_scl", [P, 3])
                with ExitStack() as st2:
                    xn = sb(st2, "f0_xn", [P, TT, HID])
                    banks = [ps(st2, f"f0_ps{i}", [P, G, P]) for i in range(4)]
                    loaded, maxed, reduced, chain = sem("f0_loaded"), sem("f0_maxed"), sem("f0_reduced"), sem("f0_chain")
                    scaled, clipped, turned, cut_hi, cut_lo = (sem(f"f0_{n}") for n in ("scaled", "clipped", "turned", "xhi", "xlo"))
                    layer_norm("f0_ln", x_sb, xn, preload=[(w[:], wffn0.rearrange("(k p) n -> p k n", p=P), loaded)])
                    with nc.Block() as block:
                        @block.gpsimd
                        def _(pool):
                            pool.wait_ge(maxed, 2)
                            pool.partition_all_reduce(most[:], most[:], P, bass.bass_isa.ReduceOp.max).then_inc(reduced, 1)

                        @block.vector
                        def _(dve):
                            dve.tensor_reduce(most[:, 0:1], xn[:].rearrange("p t n -> p (t n)"), AX.X, ALU.max, apply_absolute_value=True).then_inc(maxed, 1)
                            dve.wait_ge(loaded, 16)
                            dve.tensor_reduce(most[:, 1:2], w[:].rearrange("p t n -> p (t n)"), AX.X, ALU.max, apply_absolute_value=True).then_inc(maxed, 1)
                            dve.wait_ge(reduced, 1)
                            dve.tensor_scalar(scl[:, 0:2], most[:], 1e-12, None, ALU.max).then_inc(chain, 1)
                            dve.wait_ge(chain, 1)
                            dve.reciprocal(scl[:, 0:2], scl[:, 0:2]).then_inc(chain, 1)
                            dve.wait_ge(chain, 2)
                            dve.tensor_scalar(scl[:, 0:2], scl[:, 0:2], LIMIT, None, ALU.mult).then_inc(chain, 1)
                            dve.wait_ge(chain, 3)
                            dve.tensor_tensor(scl[:, 2:3], scl[:, 0:1], scl[:, 1:2], ALU.mult).then_inc(chain, 1)
                            dve.wait_ge(chain, 4)
                            dve.reciprocal(scl[:, 2:3], scl[:, 2:3]).then_inc(chain, 1)
                            dve.wait_ge(chain, 5)
                            dve.tensor_tensor(scl[:, 2:3], scl[:, 2:3], gates[:, 2:3], ALU.mult).then_inc(chain, 1)
                            for step in range(TT + 1):
                                if step < TT:
                                    dve.wait_ge(scaled, step + 1)
                                    dve.tensor_scalar(xn[:, step, :], xn[:, step, :], LIMIT, -LIMIT, ALU.min, ALU.max).then_inc(clipped, 1)
                                if step >= 1:
                                    for q in range(2):
                                        t, n = step - 1, 2 * (step - 1) + q
                                        dve.wait_ge(cut_hi, n + 1)
                                        dve.tensor_tensor(xt_lo[:, G * q:G * q + G, t * P:(t + 1) * P], banks[n % 4][:],
                                                          f32(xt_hi[:, G * q:G * q + G, t * P:(t + 1) * P]), ALU.subtract).then_inc(cut_lo, 1)

                        @block.scalar
                        def _(act):
                            act.wait_ge(chain, 3)
                            for step in range(TT + 1):
                                if step < TT:
                                    act.activation(xn[:, step, :], xn[:, step, :], ACT.Copy, scale=scl[:, 0:1]).then_inc(scaled, 1)
                                if step >= 1:
                                    for q in range(2):
                                        t, n = step - 1, 2 * (step - 1) + q
                                        act.wait_ge(turned, n + 1)
                                        act.activation(xt_hi[:, G * q:G * q + G, t * P:(t + 1) * P], banks[n % 4][:],
                                                       ACT.Copy).then_inc(cut_hi, 1)

                        @block.tensor
                        def _(pe):
                            for n in range(2 * TT):
                                t, q = n // 2, n % 2
                                pe.wait_ge(clipped, t + 1)
                                if n >= 4:
                                    pe.wait_ge(cut_lo, n - 3)
                                for j in range(G):
                                    last = pe.transpose(banks[n % 4][:, j, :],
                                                        xn[:, t, (G * q + j) * P:(G * q + j + 1) * P], ident[:])
                                last.then_inc(turned, 1)

                w_hi = sb(st, "f0_whi", [P, KS, HID], F32R)
                w_lo = sb(st, "f0_wlo", [P, KS, HID], F32R)
                y = [ps(st, f"f0_y{n}", [P, BANK]) for n in range(8)]
                w_scaled, w_clipped, hi_done, lo_done = sem("f0_wsc"), sem("f0_wcl"), sem("f0_hi"), sem("f0_lo")
                y_ready, y_read = sem("f0_yready"), sem("f0_yread")
                HB = HID // BANK
                lead = [(t, half) for t in range(G) for half in range(HB)]
                rest = [(t, half) for t in range(G, TT) for half in range(HB)]

                with nc.Block() as block:
                    @block.scalar
                    def _(act):
                        for k in range(KS + 1):
                            if k < KS:
                                act.activation(w[:, k, :], w[:, k, :], ACT.Copy, scale=scl[:, 1:2]).then_inc(w_scaled, 1)
                            if k:
                                act.wait_ge(w_clipped, k)
                                act.activation(w_hi[:, k - 1, :], w[:, k - 1, :], ACT.Copy).then_inc(hi_done, 1)

                    @block.gpsimd
                    def _(pool):
                        for k in range(KS):
                            pool.wait_ge(hi_done, k + 1)
                            pool.tensor_tensor(w_lo[:, k, :], w[:, k, :], f32(w_hi[:, k, :]), ALU.subtract).then_inc(lo_done, 1)

                    @block.vector
                    def _(dve):
                        for k in range(KS):
                            dve.wait_ge(w_scaled, k + 1)
                            dve.tensor_scalar(w[:, k, :], w[:, k, :], LIMIT, -LIMIT, ALU.min, ALU.max).then_inc(w_clipped, 1)
                        for n, (t, half) in enumerate(lead + rest):
                            dve.wait_ge(y_ready, n + 1)
                            cols = x_sb[:, t, half * BANK:(half + 1) * BANK]
                            dve.scalar_tensor_tensor(out=cols, in0=y[n % 8][:], scalar=scl[:, 2:3], in1=cols,
                                                     op0=ALU.mult, op1=ALU.add).then_inc(y_read, 1)

                    @block.tensor
                    def _(pe):
                        def slab(n, t, half, k):
                            return product(pe, y[n % 8][:], xt_hi[:, k, t * P:(t + 1) * P], xt_lo[:, k, t * P:(t + 1) * P],
                                           w_hi[:, k, half * BANK:(half + 1) * BANK], w_lo[:, k, half * BANK:(half + 1) * BANK],
                                           k == 0, k == KS - 1)
                        for k in range(KS):
                            pe.wait_ge(lo_done, k + 1)
                            for n, (t, half) in enumerate(lead):
                                mm = slab(n, t, half, k)
                                if k == KS - 1:
                                    mm.then_inc(y_ready, 1)
                        for n, (t, half) in enumerate(rest):
                            pe.wait_ge(y_read, n + 1)
                            for k in range(KS):
                                mm = slab(n + 8, t, half, k)
                            mm.then_inc(y_ready, 1)

        def routed_lora(x_sb):
            EX, RANK = 8, 16
            ER = EX * RANK
            NW = EX + ER
            FACTOR = 2.0 * EX
            with ExitStack() as st:
                xt_hi = sb(st, "f1_xthi", [P, KS, TOKENS], F32R)
                xt_lo = sb(st, "f1_xtlo", [P, KS, TOKENS], F32R)
                a_rows = sb(st, "f1_arows", [ER, HID])
                r_rows = sb(st, "f1_rrows", [EX, HID])
                b_rows = sb(st, "f1_brows", [P, KS, EX, RANK])
                loaded = sem("f1_loaded")
                with ExitStack() as st2:
                    xn = sb(st2, "f1_xn", [P, TT, HID])
                    layer_norm("f1_ln", x_sb, xn, xt_hi, xt_lo, preload=[
                        (a_rows[:], a1.rearrange("h r d -> (h r) d"), loaded), (r_rows[:], wr1, loaded)] + [
                        (b_rows[:, :, e, :], b1[e].rearrange("(m p) r -> p m r", p=P), loaded) for e in range(EX)])
                wra_hi = sb(st, "f1_wrahi", [P, KS, NW], F32R)
                wra_lo = sb(st, "f1_wralo", [P, KS, NW], F32R)
                wb_hi = sb(st, "f1_wbhi", [P, HID], F32R)
                wb_lo = sb(st, "f1_wblo", [P, HID], F32R)
                logit = sb(st, "f1_logit", [P, TT, EX])
                nmax = sb(st, "f1_nmax", [P, TT])
                tot = sb(st, "f1_tot", [P, TT])
                score = sb(st, "f1_score", [P, TT, EX])
                low = sb(st, "f1_low", [P, TT, ER])
                lt_hi = sb(st, "f1_lthi", [P, TT, P], F32R)
                lt_lo = sb(st, "f1_ltlo", [P, TT, P], F32R)
                ya = [ps(st, f"f1_ya{n}", [P, BANK]) for n in range(2)]
                tb = [ps(st, f"f1_tb{n}", [P, P]) for n in range(2)]
                yo = [ps(st, f"f1_yo{n}", [P, BANK]) for n in range(4)]
                names = ("wturned", "whi", "wlo", "aready", "chain", "exped", "low_s", "turned", "lthi_s", "ltlo_s", "oready", "added", "stored")
                w_turned, whi, wlo, a_ready, chain, exped, lowed, turned, lt_hi_s, lt_lo_s, o_ready, added, stored = (sem("f1_" + n) for n in names)

                with nc.Block() as block:
                    @block.sync
                    def _(sp):
                        for t in range(TT):
                            sp.wait_ge(added, 2 * t + 2)
                            sp.dma_start(out_rows[t * P:(t + 1) * P, :], x_sb[:, t, :]).then_inc(stored, 16)
                        sp.wait_ge(stored, 16 * TT)

                    @block.tensor
                    def _(pe):
                        pe.wait_ge(loaded, 16 * (2 + EX))
                        for k in range(KS):
                            if k >= 4:
                                pe.wait_ge(wlo, k - 3)
                            pe.transpose(yo[k % 4][:, 0:EX], r_rows[:, k * P:(k + 1) * P], ident[0:EX, 0:EX])
                            pe.transpose(yo[k % 4][:, EX:NW], a_rows[:, k * P:(k + 1) * P], ident[:]).then_inc(w_turned, 1)
                        for c in range(2):
                            pe.wait_ge(wlo, 5 + c)
                            for m in range(G):
                                last = pe.transpose(yo[c][:, m * P:(m + 1) * P], b_rows[:, G * c + m, :, :].rearrange("p e r -> p (e r)"), ident[:])
                            last.then_inc(w_turned, 1)
                        pe.wait_ge(wlo, KS + 2)

                        def up(t):
                            if t >= 2:
                                pe.wait_ge(lowed, t - 1)
                            for k in range(KS):
                                mm = product(pe, ya[t % 2][:, 0:NW], xt_hi[:, k, t * P:(t + 1) * P], xt_lo[:, k, t * P:(t + 1) * P],
                                             wra_hi[:, k, :], wra_lo[:, k, :], k == 0, k == KS - 1)
                            mm.then_inc(a_ready, 1)

                        def down(t):
                            pe.wait_ge(lowed, t + 1)
                            if t >= 2:
                                pe.wait_ge(lt_lo_s, t - 1)
                            pe.transpose(tb[t % 2][:], low[:, t, :], ident[:]).then_inc(turned, 1)
                            pe.wait_ge(lt_lo_s, t + 1)
                            for c in range(2):
                                n = 2 * t + c
                                if n >= 4:
                                    pe.wait_ge(added, n - 3)
                                product(pe, yo[n % 4][:], lt_hi[:, t, :], lt_lo[:, t, :], wb_hi[:, c * BANK:(c + 1) * BANK],
                                        wb_lo[:, c * BANK:(c + 1) * BANK], True, True).then_inc(o_ready, 1)
                        up(0)
                        for t in range(1, TT):
                            up(t)
                            down(t - 1)
                        down(TT - 1)

                    @block.scalar
                    def _(act):
                        for k in range(KS):
                            act.wait_ge(w_turned, k + 1)
                            act.activation(wra_hi[:, k, :], yo[k % 4][:, 0:NW], ACT.Copy).then_inc(whi, 1)
                        for c in range(2):
                            act.wait_ge(w_turned, KS + c + 1)
                            act.activation(wb_hi[:, c * BANK:(c + 1) * BANK], yo[c][:], ACT.Copy).then_inc(whi, 1)
                        for t in range(TT):
                            act.wait_ge(chain, 2 * t + 2)
                            act.activation(score[:, t, :], logit[:, t, :], ACT.Exp, bias=nmax[:, t:t + 1], accum_out=tot[:, t:t + 1]).then_inc(exped, 1)
                            act.wait_ge(turned, t + 1)
                            act.activation(lt_hi[:, t, :], tb[t % 2][:], ACT.Copy).then_inc(lt_hi_s, 1)

                    @block.vector
                    def _(dve):
                        for k in range(KS):
                            dve.wait_ge(whi, k + 1)
                            dve.tensor_tensor(wra_lo[:, k, :], yo[k % 4][:, 0:NW], f32(wra_hi[:, k, :]), ALU.subtract).then_inc(wlo, 1)
                        for c in range(2):
                            dve.wait_ge(whi, KS + c + 1)
                            dve.tensor_tensor(wb_lo[:, c * BANK:(c + 1) * BANK], yo[c][:], f32(wb_hi[:, c * BANK:(c + 1) * BANK]),
                                              ALU.subtract).then_inc(wlo, 1)
                        scores_s = sem("f1_scores_s")
                        for t in range(TT):
                            dve.wait_ge(a_ready, t + 1)
                            dve.tensor_tensor(logit[:, t, :], ya[t % 2][:, 0:EX], brb[:], ALU.add).then_inc(chain, 1)
                            dve.wait_ge(chain, 2 * t + 1)
                            dve.tensor_reduce(nmax[:, t:t + 1], logit[:, t, :], AX.X, ALU.max, negate=True).then_inc(chain, 1)
                            dve.wait_ge(exped, t + 1)
                            dve.reciprocal(tot[:, t:t + 1], tot[:, t:t + 1]).then_inc(scores_s, 1)
                            dve.wait_ge(scores_s, 2 * t + 1)
                            dve.tensor_scalar(score[:, t, :], score[:, t, :], tot[:, t:t + 1], FACTOR, ALU.mult, ALU.mult).then_inc(scores_s, 1)
                            dve.wait_ge(scores_s, 2 * t + 2)
                            dve.tensor_tensor(low[:, t, :].rearrange("p (e r) -> p e r", e=EX), ya[t % 2][:, EX:NW].rearrange("p (e r) -> p e r", e=EX),
                                              score[:, t, :].unsqueeze(2).broadcast_to([P, EX, RANK]), ALU.mult).then_inc(lowed, 1)
                            dve.wait_ge(lt_hi_s, t + 1)
                            dve.tensor_tensor(lt_lo[:, t, :], tb[t % 2][:], f32(lt_hi[:, t, :]), ALU.subtract).then_inc(lt_lo_s, 1)
                            for c in range(2):
                                dve.wait_ge(o_ready, 2 * t + c + 1)
                                cols = x_sb[:, t, c * BANK:(c + 1) * BANK]
                                dve.scalar_tensor_tensor(out=cols, in0=yo[(2 * t + c) % 4][:], scalar=gates[:, 3:4], in1=cols,
                                                         op0=ALU.mult, op1=ALU.add).then_inc(added, 1)

        def attend(n, L, x_sb, wo, source=None):
            with ExitStack() as st:
                oT = sb(st, f"oT{n}", [L.d, L.units, G * QLEN])
                rinv = sb(st, f"rinv{n}", [QLEN, L.units, G])
                attention(f"at{n}", L, oT, rinv)
                next_stage()
                out_project(f"o{n}", L, oT, rinv, wo, x_sb, n, source=source)
                next_stage()

        def norm_and_query(n, L, wq, x_sb=None, source=None):
            with ExitStack() as st:
                xt_hi = sb(st, f"xthi{n}", [P, KS, TOKENS], F32R)
                xt_lo = sb(st, f"xtlo{n}", [P, KS, TOKENS], F32R)
                with ExitStack() as st2:
                    rows = x_sb if x_sb is not None else sb(st2, f"x_rows{n}", [P, TT, HID])
                    xn = sb(st2, f"xn{n}", [P, TT, HID])
                    layer_norm(f"a{n}_ln", rows, xn, xt_hi, xt_lo, source=source, to_dram=True)
                queries(f"q{n}", L, xt_hi, xt_lo, wq, not L.normed)
                next_stage()

        constants()
        norm_and_query(0, L0, wq0, source=x_rows)
        keys_values("kv0", L0, wk0, wv0, False)
        next_stage()
        x_sb = sb(stack, "x_sb", [P, TT, HID])
        attend(0, L0, x_sb, wo0, source=x_rows)
        scaled_ffn(x_sb)
        next_stage()
        norm_and_query(1, L1, wq1, x_sb=x_sb)
        keys_values("kv1", L1, wk1, wv1, True)
        next_stage()
        attend(1, L1, x_sb, wo1)
        routed_lora(x_sb)


_INS = ["x", "ctx_4096", "g_xattn", "g_ffn", "L0_xattn_Wq", "L0_xattn_Wk", "L0_xattn_Wv", "L0_xattn_Wo",
        "L0_xattn_q_norm_w", "L0_xattn_k_norm_w", "L0_ffn_weight", "L1_xattn_Wq", "L1_xattn_Wk", "L1_xattn_Wv",
        "L1_xattn_Wo", "L1_ffn_A", "L1_ffn_B", "L1_ffn_Wr", "L1_ffn_br"]


def kernel(**inputs):
    import numpy as _np
    import concourse.bacc as _bacc
    from concourse import mybir as _mybir
    from concourse.bass_utils import run_bass_kernel_spmd as _run

    nc = _bacc.Bacc("TRN2", target_bir_lowering=False, num_devices=1)
    arrays, args = {}, []
    for name in _INS:
        a = _np.ascontiguousarray(inputs[name])
        arrays[f"in_{name}_dram"] = a
        args.append(nc.dram_tensor(f"in_{name}_dram", a.shape, _mybir.dt.from_np(a.dtype), kind="ExternalInput").ap())
    args.append(nc.dram_tensor("out_0_dram", (BATCH, QLEN, HID), _mybir.dt.float32, kind="ExternalOutput").ap())
    flamingo(nc, *args)
    r = _run(nc, [arrays], core_ids=[0])
    return r.results[0]["out_0_dram"]
```

```python
from contextlib import ExitStack

import numpy as np

import concourse.bass as bass
from concourse import mybir

F32 = mybir.dt.float32
F32R = mybir.dt.float32r
ACT = mybir.ActivationFunctionType
ALU = mybir.AluOpType
AX = mybir.AxisListType

BATCH, QLEN, HID = 8, 112, 1024
CTX = 375
KVLEN = CTX + QLEN
KVPAD = KVLEN + 1
TOKENS = BATCH * QLEN
P = 128
TT = TOKENS // P
KS = HID // P
CT = 3
CR = CTX // CT
PT = 2 * CT
ROWS = [CR] * CT + [QLEN]
KVT = len(ROWS)
BANK = 512
G = 4



def f32(ap):
    return ap.bitcast(F32)


def product(pe, out, stat_hi, stat_lo, mov_hi, mov_lo, start, stop):
    pe.matmul(out, stat_hi, mov_hi, start=start, stop=False)
    pe.matmul(out, stat_hi, mov_lo, start=False, stop=False)
    return pe.matmul(out, stat_lo, mov_hi, start=False, stop=stop)


class Layer:

    def __init__(self, heads, kv_heads, dim, normed):
        self.heads, self.kvh, self.d, self.normed = heads, kv_heads, dim, normed
        self.cw = G * dim
        self.nkc = kv_heads // G
        self.units = BATCH * kv_heads
        self.scale = float(dim) ** -0.5


L0 = Layer(32, 8, 128, True)
L1 = Layer(16, 4, 96, False)


def flamingo(nc, x, ctx4096, g_xattn, g_ffn, wq0, wk0, wv0, wo0, qw0, kw0, wffn0,
             wq1, wk1, wv1, wo1, a1, b1, wr1, br1, out):
    stack = ExitStack()

    in_use = []

    def sem(name):
        in_use.append(nc.alloc_semaphore(name=name))
        return in_use[-1]

    def next_stage():
        nc.clear_and_free_semaphores(in_use)
        in_use.clear()
        nc.all_engine_barrier()

    def sb(st, name, shape, dt=F32):
        return st.enter_context(nc.sbuf_tensor(name, shape, dt))

    def ps(st, name, shape):
        return st.enter_context(nc.psum_tensor(name, shape, F32))

    def dram(name, shape, dt=F32):
        return nc.dram_tensor(name, shape, dt, kind="Internal").ap()

    x_rows = x.rearrange("b q h -> (b q) h")
    out_rows = out.rearrange("b q h -> (b q) h")
    ctx_rows = ctx4096.rearrange("b s h -> (b s) h")

    scratch = {}
    for n, L in enumerate((L0, L1)):
        scratch[L] = (dram(f"qT{n}_d", (L.kvh, L.d, G, TOKENS)),
                      (dram(f"kT{n}_d", (L.units, L.d, CTX)), dram(f"kl{n}_d", (L.kvh, L.d, TOKENS))),
                      (dram(f"v{n}_d", (BATCH * CTX, L.kvh * L.d)), dram(f"vl{n}_d", (TOKENS, L.kvh * L.d))),
                      dram(f"rT{n}_d", (BATCH, L.heads, QLEN)))

    with stack:
        ident = sb(stack, "ident", [P, P])
        gates = sb(stack, "gates", [P, 4])
        eps5 = sb(stack, "eps5", [P, 1])
        eps6 = sb(stack, "eps6", [P, 1])
        qw = sb(stack, "qw", [P, 1])
        kw = sb(stack, "kw", [P, 1])
        brb = sb(stack, "brb", [P, 8])

        def constants(ahead):
            loaded, zeroed, diag, gated = sem("c_loaded"), sem("c_zeroed"), sem("c_diag"), sem("c_gated")
            with nc.Block() as block:
                @block.sync
                def _(sp):
                    for dst, src, arrived in ahead[:1]:
                        sp.dma_start(dst, src).then_inc(arrived, 16)
                    sp.dma_start(gates[:, 0:2], g_xattn.rearrange("(a n) -> a n", a=1).broadcast_to([P, 2])).then_inc(loaded, 16)
                    sp.dma_start(gates[:, 2:4], g_ffn.rearrange("(a n) -> a n", a=1).broadcast_to([P, 2])).then_inc(loaded, 16)
                    sp.dma_start(qw[:], qw0.rearrange("(n a) -> n a", a=1)).then_inc(loaded, 16)
                    sp.dma_start(kw[:], kw0.rearrange("(n a) -> n a", a=1)).then_inc(loaded, 16)
                    sp.dma_start(brb[:], br1.rearrange("(a n) -> a n", a=1).broadcast_to([P, 8])).then_inc(loaded, 16)
                    for dst, src, arrived in ahead[1:]:
                        sp.dma_start(dst, src).then_inc(arrived, 16)

                @block.gpsimd
                def _(pool):
                    pool.memset(ident[:], 0.0).then_inc(zeroed, 1)
                    pool.memset(eps5[:], 1e-5)
                    pool.memset(eps6[:], 1e-6)
                    pool.wait_ge(zeroed, 1)
                    pool.affine_select(out=ident[:], in_=ident[:], compare_op=ALU.not_equal, fill=1.0,
                                       base=0, pattern=[[-1, P]], channel_multiplier=1).then_inc(diag, 1)
                    pool.wait_ge(diag, 1)

                @block.scalar
                def _(act):
                    act.wait_ge(loaded, 80)
                    act.activation(gates[:], gates[:], ACT.Tanh).then_inc(gated, 1)

                @block.vector
                def _(dve):
                    dve.wait_ge(loaded, 80)
                    dve.tensor_scalar(qw[:], qw[:], L0.scale, None, ALU.mult).then_inc(gated, 1)

        def layer_norm(tag, x_sb, xn, xt_hi=None, xt_lo=None, x_loaded=None, preload=(), xt=None, tops=None):
            with ExitStack() as st:
                stats = sb(st, f"{tag}_stats", [P, TT, 2, 6])
                mv = sb(st, f"{tag}_mv", [P, TT, 2])
                rstd = sb(st, f"{tag}_rstd", [P, TT])
                shift = sb(st, f"{tag}_shift", [P, TT])
                banks = [ps(st, f"{tag}_ps{i}", [P, G, P]) for i in range(4)]
                s_stats, s_mv, s_sd, s_rstd, s_shift, s_xn, turned, hi_done, lo_done = (
                    sem(f"{tag}_{n}") for n in ("stats_s", "mv_s", "sd_s", "rstd_s", "shift_s", "xn_s", "turned", "hi_s", "lo_s"))
                with nc.Block() as block:
                    @block.sync
                    def _(sp):
                        for dst, src, arrived in preload:
                            sp.dma_start(dst, src).then_inc(arrived, 16)

                    @block.vector
                    def _(dve):
                        for step in range(TT + 3):
                            if step < TT:
                                t = step
                                if x_loaded is not None:
                                    dve.wait_ge(x_loaded[t], 16)
                                for h in range(2):
                                    dve.bn_stats(stats[:, t, h, :], x_sb[:, t, h * BANK:(h + 1) * BANK]).then_inc(s_stats, 1)
                                dve.wait_ge(s_stats, 2 * t + 2)
                                dve.bn_aggr(mv[:, t, :], stats[:, t, :, :]).then_inc(s_mv, 1)
                            if 1 <= step <= TT:
                                dve.wait_ge(s_sd, step)
                                dve.reciprocal(rstd[:, step - 1:step], rstd[:, step - 1:step]).then_inc(s_rstd, 1)
                                dve.wait_ge(s_rstd, step)
                                dve.scalar_tensor_tensor(out=shift[:, step - 1:step], in0=mv[:, step - 1, 0:1], scalar=-1.0,
                                                         in1=rstd[:, step - 1:step], op0=ALU.mult, op1=ALU.mult).then_inc(s_shift, 1)
                            if tops is not None:
                                w, w_loaded, x_tops, w_tops, topped = tops
                                if 2 <= step < TT + 2:
                                    dve.wait_ge(s_xn, step - 1)
                                    dve.tensor_reduce(x_tops[:, step - 2:step - 1], xn[:, step - 2, :], AX.X, ALU.max,
                                                      apply_absolute_value=True).then_inc(topped, 1)
                                for k in [step - 3] if step < TT + 2 else [step - 3, step - 2]:
                                    if k >= 0:
                                        dve.wait_ge(w_loaded[k], 16)
                                        dve.tensor_reduce(w_tops[:, k:k + 1], w[:, k, :], AX.X, ALU.max,
                                                          apply_absolute_value=True).then_inc(topped, 1)
                            if xt is None and step >= 3:
                                for q in range(KS // G):
                                    t, n = step - 3, 2 * (step - 3) + q
                                    dve.wait_ge(hi_done, n + 1)
                                    dve.tensor_tensor(xt_lo[:, G * q:G * q + G, t * P:(t + 1) * P], banks[n % 4][:],
                                                      f32(xt_hi[:, G * q:G * q + G, t * P:(t + 1) * P]), ALU.subtract).then_inc(lo_done, 1)

                    @block.tensor
                    def _(pe):
                        for n in range(2 * TT):
                            t, q = n // 2, n % 2
                            pe.wait_ge(s_xn, t + 1)
                            if n >= 4:
                                pe.wait_ge(lo_done if xt is None else hi_done, n - 3)
                            for j in range(G):
                                last = pe.transpose(banks[n % 4][:, j, :],
                                                    xn[:, t, (G * q + j) * P:(G * q + j + 1) * P], ident[:])
                            last.then_inc(turned, 1)

                    @block.scalar
                    def _(act):
                        for step in range(TT + 2):
                            if step < TT:
                                act.wait_ge(s_mv, step + 1)
                                act.activation(rstd[:, step:step + 1], mv[:, step, 1:2], ACT.Sqrt, bias=eps5[:]).then_inc(s_sd, 1)
                            if 1 <= step <= TT:
                                t = step - 1
                                act.wait_ge(s_shift, step)
                                act.activation(xn[:, t, :], x_sb[:, t, :], ACT.Identity, scale=rstd[:, t:t + 1],
                                               bias=shift[:, t:t + 1]).then_inc(s_xn, 1)
                            if step >= 2:
                                for q in range(KS // G):
                                    t, n = step - 2, 2 * (step - 2) + q
                                    act.wait_ge(turned, n + 1)
                                    act.activation((xt_hi if xt is None else xt)[:, G * q:G * q + G, t * P:(t + 1) * P], banks[n % 4][:],
                                                   ACT.Copy).then_inc(hi_done, 1)

        class Weights:

            def __init__(self, tag, st, L, fetch, turned_first, bufs=1):
                self.L, self.fetch, self.flip, self.bufs = L, fetch, turned_first, bufs
                self.nr = L.cw // P
                shape = [P, bufs, self.nr, HID] if self.flip else [P, bufs, KS, L.cw]
                self.raw = sb(st, f"{tag}_raw", shape)
                self.loaded = [sem(f"{tag}_w_loaded{b}") for b in range(bufs)]
                self.turned, self.hi_done, self.lo_dve, self.lo_pool = (
                    sem(f"{tag}_{n}") for n in ("w_turned", "w_hi", "w_lodve", "w_lopool"))

            def place(self, hi, lo, banks):
                self.hi, self.lo, self.banks = hi, lo, banks

            def ahead(self, c):
                return self.raw[:, self.buffer(c)], self.fetch(c), self.loaded[self.buffer(c)]

            def buffer(self, c):
                return c % self.bufs if self.bufs > 1 else 0

            def load(self, sp, c):
                b = self.buffer(c)
                sp.dma_start(self.raw[:, b], self.fetch(c)).then_inc(self.loaded[b], 16)

            def wait_loaded(self, eng, c):
                eng.wait_ge(self.loaded[self.buffer(c)], 16 * (c // self.bufs if self.bufs > 1 else c) + 16)

            def turn(self, pe, c, k):
                if self.flip:
                    if k == 0:
                        self.wait_loaded(pe, c)
                    if k >= 2:
                        pe.wait_ge(self.lo_dve, KS * c + k - 1)
                    for m in range(self.nr):
                        last = pe.transpose(self.banks[k % 2][:, m * P:(m + 1) * P], self.raw[:, self.buffer(c), m, k * P:(k + 1) * P], ident[:])
                    last.then_inc(self.turned, 1)

            def slab(self, c, k):
                return self.banks[k % 2][:, 0:self.L.cw] if self.flip else self.raw[:, self.buffer(c), k, :]

            def cut_hi(self, act, b, c, k):
                if self.flip:
                    act.wait_ge(self.turned, KS * c + k + 1)
                elif k == 0:
                    self.wait_loaded(act, c)
                act.activation(self.hi[:, b, k, :], self.slab(c, k), ACT.Copy).then_inc(self.hi_done, 1)

            def on_dve(self, k):
                return self.flip or k % 2 == 0

            def cut_lo(self, eng, b, c, k):
                eng.wait_ge(self.hi_done, KS * c + k + 1)
                eng.tensor_tensor(self.lo[:, b, k, :], self.slab(c, k), f32(self.hi[:, b, k, :]),
                                  ALU.subtract).then_inc(self.lo_dve if self.on_dve(k) else self.lo_pool, 1)

            def wait_slab(self, eng, c, k):
                if self.flip:
                    eng.wait_ge(self.lo_dve, KS * c + k + 1)
                else:
                    eng.wait_ge(self.lo_dve if self.on_dve(k) else self.lo_pool, KS // 2 * c + k // 2 + 1)

            def wait(self, eng, chunks):
                if self.flip:
                    eng.wait_ge(self.lo_dve, KS * chunks)
                else:
                    eng.wait_ge(self.lo_dve, KS // 2 * chunks)
                    eng.wait_ge(self.lo_pool, KS // 2 * chunks)

        def chunk_of(w, L, turned_first):
            if turned_first:
                return lambda c: w[bass.ds(c * L.cw, L.cw), :].rearrange("(m p) k -> p m k", p=P)
            v = w.rearrange("(k p) n -> p k n", p=P)
            return lambda c: v[:, :, bass.ds(c * L.cw, L.cw)]

        def latents(tag, L, xt_hi, xt_lo, W, ahead):
            CW, D = L.cw, L.d
            QP = L.kvh // 2
            qT_d, (_, kl_d), (_, vl_d), _ = scratch[L]
            extra = [("K", c) for c in range(L.nkc)] + [("V", c) for c in range(L.nkc)]
            PAIR = 2 * TT
            with ExitStack() as st:
                w_hi = sb(st, f"{tag}_whi", [P, 2, KS, CW], F32R)
                w_lo = sb(st, f"{tag}_wlo", [P, 2, KS, CW], F32R)
                sq = sb(st, f"{tag}_sq", [P, CW])
                inv = sb(st, f"{tag}_inv", [P, 2, G])
                qn = sb(st, f"{tag}_qn", [P, 2, CW])
                stage = sb(st, f"{tag}_stage", [P, 2, G, P])
                y = [ps(st, f"{tag}_y{i}", [P, BANK]) for i in range(2)]
                qt = [ps(st, f"{tag}_qt{i}", [P, G, P]) for i in range(2)]
                wt = [ps(st, f"{tag}_wt{i}", [P, BANK]) for i in range(2)]
                W.place(w_hi, w_lo, wt)
                squared, summed, rooted, inverted = (sem(f"{tag}_{n}") for n in ("sq_s", "sum_s", "root_s", "inv_s"))
                y_ready = sem(f"{tag}_yready")
                normed, turned, staged = ([sem(f"{tag}_{n}{p}") for p in range(2)] for n in ("norm", "turned", "staged"))
                stored = [sem(f"{tag}_stored{p}") for p in range(2)]
                primed = sem(f"{tag}_primed")

                def slabs(t):
                    return [[0, 1], [2, 3], [4, 5], [6, 7], [], [], []][t]

                def walk(eng, pair):
                    queries = (("Q", 0), ("Q", 0))
                    pair(0, queries, True, None)
                    if QP > 2:
                        with eng.Fori(1, QP - 1) as i:
                            pair(i, queries, True, queries)
                    pair(QP - 1, queries, True, queries)
                    before = queries
                    for e in range(L.nkc):
                        kinds = extra[2 * e:2 * e + 2]
                        pair(QP + e, kinds, e < L.nkc - 1, before)
                        before = kinds

                def target(kinds, i, c, t):
                    kind, m = kinds[c]
                    if kind == "Q":
                        return qT_d[2 * i + c, :, :, t * P:(t + 1) * P]
                    if kind == "K":
                        return kl_d[m * G:(m + 1) * G, :, t * P:(t + 1) * P].rearrange("g d s -> d g s")
                    return vl_d[t * P:(t + 1) * P, m * CW:(m + 1) * CW]

                def staging(kinds, c, p):
                    if kinds[c][0] == "V":
                        return stage[:, p, :, :].rearrange("p g s -> p (g s)")[:, 0:CW]
                    return stage[0:D, p, :, :]

                with nc.Block() as block:
                    @block.sync
                    def _(sp):
                        W.wait(sp, 1)
                        W.load(sp, 1)

                        def pair(i, kinds, more, before):
                            if not more:
                                for dst, src, arrived in ahead:
                                    sp.dma_start(dst, src).then_inc(arrived, 16)
                            for n in range(PAIR):
                                c, t = n // TT, n % TT
                                if t == 4 and more:
                                    W.wait(sp, 2 * i + c + 2)
                                    W.load(sp, 2 * i + c + 2)
                                sp.wait_ge(staged[n % 2], TT * i + n // 2 + 2)
                                sp.dma_start(target(kinds, i, c, t), staging(kinds, c, n % 2)).then_inc(stored[n % 2], 16)
                        walk(sp, pair)
                        for p in range(2):
                            sp.wait_ge(stored[p], 16 * TT * (QP + L.nkc) + 1)

                    @block.gpsimd
                    def _(pool):
                        for p in range(2):
                            pool.sem_inc(stored[p], 1)
                        if not W.flip:
                            for k in range(1, KS, 2):
                                W.cut_lo(pool, 0, 0, k)

                            def pair(i, kinds, more, before):
                                for n in range(PAIR):
                                    c, t = n // TT, n % TT
                                    if more or c == 0:
                                        for k in slabs(t):
                                            if not W.on_dve(k):
                                                W.cut_lo(pool, 1 - c, 2 * i + c + 1, k)
                            walk(pool, pair)

                    @block.tensor
                    def _(pe):
                        def turn(i, kinds, n):
                            p = n % 2
                            pe.wait_ge(normed[p], TT * i + n // 2 + 2)
                            pe.wait_ge(staged[p], TT * i + n // 2 + 1)
                            if kinds[n // TT][0] == "V":
                                pe.sem_inc(turned[p], 1)
                                return
                            for h in range(G):
                                last = pe.transpose(qt[p][0:D, h, :], qn[:, p, h * D:(h + 1) * D], ident[:])
                            last.then_inc(turned[p], 1)

                        def pair(i, kinds, more, before):
                            for n in range(PAIR):
                                c, t, p = n // TT, n % TT, n % 2
                                pe.wait_ge(normed[p], TT * i + n // 2 + 1)
                                for k in range(KS):
                                    if t == 0:
                                        W.wait_slab(pe, 2 * i + c, k)
                                    last = product(pe, y[p][:, 0:CW], xt_hi[:, k, t * P:(t + 1) * P], xt_lo[:, k, t * P:(t + 1) * P],
                                                   w_hi[:, c, k, :], w_lo[:, c, k, :], k == 0, k == KS - 1)
                                last.then_inc(y_ready, 1)
                                if n:
                                    turn(i, kinds, n - 1)
                                elif before:
                                    turn(i - 1, before, PAIR - 1)
                                if more or c == 0:
                                    for k in slabs(t):
                                        W.turn(pe, 2 * i + c + 1, k)

                        for p in range(2):
                            pe.sem_inc(turned[p], 1)
                        for k in range(KS):
                            W.turn(pe, 0, k)
                        walk(pe, pair)
                        turn(QP + L.nkc - 1, extra[-2:], PAIR - 1)

                    @block.scalar
                    def _(act):
                        def put(i, kinds, n):
                            p = n % 2
                            act.wait_ge(turned[p], TT * i + n // 2 + 2)
                            act.wait_ge(stored[p], 16 * (TT * i + n // 2) + 1)
                            kind = kinds[n // TT][0]
                            if kind == "V":
                                act.activation(staging(kinds, n // TT, p), qn[:, p, :], ACT.Copy).then_inc(staged[p], 1)
                                return
                            scale = {"Q": L.scale, "K": 1.0} if not L.normed else {"Q": qw[0:D, :], "K": kw[0:D, :]}
                            act.activation(stage[0:D, p, :, :], qt[p][0:D, :, :], ACT.Copy, scale=scale[kind]).then_inc(staged[p], 1)

                        def pair(i, kinds, more, before):
                            for n in range(PAIR):
                                c, t, p = n // TT, n % TT, n % 2
                                m = PAIR * i + n
                                act.wait_ge(y_ready, m + 1)
                                if L.normed and kinds[c][0] != "V":
                                    act.wait_ge(summed, m + 1)
                                    act.activation(sq[:], y[p][:, 0:CW], ACT.Square).then_inc(squared, 1)
                                    act.wait_ge(summed, m + 2)
                                    act.activation(inv[:, p, :], inv[:, p, :], ACT.Sqrt, scale=1.0 / D, bias=eps6[:]).then_inc(rooted, 1)
                                else:
                                    act.wait_ge(turned[p], TT * i + n // 2 + 1)
                                    if kinds[c][0] == "V":
                                        act.wait_ge(staged[p], TT * i + n // 2 + 1)
                                    act.activation(qn[:, p, :], y[p][:, 0:CW], ACT.Copy).then_inc(normed[p], 1)
                                if more or c == 0:
                                    for k in slabs(t):
                                        W.cut_hi(act, 1 - c, 2 * i + c + 1, k)
                                if n:
                                    put(i, kinds, n - 1)
                                elif before:
                                    put(i - 1, before, PAIR - 1)

                        for p in range(2):
                            act.sem_inc(staged[p], 1)
                            if not L.normed:
                                act.sem_inc(normed[p], 1)
                        for k in range(KS):
                            W.cut_hi(act, 0, 0, k)
                        walk(act, pair)
                        put(QP + L.nkc - 1, extra[-2:], PAIR - 1)

                    @block.vector
                    def _(dve):
                        def pair(i, kinds, more, before):
                            for n in range(PAIR):
                                c, t, p = n // TT, n % TT, n % 2
                                m = PAIR * i + n
                                if L.normed and kinds[c][0] != "V":
                                    dve.wait_ge(squared, m + 1)
                                    dve.tensor_reduce(inv[:, p, :], sq[:].rearrange("p (g d) -> p g d", g=G), AX.X, ALU.add).then_inc(summed, 1)
                                    dve.wait_ge(rooted, m + 1)
                                    dve.reciprocal(inv[:, p, :], inv[:, p, :]).then_inc(inverted, 1)
                                    dve.wait_ge(inverted, m + 1)
                                    dve.wait_ge(turned[p], TT * i + n // 2 + 1)
                                    dve.tensor_tensor(qn[:, p, :].rearrange("p (g d) -> p g d", g=G),
                                                      y[p][:, 0:CW].rearrange("p (g d) -> p g d", g=G),
                                                      inv[:, p, :].unsqueeze(2).broadcast_to([P, G, D]), ALU.mult).then_inc(normed[p], 1)
                                if more or c == 0:
                                    for k in slabs(t):
                                        if W.on_dve(k):
                                            W.cut_lo(dve, 1 - c, 2 * i + c + 1, k)

                        if L.normed:
                            dve.sem_inc(summed, 1)
                            for p in range(2):
                                dve.sem_inc(normed[p], 1)
                        for k in range(KS):
                            if W.on_dve(k):
                                W.cut_lo(dve, 0, 0, k)
                        walk(dve, pair)

        def context(tag, L, W, xin, x_loaded, source):
            CW, D, NK, T, R = L.cw, L.d, L.nkc, PT, CR
            C = 2 * NK
            _, (kT_d, _), (v_d, _), _ = scratch[L]
            order = {4: ["Y0", "Y1", "X0", "Y2", "K0", "Y3", "K1"], 2: ["Y0", "X0", "Y1", "K0"]}[C]
            with ExitStack() as st:
                w_hi = sb(st, f"{tag}_whi", [P, C, KS, CW], F32R)
                w_lo = sb(st, f"{tag}_wlo", [P, C, KS, CW], F32R)
                xt_hi = sb(st, f"{tag}_xthi", [P, 2, KS, P], F32R)
                xt_lo = sb(st, f"{tag}_xtlo", [P, 2, KS, P], F32R)
                sq = sb(st, f"{tag}_sq", [P, CW])
                inv = sb(st, f"{tag}_inv", [P, NK, G])
                yn = sb(st, f"{tag}_yn", [P, NK, CW])
                stage = sb(st, f"{tag}_stage", [P, C, BANK])
                y = [ps(st, f"{tag}_y{c}", [P, BANK]) for c in range(C)]
                xb = [ps(st, f"{tag}_xb{q}", [P, G, P]) for q in range(2)]
                tb = [ps(st, f"{tag}_tb{c}", [P, G, P]) for c in range(2)]
                W.place(w_hi, w_lo, [b.ap().rearrange("p g s -> p (g s)") for b in tb])
                x_turned, x_hi_done, x_lo_done, y_ready = (sem(f"{tag}_{n}") for n in ("xturn", "xhi_s", "xlo_s", "yready"))
                squared, summed, rooted, inverted = (sem(f"{tag}_{n}") for n in ("sq_s", "sum_s", "root_s", "inv_s"))
                normed = [sem(f"{tag}_norm{c}") for c in range(NK)]
                turned = [sem(f"{tag}_turned{c}") for c in range(NK)]
                staged = [sem(f"{tag}_staged{c}") for c in range(C)]
                stored = [sem(f"{tag}_stored{c}") for c in range(C)]
                y_read = normed + staged[NK:]

                def target(c, i, j):
                    if c < NK:
                        unit = i * (2 * L.kvh) + (j // CT * L.kvh + c * G)
                        return kT_d[bass.ds(unit, G), :, j % CT * R:(j % CT + 1) * R].rearrange("u d s -> d u s")
                    return v_d[bass.ds(i * (T * R) + j * R, R), (c - NK) * CW:(c - NK + 1) * CW]

                def staging(c):
                    if c < NK:
                        return stage[0:D, c, :].rearrange("p (g s) -> p g s", g=G)[:, :, 0:R]
                    return stage[0:R, c, 0:CW]

                def walk(eng, step):
                    with eng.Fori(0, BATCH // 2 - 1) as i:
                        for j in range(T):
                            step(i, j, 2)
                    for j in range(T):
                        step(BATCH // 2 - 1, j, min(T - 1 - j, 2))

                with nc.Block() as block:
                    @block.sync
                    def _(sp):
                        for c in range(2, C):
                            W.wait(sp, c - 1)
                            W.load(sp, c)

                        def step(i, j, left):
                            n = i * T + j
                            if left == 2:
                                sp.wait_ge(x_turned, 2 * n + 2)
                                sp.dma_start(xin[0:R, j % 2, :], source(i, j + 2)).then_inc(x_loaded[j % 2], 16)
                            for what in order:
                                c = int(what[1])
                                if what[0] == "K" or (what[0] == "Y" and c >= NK):
                                    sp.wait_ge(staged[c], n + 2)
                                    sp.dma_start(target(c, i, j), staging(c)).then_inc(stored[c], 16)
                        walk(sp, step)
                        for c in range(C):
                            sp.wait_ge(stored[c], 16 * (BATCH // 2) * T + 1)

                    @block.gpsimd
                    def _(pool):
                        for c in range(C):
                            pool.sem_inc(stored[c], 1)
                        if not W.flip:
                            for c in range(C):
                                for k in range(1, KS, 2):
                                    W.cut_lo(pool, c, c, k)

                    @block.tensor
                    def _(pe):
                        def turn_rows(p):
                            for q in range(2):
                                for m in range(G):
                                    k = G * q + m
                                    last = pe.transpose(xb[q][:, m, 0:R], xin[0:R, p, k * P:(k + 1) * P], ident[0:R, 0:R])
                                last.then_inc(x_turned, 1)

                        def step(i, j, left):
                            n, p = i * T + j, j % 2
                            for what in order:
                                c = int(what[1])
                                if what[0] == "Y":
                                    pe.wait_ge(x_lo_done, 2 * n + 2)
                                    pe.wait_ge(y_read[c], n + 1)
                                    for k in range(KS):
                                        if not W.flip:
                                            W.wait_slab(pe, c, k)
                                        last = product(pe, y[c][0:R, 0:CW], xt_hi[:, p, k, 0:R], xt_lo[:, p, k, 0:R],
                                                       w_hi[:, c, k, :], w_lo[:, c, k, :], k == 0, k == KS - 1)
                                    last.then_inc(y_ready, 1)
                                elif what[0] == "X" and left:
                                    pe.wait_ge(x_loaded[1 - p], 16 * (i * (T // 2) + (j + 1) // 2 + 1))
                                    turn_rows(1 - p)
                                elif what[0] == "K":
                                    pe.wait_ge(normed[c], n + 2)
                                    pe.wait_ge(staged[c], n + 1)
                                    for m in range(G):
                                        last = pe.transpose(tb[c][0:D, m, 0:R], yn[0:R, c, m * D:(m + 1) * D], ident[0:R, 0:R])
                                    last.then_inc(turned[c], 1)

                        for c in range(NK):
                            pe.sem_inc(turned[c], 1)
                        pe.wait_ge(x_loaded[0], 16)
                        turn_rows(0)
                        if W.flip:
                            for c in range(C):
                                for k in range(KS):
                                    if k < 2 and c:
                                        W.wait(pe, c)
                                    W.turn(pe, c, k)
                            W.wait(pe, C)
                        walk(pe, step)

                    @block.scalar
                    def _(act):
                        def x_highs(n, p):
                            for q in range(2):
                                act.wait_ge(x_turned, 2 * n + q + 1)
                                act.activation(xt_hi[:, p, G * q:G * q + G, 0:R], xb[q][:, :, 0:R], ACT.Copy).then_inc(x_hi_done, 1)

                        for c in range(C):
                            act.sem_inc(staged[c], 1)
                        if not L.normed:
                            for c in range(NK):
                                act.sem_inc(normed[c], 1)
                        x_highs(0, 0)
                        for c in range(C):
                            for k in range(KS):
                                W.cut_hi(act, c, c, k)

                        def step(i, j, left):
                            n = i * T + j
                            for what in order:
                                c = int(what[1])
                                if what[0] == "Y":
                                    act.wait_ge(y_ready, C * n + c + 1)
                                    if c >= NK:
                                        act.wait_ge(stored[c], 16 * n + 1)
                                        act.activation(staging(c), y[c][0:R, 0:CW], ACT.Copy).then_inc(staged[c], 1)
                                    elif L.normed:
                                        act.wait_ge(summed, NK * n + c + 1)
                                        act.activation(sq[0:R, :], y[c][0:R, 0:CW], ACT.Square).then_inc(squared, 1)
                                        act.wait_ge(summed, NK * n + c + 2)
                                        act.activation(inv[0:R, c, :], inv[0:R, c, :], ACT.Sqrt, scale=1.0 / D, bias=eps6[0:R, :]).then_inc(rooted, 1)
                                    else:
                                        act.wait_ge(turned[c], n + 1)
                                        act.activation(yn[0:R, c, :], y[c][0:R, 0:CW], ACT.Copy).then_inc(normed[c], 1)
                                elif what[0] == "X" and left:
                                    x_highs(n + 1, 1 - j % 2)
                                elif what[0] == "K":
                                    act.wait_ge(turned[c], n + 2)
                                    act.wait_ge(stored[c], 16 * n + 1)
                                    act.activation(staging(c), tb[c][0:D, :, 0:R], ACT.Copy,
                                                   scale=kw[0:D, :] if L.normed else 1.0).then_inc(staged[c], 1)
                        walk(act, step)

                    @block.vector
                    def _(dve):
                        def x_lows(n, p):
                            for q in range(2):
                                dve.wait_ge(x_hi_done, 2 * n + q + 1)
                                dve.tensor_tensor(xt_lo[:, p, G * q:G * q + G, 0:R], xb[q][:, :, 0:R],
                                                  f32(xt_hi[:, p, G * q:G * q + G, 0:R]), ALU.subtract).then_inc(x_lo_done, 1)

                        if L.normed:
                            dve.sem_inc(summed, 1)
                            for c in range(NK):
                                dve.sem_inc(normed[c], 1)
                        x_lows(0, 0)
                        for c in range(C):
                            for k in range(KS):
                                if W.on_dve(k):
                                    W.cut_lo(dve, c, c, k)

                        def step(i, j, left):
                            n = i * T + j
                            for what in order:
                                c = int(what[1])
                                if what[0] == "Y" and c < NK and L.normed:
                                    dve.wait_ge(squared, NK * n + c + 1)
                                    dve.tensor_reduce(inv[0:R, c, :], sq[0:R, :].rearrange("p (g d) -> p g d", g=G),
                                                      AX.X, ALU.add).then_inc(summed, 1)
                                    dve.wait_ge(rooted, NK * n + c + 1)
                                    dve.reciprocal(inv[0:R, c, :], inv[0:R, c, :]).then_inc(inverted, 1)
                                    dve.wait_ge(inverted, NK * n + c + 1)
                                    dve.wait_ge(turned[c], n + 1)
                                    dve.tensor_tensor(yn[0:R, c, :].rearrange("p (g d) -> p g d", g=G),
                                                      y[c][0:R, 0:CW].rearrange("p (g d) -> p g d", g=G),
                                                      inv[0:R, c, :].unsqueeze(2).broadcast_to([R, G, D]), ALU.mult).then_inc(normed[c], 1)
                                elif what[0] == "X" and left:
                                    x_lows(n + 1, 1 - j % 2)
                        walk(dve, step)

        def attention(tag, L, oT, rinv):
            D, U = L.d, L.units
            qT_d, (kT_d, kl_d), (v_d, vl_d), _ = scratch[L]
            GP = L.kvh // 2
            with ExitStack() as st:
                qr = sb(st, f"{tag}_qr", [D, 2, G * QLEN])
                kr = sb(st, f"{tag}_kr", [D, 2, KVPAD])
                vr = sb(st, f"{tag}_vr", [P, 2, KVT, D])
                qs = sb(st, f"{tag}_q", [D, 2, 2, G * QLEN], F32R)
                ks = sb(st, f"{tag}_k", [D, 2, 2, KVPAD], F32R)
                vs = sb(st, f"{tag}_v", [P, 2, 2, KVT, D], F32R)
                pr = sb(st, f"{tag}_p", [QLEN, 2, G, KVPAD])
                nmax = sb(st, f"{tag}_nmax", [QLEN, 2, G])
                rsum = sb(st, f"{tag}_rsum", [QLEN, 2, G])
                pt_hi = sb(st, f"{tag}_pthi", [P, KVT, G * QLEN], F32R)
                pt_lo = sb(st, f"{tag}_ptlo", [P, KVT, G * QLEN], F32R)
                s = [ps(st, f"{tag}_s{h}", [QLEN, BANK]) for h in range(G)]
                tb = [ps(st, f"{tag}_tb{b}", [P, G * QLEN]) for b in range(2)]
                o = [ps(st, f"{tag}_o{p}", [P, G * QLEN]) for p in range(2)]
                padded = sem(f"{tag}_padded")
                qk_loaded = [sem(f"{tag}_qkl{p}") for p in range(2)]
                v_loaded = [sem(f"{tag}_vl{p}") for p in range(2)]
                k_hi, q_hi = ([sem(f"{tag}_{n}hi{p}") for p in range(2)] for n in "kq")
                v_hi, arrived, k_first = sem(f"{tag}_vhi"), sem(f"{tag}_arrived"), sem(f"{tag}_kfirst")
                qk_cut = [sem(f"{tag}_qkc{p}") for p in range(2)]
                v_cut = [sem(f"{tag}_vc{p}") for p in range(2)]
                scored = [sem(f"{tag}_scored{h}") for h in range(G - 1)]
                qk_used = [sem(f"{tag}_qku{p}") for p in range(2)]
                exped = [sem(f"{tag}_exped{h}") for h in range(G)]
                maxed, inverted = sem(f"{tag}_maxed"), sem(f"{tag}_inverted")
                turned = [sem(f"{tag}_turned{x}") for x in range(KVT)]
                hi_done, lo_done = sem(f"{tag}_hi_s"), sem(f"{tag}_lo_s")
                multiplied = [sem(f"{tag}_mult{x}") for x in range(KVT - 1)]
                v_used = [sem(f"{tag}_vu{p}") for p in range(2)]
                o_read = [sem(f"{tag}_oread{p}") for p in range(2)]

                def walk(eng, step):
                    step(0, 0, 2, True)
                    step(0, 1, 2)
                    with eng.Fori(1, U // 2 - 1) as i:
                        step(i, 0, 2)
                        step(i, 1, 2)
                    step(U // 2 - 1, 0, 1)
                    step(U // 2 - 1, 1, 0)

                ORDER = ["S0", "T0", "S1", "T1", "S2", "S3", "v2", "T2", "v3", "V0", "T3", "V1"]
                ACT_ORDER = ["T0", "q", "T1", "S0", "S1", "T2", "S2", "S3", "T3", "o"]
                DVE_ORDER = ["k", "S0", "T0", "S1", "T1", "S2", "S3", "T2", "T3", "o"]

                with nc.Block() as block:
                    @block.sync
                    def _(sp):
                        sp.wait_ge(padded, 2)
                        with sp.Fori(0, BATCH) as b:
                            with sp.Fori(0, GP) as gp:
                                for p in range(2):
                                    half = b * GP + gp
                                    u = half * 2 + p
                                    sp.wait_ge(qk_cut[p], half + 1)
                                    sp.dma_start(qr[:, p, :].rearrange("d (g s) -> d g s", g=G),
                                                 qT_d[gp * 2 + p, :, :, bass.ds(b * QLEN, QLEN)]).then_inc(qk_loaded[p], 16)
                                    sp.dma_start(kr[:, p, 0:CTX], kT_d[u, :, :]).then_inc(qk_loaded[p], 16)
                                    sp.dma_start(kr[:, p, CTX:KVLEN], kl_d[gp * 2 + p, :, bass.ds(b * QLEN, QLEN)]).then_inc(qk_loaded[p], 16)
                                    sp.wait_ge(v_cut[p], half + 1)
                                    cols = bass.ds((gp * 2 + p) * D, D)
                                    sp.dma_start(vr[0:CR, p, 0:CT, :], v_d[bass.ds(b * CTX, CTX), cols].rearrange("(j r) d -> r j d", r=CR)).then_inc(v_loaded[p], 16)
                                    sp.dma_start(vr[0:QLEN, p, CT, :], vl_d[bass.ds(b * QLEN, QLEN), cols]).then_inc(v_loaded[p], 16)

                    @block.gpsimd
                    def _(pool):
                        pool.memset(kr[:, :, KVLEN:KVPAD], 0.0).then_inc(padded, 1)
                        pool.memset(vr[:, :, CT, :], 0.0).then_inc(padded, 1)
                        for p in range(2):
                            pool.sem_inc(qk_cut[p], 1)
                            pool.sem_inc(v_cut[p], 1)

                        def cut_qk(p, half):
                            if not (isinstance(half, int) and half == 0 and p == 0):
                                pool.wait_ge(k_hi[p], half + 1)
                                pool.tensor_tensor(ks[:, p, 1, :], kr[:, p, :], f32(ks[:, p, 0, :]), ALU.subtract)
                            else:
                                pool.wait_ge(k_first, 1)
                            pool.wait_ge(q_hi[p], half + 1)
                            pool.tensor_tensor(qs[:, p, 1, :], qr[:, p, :], f32(qs[:, p, 0, :]), ALU.subtract).then_inc(qk_cut[p], 1)

                        def cut_v(p, half):
                            pool.wait_ge(v_used[p], half + 1)
                            pool.wait_ge(v_loaded[p], 32 * half + 32)
                            pool.sem_inc(arrived, 1)
                            pool.tensor_copy(vs[0:CR, p, 0, :, :], vr[0:CR, p, :, :]).then_inc(v_hi, 1)
                            pool.wait_ge(v_hi, 2 * half + p + 1)
                            pool.tensor_tensor(vs[0:CR, p, 1, :, :], vr[0:CR, p, :, :], f32(vs[0:CR, p, 0, :, :]), ALU.subtract).then_inc(v_cut[p], 1)

                        def step(i, p, more, first=False):
                            if more == 2:
                                cut_qk(p, i + 1)
                            if more:
                                cut_v(1 - p, i + p)
                        cut_qk(0, 0)
                        cut_v(0, 0)
                        cut_qk(1, 0)
                        walk(pool, step)

                    @block.tensor
                    def _(pe):
                        def scores(p, h, half, u):
                            if h == 0:
                                pe.wait_ge(qk_cut[p], half + 2)
                            if not (isinstance(u, int) and u == 0):
                                pe.wait_ge(exped[h], u)
                            last = product(pe, s[h][:, 0:KVPAD], qs[:, p, 0, h * QLEN:(h + 1) * QLEN], qs[:, p, 1, h * QLEN:(h + 1) * QLEN],
                                           ks[:, p, 0, :], ks[:, p, 1, :], True, True)
                            last.then_inc(scored[h] if h < G - 1 else qk_used[p], 1)

                        def multiply(p, x, i, u):
                            r = ROWS[x]
                            if x == 0:
                                pe.wait_ge(v_cut[p], i + 2)
                                pe.wait_ge(o_read[p], i + 1)
                            pe.wait_ge(lo_done, KVT * u + x + 1)
                            last = product(pe, o[p][0:D, :], vs[0:r, p, 0, x, :], vs[0:r, p, 1, x, :],
                                           pt_hi[0:r, x, :], pt_lo[0:r, x, :], x == 0, x == KVT - 1)
                            last.then_inc(multiplied[x] if x < KVT - 1 else v_used[p], 1)

                        def step(i, p, more, first=False):
                            u = 2 * i + p
                            for what in ORDER:
                                x = int(what[1])
                                if what[0] == "S" and more:
                                    scores(1 - p, x, i + p, u + 1)
                                elif what[0] == "T":
                                    if x == 0:
                                        pe.wait_ge(exped[G - 1], u + 1)
                                    if not first or x >= 2:
                                        pe.wait_ge(lo_done, KVT * u + x - 1)
                                    r = ROWS[x]
                                    for h in range(G):
                                        last = pe.transpose(tb[x % 2][0:r, h * QLEN:(h + 1) * QLEN], pr[:, p, h, x * CR:x * CR + r], ident[0:QLEN, 0:QLEN])
                                    last.then_inc(turned[x], 1)
                                elif what[0] == "V":
                                    multiply(p, x, i, u)
                                elif what[0] == "v" and not first:
                                    multiply(1 - p, x, i + p - 1, u - 1)

                        for one in qk_used + v_used + multiplied + turned:
                            pe.sem_inc(one, 1)
                        for h in range(G):
                            scores(0, h, 0, 0)
                        walk(pe, step)
                        for x in (2, 3):
                            multiply(1, x, U // 2 - 1, U - 1)

                    @block.scalar
                    def _(act):
                        def exp(p, h, u, transposed):
                            act.wait_ge(maxed, G * u + h + 1)
                            if h == 0:
                                act.wait_ge(turned[KVT - 1], transposed + 1)
                            act.activation(pr[:, p, h, 0:KVLEN], s[h][:, 0:KVLEN], ACT.Exp, bias=nmax[:, p, h:h + 1],
                                           accum_out=rsum[:, p, h:h + 1]).then_inc(exped[h], 1)

                        def cut_q(p, half):
                            act.wait_ge(qk_used[p], half + 1)
                            act.wait_ge(qk_loaded[p], 48 * half + 48)
                            act.activation(qs[:, p, 0, :], qr[:, p, :], ACT.Copy).then_inc(q_hi[p], 1)

                        def step(i, p, more, first=False):
                            u = 2 * i + p
                            for what in ACT_ORDER:
                                x = int(what[1:] or 0)
                                if what[0] == "S" and more:
                                    exp(1 - p, x, u + 1, u)
                                elif what[0] == "T":
                                    act.wait_ge(turned[x], u + 2)
                                    if x < KVT - 1:
                                        act.wait_ge(multiplied[x], u + 1)
                                    else:
                                        act.wait_ge(v_used[1 - p], i + p + 1)
                                    act.activation(pt_hi[0:ROWS[x], x, :], tb[x % 2][0:ROWS[x], :], ACT.Copy).then_inc(hi_done, 1)
                                elif what == "q" and more == 2:
                                    cut_q(p, i + 1)
                                elif what == "o" and p == 1:
                                    act.wait_ge(v_used[0], i + 2)
                                    act.activation(oT[:, bass.ds(u - 1, 1), :], o[0][0:D, :].unsqueeze(1), ACT.Copy).then_inc(o_read[0], 1)

                        act.sem_inc(o_read[0], 1)
                        cut_q(0, 0)
                        cut_q(1, 0)
                        for h in range(G):
                            exp(0, h, 0, 0)
                        walk(act, step)

                    @block.vector
                    def _(dve):
                        def neg_max(p, h, half, u):
                            if h < G - 1:
                                dve.wait_ge(scored[h], u + 1)
                            else:
                                dve.wait_ge(qk_used[p], half + 2)
                            dve.tensor_reduce(nmax[:, p, h:h + 1], s[h][:, 0:KVLEN], AX.X, ALU.max, negate=True).then_inc(maxed, 1)

                        def invert(p, u):
                            dve.wait_ge(exped[G - 1], u + 1)
                            dve.reciprocal(rinv[:, bass.ds(u, 1), :], rsum[:, p:p + 1, :]).then_inc(inverted, 1)

                        def cut_k(p, half):
                            dve.wait_ge(qk_used[p], half + 1)
                            dve.wait_ge(qk_loaded[p], 48 * half + 48)
                            dve.tensor_copy(ks[:, p, 0, :], kr[:, p, :]).then_inc(k_hi[p], 1)

                        def keep_sums(i, u):
                            dve.wait_ge(v_used[1], i + 2)
                            dve.tensor_copy(oT[:, bass.ds(u, 1), :], o[1][0:D, :].unsqueeze(1)).then_inc(o_read[1], 1)

                        def step(i, p, more, first=False):
                            u = 2 * i + p
                            for what in DVE_ORDER:
                                x = int(what[1:] or 0)
                                if what[0] == "S" and more:
                                    neg_max(1 - p, x, i + p, u + 1)
                                elif what[0] == "T":
                                    dve.wait_ge(hi_done, KVT * u + x + 1)
                                    dve.tensor_tensor(pt_lo[0:ROWS[x], x, :], tb[x % 2][0:ROWS[x], :], f32(pt_hi[0:ROWS[x], x, :]),
                                                      ALU.subtract).then_inc(lo_done, 1)
                                    if x == 0:
                                        invert(p, u)
                                elif what == "k" and more == 2:
                                    cut_k(p, i + 1)
                                elif what == "o" and p == 0 and not first:
                                    keep_sums(i - 1, u - 1)

                        dve.sem_inc(o_read[1], 1)
                        cut_k(0, 0)
                        dve.wait_ge(k_hi[0], 1)
                        dve.tensor_tensor(ks[:, 0, 1, :], kr[:, 0, :], f32(ks[:, 0, 0, :]), ALU.subtract).then_inc(k_first, 1)
                        cut_k(1, 0)
                        for h in range(G):
                            neg_max(0, h, 0, 0)
                        walk(dve, step)
                        keep_sums(U // 2 - 1, U - 1)

        def out_project(tag, L, oT, rinv, wo, x_sb, gate, source=None):
            D, H = L.d, L.heads
            flip = not L.normed
            rT_d = scratch[L][3]
            NR = L.units * G // P
            NM = BANK // P
            o_v = oT[:].rearrange("d (b g) (h s) -> d b g h s", b=BATCH, h=G)
            with ExitStack() as st:
                rt = sb(st, f"{tag}_rt", [P, NR, QLEN])
                rb = sb(st, f"{tag}_rb", [D, 2, BATCH, QLEN])
                raw = sb(st, f"{tag}_raw", [P, 2, NM, D] if flip else [D, 2, BANK])
                w_hi = sb(st, f"{tag}_whi", [D, 2, BANK], F32R)
                w_lo = sb(st, f"{tag}_wlo", [D, 2, BANK], F32R)
                o_hi = sb(st, f"{tag}_ohi", [D, 2, TOKENS], F32R)
                o_lo = sb(st, f"{tag}_olo", [D, 2, TOKENS], F32R)
                y = [ps(st, f"{tag}_y{t}", [P, BANK]) for t in range(TT)]
                tb = ps(st, f"{tag}_tb", [P, BANK])
                x_loaded, r_turned, r_copied, r_stored = (sem(f"{tag}_{n}") for n in ("xl", "rturned", "rcopied", "rstored"))
                raw_loaded, r_loaded, o_normed, wt_done, wh_done, wl_done, oh_done, ol_done, used = (
                    [sem(f"{tag}_{n}{p}") for p in range(2)] for n in ("rawl", "rl", "on", "wt", "wh", "wl", "oh", "ol", "used"))
                y_ready, y_read = sem(f"{tag}_yready"), sem(f"{tag}_yread")

                def walk(eng, step):
                    for half in range(2):
                        def group(g, first, last):
                            for h in range(G):
                                step(half, g, h, half * (H // 2) + g * 2 + h // 2, first and h == 0, last and h == G - 1)
                        group(0, True, False)
                        if L.kvh > 2:
                            with eng.Fori(1, L.kvh - 1) as g:
                                group(g, False, False)
                        group(L.kvh - 1, False, True)

                with nc.Block() as block:
                    @block.sync
                    def _(sp):
                        def step(half, g, h, m, first, last):
                            p = h % 2
                            sp.wait_ge(wl_done[p], m)
                            if flip:
                                src = wo[half * BANK:(half + 1) * BANK, bass.ds((g * G + h) * D, D)].rearrange("(m p) d -> p m d", p=P)
                                sp.dma_start(raw[:, p, :, :], src).then_inc(raw_loaded[p], 16)
                            else:
                                sp.dma_start(raw[:, p, :], wo[bass.ds((g * G + h) * D, D), half * BANK:(half + 1) * BANK]).then_inc(raw_loaded[p], 16)
                            if half == 0:
                                if first:
                                    sp.wait_ge(r_copied, NR)
                                    sp.dma_start(rT_d.rearrange("b h s -> (b h) s").rearrange("(n p) s -> p n s", p=P), rt[:]).then_inc(r_stored, 16)
                                    sp.wait_ge(r_stored, 16)
                                sp.wait_ge(o_normed[p], m)
                                sp.dma_start(rb[:, p, :, :], rT_d[:, bass.ds(g * G + h, 1), :].rearrange("b o s -> o b s")
                                             .broadcast_to([D, BATCH, QLEN])).then_inc(r_loaded[p], 16)
                            if source is not None and half == 0 and h == G - 1 and not last:
                                assert L.kvh - 1 == TT
                                sp.dma_start(x_sb[:, bass.ds(g, 1), :], source[bass.ds(g * P, P), :].unsqueeze(1)).then_inc(x_loaded, 16)
                        walk(sp, step)

                    @block.gpsimd
                    def _(pool):
                        def step(half, g, h, m, first, last):
                            p = h % 2
                            if not flip:
                                pool.wait_ge(wh_done[p], m + 1)
                                pool.tensor_tensor(w_lo[:, p, :], raw[:, p, :], f32(w_hi[:, p, :]), ALU.subtract).then_inc(wl_done[p], 1)
                            if half == 0 and not first:
                                pool.wait_ge(oh_done[p], m + 1)
                                pool.tensor_tensor(o_lo[:, p, :].rearrange("d (b s) -> d b s", b=BATCH), o_v[:, :, g, h, :],
                                                   f32(o_hi[:, p, :]).rearrange("d (b s) -> d b s", b=BATCH), ALU.subtract).then_inc(ol_done[p], 1)
                        walk(pool, step)

                    @block.scalar
                    def _(act):
                        act.wait_ge(r_turned, NR)
                        for n in range(NR):
                            act.activation(rt[:, n, :], tb[:, n * P:n * P + QLEN], ACT.Copy).then_inc(r_copied, 1)

                        def step(half, g, h, m, first, last):
                            p = h % 2
                            act.wait_ge(used[p], m)
                            if flip:
                                act.wait_ge(wt_done[p], m + 1)
                                act.activation(w_hi[:, p, :], tb[0:D, :], ACT.Copy).then_inc(wh_done[p], 1)
                            else:
                                act.wait_ge(raw_loaded[p], 16 * m + 16)
                                act.activation(w_hi[:, p, :], raw[:, p, :], ACT.Copy).then_inc(wh_done[p], 1)
                            if half == 0:
                                act.wait_ge(o_normed[p], m + 1)
                            act.activation(o_hi[:, p, :].rearrange("d (b s) -> d b s", b=BATCH), o_v[:, :, g, h, :], ACT.Copy).then_inc(oh_done[p], 1)
                        walk(act, step)

                    @block.tensor
                    def _(pe):
                        for n in range(NR):
                            pe.transpose(tb[:, n * P:n * P + QLEN], rinv[:].rearrange("q u h -> q (u h)")[:, n * P:(n + 1) * P],
                                         ident[0:QLEN, 0:QLEN]).then_inc(r_turned, 1)
                        pe.wait_ge(r_copied, NR)

                        def turn(p, m):
                            pe.wait_ge(raw_loaded[p], 16 * m + 16)
                            for n in range(NM):
                                last = pe.transpose(tb[0:D, n * P:(n + 1) * P], raw[:, p, n, :], ident[:])
                            last.then_inc(wt_done[p], 1)

                        if flip:
                            turn(0, 0)

                        def step(half, g, h, m, first, last):
                            p = h % 2
                            pe.wait_ge(wl_done[p], m + 1)
                            if flip and not (half and last):
                                turn(1 - p, m + p)
                            pe.wait_ge(ol_done[p], m + 1)
                            for t in range(TT):
                                if first and half:
                                    pe.wait_ge(y_read, t + 1)
                                mm = product(pe, y[t][:], o_hi[:, p, t * P:(t + 1) * P], o_lo[:, p, t * P:(t + 1) * P],
                                             w_hi[:, p, :], w_lo[:, p, :], first, last)
                                if last and t < TT - 1:
                                    mm.then_inc(y_ready, 1)
                            mm.then_inc(used[p], 1)
                        walk(pe, step)

                    @block.vector
                    def _(dve):
                        def step(half, g, h, m, first, last):
                            p = h % 2
                            if half == 0:
                                dve.wait_ge(r_loaded[p], 16 * m + 16)
                                dve.tensor_tensor(o_v[:, :, g, h, :], o_v[:, :, g, h, :], rb[:, p, :, :], ALU.mult).then_inc(o_normed[p], 1)
                            if flip:
                                dve.wait_ge(wh_done[p], m + 1)
                                dve.tensor_tensor(w_lo[:, p, :], tb[0:D, :], f32(w_hi[:, p, :]), ALU.subtract).then_inc(wl_done[p], 1)
                            if half or first:
                                dve.wait_ge(oh_done[p], m + 1)
                                dve.tensor_tensor(o_lo[:, p, :].rearrange("d (b s) -> d b s", b=BATCH), o_v[:, :, g, h, :],
                                                  f32(o_hi[:, p, :]).rearrange("d (b s) -> d b s", b=BATCH), ALU.subtract).then_inc(ol_done[p], 1)
                            if last:
                                if source is not None:
                                    dve.wait_ge(x_loaded, 16 * TT)
                                for t in range(TT):
                                    if t < TT - 1:
                                        dve.wait_ge(y_ready, half * (TT - 1) + t + 1)
                                    else:
                                        dve.wait_ge(used[p], m + 1)
                                    cols = x_sb[:, t, half * BANK:(half + 1) * BANK]
                                    dve.scalar_tensor_tensor(out=cols, in0=y[t][:], scalar=gates[:, gate:gate + 1], in1=cols,
                                                             op0=ALU.mult, op1=ALU.add).then_inc(y_read, 1)
                        walk(dve, step)

        def scaled_ffn(x_sb):
            LIMIT = 448.0
            HALVES = HID // BANK
            SLABS = HALVES * KS
            with ExitStack() as st:
                xt = sb(st, "f0_xt", [P, KS, TOKENS])
                w = sb(st, "f0_w", [P, KS, HID])
                x_tops = sb(st, "f0_xtops", [P, TT])
                w_tops = sb(st, "f0_wtops", [P, KS])
                most = sb(st, "f0_most", [P, 2])
                scl = sb(st, "f0_scl", [P, 3])
                loaded = [sem(f"f0_loaded{k}") for k in range(KS)]
                topped = sem("f0_topped")
                with ExitStack() as st2:
                    xn = sb(st2, "f0_xn", [P, TT, HID])
                    layer_norm("f0_ln", x_sb, xn, preload=[(w[:, k, :], wffn0[k * P:(k + 1) * P, :], loaded[k]) for k in range(KS)],
                               xt=xt, tops=(w, loaded, x_tops, w_tops, topped))
                xt_hi = sb(st, "f0_xthi", [P, KS, TOKENS], F32R)
                xt_lo = sb(st, "f0_xtlo", [P, KS, TOKENS], F32R)
                w_hi = sb(st, "f0_whi", [P, KS, BANK], F32R)
                w_lo = sb(st, "f0_wlo", [P, KS, BANK], F32R)
                y = [ps(st, f"f0_y{n}", [P, BANK]) for n in range(8)]
                names = ("maxed", "reduced", "chain", "xsc", "xcl", "xhi", "xlo", "wsc", "wcl", "whi", "wlo", "used", "yready", "yread")
                maxed, reduced, chain, x_scaled, x_clipped, x_hi_s, x_lo_s, w_scaled, w_clipped, w_hi_s, w_lo_s, used, y_ready, y_read = (
                    sem("f0_" + name) for name in names)

                def w_slab(j):
                    return w[:, j % KS, j // KS * BANK:(j // KS + 1) * BANK]

                with nc.Block() as block:
                    @block.gpsimd
                    def _(pool):
                        pool.wait_ge(maxed, 2)
                        pool.partition_all_reduce(most[:], most[:], P, bass.bass_isa.ReduceOp.max).then_inc(reduced, 1)
                        for j in range(SLABS):
                            pool.wait_ge(w_hi_s, j + 1)
                            pool.tensor_tensor(w_lo[:, j % KS, :], w_slab(j), f32(w_hi[:, j % KS, :]), ALU.subtract).then_inc(w_lo_s, 1)

                    @block.scalar
                    def _(act):
                        act.wait_ge(chain, 3)
                        for j in range(SLABS + 1):
                            if 1 <= j <= KS:
                                act.wait_ge(x_clipped, j)
                                act.activation(xt_hi[:, j - 1, :], xt[:, j - 1, :], ACT.Copy).then_inc(x_hi_s, 1)
                            if j:
                                act.wait_ge(w_clipped, j)
                                if j > KS:
                                    act.wait_ge(used, j - KS)
                                act.activation(w_hi[:, (j - 1) % KS, :], w_slab(j - 1), ACT.Copy).then_inc(w_hi_s, 1)
                            if j < KS:
                                act.activation(xt[:, j, :], xt[:, j, :], ACT.Copy, scale=scl[:, 0:1]).then_inc(x_scaled, 1)
                            if j < SLABS:
                                act.activation(w_slab(j), w_slab(j), ACT.Copy, scale=scl[:, 1:2]).then_inc(w_scaled, 1)

                    @block.vector
                    def _(dve):
                        dve.wait_ge(topped, TT + KS)
                        dve.tensor_reduce(most[:, 0:1], x_tops[:], AX.X, ALU.max).then_inc(maxed, 1)
                        dve.tensor_reduce(most[:, 1:2], w_tops[:], AX.X, ALU.max).then_inc(maxed, 1)
                        dve.wait_ge(reduced, 1)
                        dve.tensor_scalar(scl[:, 0:2], most[:], 1e-12, None, ALU.max).then_inc(chain, 1)
                        dve.wait_ge(chain, 1)
                        dve.reciprocal(scl[:, 0:2], scl[:, 0:2]).then_inc(chain, 1)
                        dve.wait_ge(chain, 2)
                        dve.tensor_scalar(scl[:, 0:2], scl[:, 0:2], LIMIT, None, ALU.mult).then_inc(chain, 1)
                        dve.wait_ge(chain, 3)
                        dve.tensor_tensor(scl[:, 2:3], scl[:, 0:1], scl[:, 1:2], ALU.mult).then_inc(chain, 1)
                        dve.wait_ge(chain, 4)
                        dve.reciprocal(scl[:, 2:3], scl[:, 2:3]).then_inc(chain, 1)
                        dve.wait_ge(chain, 5)
                        dve.tensor_tensor(scl[:, 2:3], scl[:, 2:3], gates[:, 2:3], ALU.mult).then_inc(chain, 1)
                        for j in range(SLABS):
                            if j < KS:
                                dve.wait_ge(x_scaled, j + 1)
                                dve.tensor_scalar(xt[:, j, :], xt[:, j, :], LIMIT, -LIMIT, ALU.min, ALU.max).then_inc(x_clipped, 1)
                            dve.wait_ge(w_scaled, j + 1)
                            dve.tensor_scalar(w_slab(j), w_slab(j), LIMIT, -LIMIT, ALU.min, ALU.max).then_inc(w_clipped, 1)
                            if j < KS:
                                dve.wait_ge(x_hi_s, j + 1)
                                dve.tensor_tensor(xt_lo[:, j, :], xt[:, j, :], f32(xt_hi[:, j, :]), ALU.subtract).then_inc(x_lo_s, 1)
                        dve.wait_ge(chain, 6)
                        for n in range(HALVES * TT):
                            half, t = n // TT, n % TT
                            if t < TT - 1:
                                dve.wait_ge(y_ready, half * (TT - 1) + t + 1)
                            else:
                                dve.wait_ge(used, (half + 1) * KS)
                            cols = x_sb[:, t, half * BANK:(half + 1) * BANK]
                            dve.scalar_tensor_tensor(out=cols, in0=y[n % 8][:], scalar=scl[:, 2:3], in1=cols,
                                                     op0=ALU.mult, op1=ALU.add).then_inc(y_read, 1)

                    @block.tensor
                    def _(pe):
                        for half in range(HALVES):
                            for k in range(KS):
                                if half == 0:
                                    pe.wait_ge(x_lo_s, k + 1)
                                pe.wait_ge(w_lo_s, half * KS + k + 1)
                                for t in range(TT):
                                    n = half * TT + t
                                    if k == 0 and n >= 8:
                                        pe.wait_ge(y_read, n - 7)
                                    mm = product(pe, y[n % 8][:], xt_hi[:, k, t * P:(t + 1) * P], xt_lo[:, k, t * P:(t + 1) * P],
                                                 w_hi[:, k, :], w_lo[:, k, :], k == 0, k == KS - 1)
                                    if k == KS - 1 and t < TT - 1:
                                        mm.then_inc(y_ready, 1)
                                mm.then_inc(used, 1)

        def routed_lora(x_sb):
            EX, RANK = 8, 16
            ER = EX * RANK
            NW = EX + ER
            FACTOR = 2.0 * EX
            with ExitStack() as st:
                xt_hi = sb(st, "f1_xthi", [P, KS, TOKENS], F32R)
                xt_lo = sb(st, "f1_xtlo", [P, KS, TOKENS], F32R)
                a_rows = sb(st, "f1_arows", [ER, HID])
                r_rows = sb(st, "f1_rrows", [EX, HID])
                b_rows = sb(st, "f1_brows", [P, KS, EX, RANK])
                loaded = sem("f1_loaded")
                with ExitStack() as st2:
                    xn = sb(st2, "f1_xn", [P, TT, HID])
                    layer_norm("f1_ln", x_sb, xn, xt_hi, xt_lo, preload=[
                        (a_rows[:], a1.rearrange("h r d -> (h r) d"), loaded), (r_rows[:], wr1, loaded)] + [
                        (b_rows[:, :, e, :], b1[e].rearrange("(m p) r -> p m r", p=P), loaded) for e in range(EX)])
                wra_hi = sb(st, "f1_wrahi", [P, KS, NW], F32R)
                wra_lo = sb(st, "f1_wralo", [P, KS, NW], F32R)
                wb_hi = sb(st, "f1_wbhi", [P, HID], F32R)
                wb_lo = sb(st, "f1_wblo", [P, HID], F32R)
                logit_t = sb(st, "f1_logitt", [EX, TOKENS])
                logit = sb(st, "f1_logit", [P, TT, EX])
                nmax = sb(st, "f1_nmax", [P, TT])
                tot = sb(st, "f1_tot", [P, TT])
                score = sb(st, "f1_score", [P, TT, EX])
                spread = sb(st, "f1_spread", [P, TT, ER])
                score_t = sb(st, "f1_scoret", [P, TOKENS])
                low = sb(st, "f1_low", [P, TOKENS])
                low_hi = sb(st, "f1_lowhi", [P, TOKENS], F32R)
                low_lo = sb(st, "f1_lowlo", [P, TOKENS], F32R)
                rb = [ps(st, f"f1_rb{n}", [P, BANK]) for n in range(2)]
                ab = [ps(st, f"f1_ab{n}", [P, BANK]) for n in range(2)]
                yo = [ps(st, f"f1_yo{n}", [P, BANK]) for n in range(4)]
                names = ("wturned", "whi", "wlo", "rready", "rcopied", "lturned", "chain", "exped", "spread_s", "aready",
                         "sturned", "scopied", "low_s", "lowhi_s", "lowlo_s", "oready", "added", "stored")
                (w_turned, whi, wlo, r_ready, r_copied, l_turned, chain, exped, spread_s, a_ready,
                 s_turned, s_copied, low_s, low_hi_s, low_lo_s, o_ready, added, stored) = (sem("f1_" + n) for n in names)
                GROUPS = [(range(0, G), slice(0, G * P)), (range(G, TT), slice(G * P, TOKENS))]

                def bank(b, g):
                    return b[:, 0:len(GROUPS[g][0]) * P]

                with nc.Block() as block:
                    @block.sync
                    def _(sp):
                        for t in range(TT):
                            sp.wait_ge(added, 2 * t + 2)
                            sp.dma_start(out_rows[t * P:(t + 1) * P, :], x_sb[:, t, :]).then_inc(stored, 16)
                        sp.wait_ge(stored, 16 * TT)

                    @block.tensor
                    def _(pe):
                        def up(out, cols, tokens):
                            for k in range(KS):
                                mm = product(pe, out, wra_hi[:, k, cols], wra_lo[:, k, cols],
                                             xt_hi[:, k, tokens], xt_lo[:, k, tokens], k == 0, k == KS - 1)
                            return mm

                        pe.wait_ge(loaded, 16 * (2 + EX))
                        for k in range(KS):
                            if k >= 4:
                                pe.wait_ge(wlo, k - 3)
                            pe.transpose(yo[k % 4][:, 0:EX], r_rows[:, k * P:(k + 1) * P], ident[0:EX, 0:EX])
                            pe.transpose(yo[k % 4][:, EX:NW], a_rows[:, k * P:(k + 1) * P], ident[:]).then_inc(w_turned, 1)
                        pe.wait_ge(wlo, KS)
                        for g, (tiles, tokens) in enumerate(GROUPS):
                            up(bank(rb[g], g)[0:EX], slice(0, EX), tokens).then_inc(r_ready, 1)
                        for c in range(2):
                            for m in range(G):
                                last = pe.transpose(yo[c][:, m * P:(m + 1) * P], b_rows[:, G * c + m, :, :].rearrange("p e r -> p (e r)"), ident[:])
                            last.then_inc(w_turned, 1)
                        for g, (tiles, tokens) in enumerate(GROUPS):
                            up(bank(ab[g], g), slice(EX, NW), tokens).then_inc(a_ready, 1)
                            if g == 0:
                                pe.wait_ge(r_copied, 2)
                                for t in range(TT):
                                    last = pe.transpose(rb[0][:, t * EX:(t + 1) * EX], logit_t[:, t * P:(t + 1) * P], ident[0:EX, 0:EX])
                                last.then_inc(l_turned, 1)
                        pe.wait_ge(spread_s, 1)
                        for g, (tiles, tokens) in enumerate(GROUPS):
                            for t in tiles:
                                last = pe.transpose(yo[2 + g][:, (t % G) * P:(t % G + 1) * P], spread[:, t, :], ident[:])
                            last.then_inc(s_turned, 1)
                        pe.wait_ge(wlo, KS + 2)
                        for g, (tiles, tokens) in enumerate(GROUPS):
                            pe.wait_ge(low_lo_s, g + 1)
                            for t in tiles:
                                for c in range(2):
                                    n = 2 * t + c
                                    if n in (2, 3):
                                        pe.wait_ge(s_copied, n - 1)
                                    if n >= 4:
                                        pe.wait_ge(added, n - 3)
                                    product(pe, yo[n % 4][:], low_hi[:, t * P:(t + 1) * P], low_lo[:, t * P:(t + 1) * P],
                                            wb_hi[:, c * BANK:(c + 1) * BANK], wb_lo[:, c * BANK:(c + 1) * BANK], True, True).then_inc(o_ready, 1)

                    @block.scalar
                    def _(act):
                        for k in range(KS):
                            act.wait_ge(w_turned, k + 1)
                            act.activation(wra_hi[:, k, :], yo[k % 4][:, 0:NW], ACT.Copy).then_inc(whi, 1)
                        for g, (tiles, tokens) in enumerate(GROUPS):
                            act.wait_ge(r_ready, g + 1)
                            act.activation(logit_t[:, tokens], bank(rb[g], g)[0:EX], ACT.Copy).then_inc(r_copied, 1)
                        for c in range(2):
                            act.wait_ge(w_turned, KS + c + 1)
                            act.activation(wb_hi[:, c * BANK:(c + 1) * BANK], yo[c][:], ACT.Copy).then_inc(whi, 1)
                        act.wait_ge(chain, 3)
                        act.activation(score[:], logit[:], ACT.Exp).then_inc(exped, 1)
                        for g, (tiles, tokens) in enumerate(GROUPS):
                            act.wait_ge(s_turned, g + 1)
                            act.activation(score_t[:, tokens], bank(yo[2 + g], g), ACT.Copy).then_inc(s_copied, 1)
                        for g, (tiles, tokens) in enumerate(GROUPS):
                            act.wait_ge(low_s, g + 1)
                            act.activation(low_hi[:, tokens], low[:, tokens], ACT.Copy).then_inc(low_hi_s, 1)

                    @block.vector
                    def _(dve):
                        for k in range(KS):
                            dve.wait_ge(whi, k + 1)
                            dve.tensor_tensor(wra_lo[:, k, :], yo[k % 4][:, 0:NW], f32(wra_hi[:, k, :]), ALU.subtract).then_inc(wlo, 1)
                        for c in range(2):
                            dve.wait_ge(whi, KS + c + 1)
                            dve.tensor_tensor(wb_lo[:, c * BANK:(c + 1) * BANK], yo[c][:], f32(wb_hi[:, c * BANK:(c + 1) * BANK]),
                                              ALU.subtract).then_inc(wlo, 1)
                        shape = [P, TT, EX]
                        dve.wait_ge(l_turned, 1)
                        dve.tensor_tensor(logit[:], rb[0][:, 0:TT * EX].rearrange("p (t e) -> p t e", e=EX),
                                          brb[:].unsqueeze(1).broadcast_to(shape), ALU.add).then_inc(chain, 1)
                        dve.wait_ge(chain, 1)
                        dve.tensor_reduce(nmax[:], logit[:], AX.X, ALU.max, negate=True).then_inc(chain, 1)
                        dve.wait_ge(chain, 2)
                        dve.tensor_tensor(logit[:], logit[:], nmax[:].unsqueeze(2).broadcast_to(shape), ALU.add).then_inc(chain, 1)
                        dve.wait_ge(exped, 1)
                        dve.tensor_reduce(tot[:], score[:], AX.X, ALU.add).then_inc(chain, 1)
                        dve.wait_ge(chain, 4)
                        dve.reciprocal(tot[:], tot[:]).then_inc(chain, 1)
                        dve.wait_ge(chain, 5)
                        dve.tensor_scalar(tot[:], tot[:], FACTOR, None, ALU.mult).then_inc(chain, 1)
                        dve.wait_ge(chain, 6)
                        dve.tensor_tensor(score[:], score[:], tot[:].unsqueeze(2).broadcast_to(shape), ALU.mult).then_inc(chain, 1)
                        dve.wait_ge(chain, 7)
                        dve.tensor_copy(spread[:].rearrange("p t (e r) -> p (t e) r", e=EX),
                                        score[:].rearrange("p t e -> p (t e)").unsqueeze(2).broadcast_to([P, TT * EX, RANK])).then_inc(spread_s, 1)
                        for g, (tiles, tokens) in enumerate(GROUPS):
                            dve.wait_ge(a_ready, g + 1)
                            dve.wait_ge(s_copied, g + 1)
                            dve.tensor_tensor(low[:, tokens], bank(ab[g], g), score_t[:, tokens], ALU.mult).then_inc(low_s, 1)
                        for g, (tiles, tokens) in enumerate(GROUPS):
                            dve.wait_ge(low_hi_s, g + 1)
                            dve.tensor_tensor(low_lo[:, tokens], low[:, tokens], f32(low_hi[:, tokens]), ALU.subtract).then_inc(low_lo_s, 1)
                        for n in range(2 * TT):
                            t, c = n // 2, n % 2
                            dve.wait_ge(o_ready, n + 1)
                            cols = x_sb[:, t, c * BANK:(c + 1) * BANK]
                            dve.scalar_tensor_tensor(out=cols, in0=yo[n % 4][:], scalar=gates[:, 3:4], in1=cols,
                                                     op0=ALU.mult, op1=ALU.add).then_inc(added, 1)

        def attend(n, L, x_sb, wo, source=None):
            with ExitStack() as st:
                oT = sb(st, f"oT{n}", [L.d, L.units, G * QLEN])
                rinv = sb(st, f"rinv{n}", [QLEN, L.units, G])
                attention(f"at{n}", L, oT, rinv)
                next_stage()
                out_project(f"o{n}", L, oT, rinv, wo, x_sb, n, source=source)
                next_stage()

        def project(n, L, wq, wk, wv, x_sb=None, source=None):
            flip = not L.normed
            of_q, of_k, of_v = (chunk_of(w, L, flip) for w in (wq, wk, wv))

            def latents_chunk(c):
                if isinstance(c, int) and c >= L.kvh:
                    return (of_k, of_v)[(c - L.kvh) // L.nkc]((c - L.kvh) % L.nkc)
                return of_q(c)

            def context_chunk(c):
                return (of_k, of_v)[c // L.nkc](c % L.nkc)

            def rows(i, j):
                return ctx_rows[bass.ds(i * (PT * CR) + j * CR, CR), :]

            with ExitStack() as st:
                Wc = Weights(f"kv{n}", st, L, context_chunk, flip, bufs=2)
                xin = sb(st, f"kv{n}_xin", [P, 2, HID])
                x_loaded = [sem(f"kv{n}_xl{p}") for p in range(2)]
                with ExitStack() as st1:
                    Wl = Weights(f"q{n}", st1, L, latents_chunk, flip)
                    xt_hi = sb(st1, f"xthi{n}", [P, KS, TOKENS], F32R)
                    xt_lo = sb(st1, f"xtlo{n}", [P, KS, TOKENS], F32R)
                    with ExitStack() as st2:
                        x_in = x_sb if x_sb is not None else sb(st2, f"x_rows{n}", [P, TT, HID])
                        xn = sb(st2, f"xn{n}", [P, TT, HID])
                        if source is None:
                            layer_norm(f"a{n}_ln", x_in, xn, xt_hi, xt_lo, preload=[Wl.ahead(0)])
                        else:
                            rows_loaded = [sem(f"x_loaded{t}") for t in range(TT)]
                            constants([(x_in[:, t, :], source[t * P:(t + 1) * P, :], rows_loaded[t]) for t in range(TT)] + [Wl.ahead(0)])
                            layer_norm(f"a{n}_ln", x_in, xn, xt_hi, xt_lo, x_loaded=rows_loaded)
                    latents(f"q{n}", L, xt_hi, xt_lo, Wl,
                            [(xin[0:CR, j, :], rows(0, j), x_loaded[j]) for j in range(2)] + [Wc.ahead(0), Wc.ahead(1)])
                context(f"kv{n}", L, Wc, xin, x_loaded, rows)
                next_stage()

        project(0, L0, wq0, wk0, wv0, source=x_rows)
        x_sb = sb(stack, "x_sb", [P, TT, HID])
        attend(0, L0, x_sb, wo0, source=x_rows)
        scaled_ffn(x_sb)
        next_stage()
        project(1, L1, wq1, wk1, wv1, x_sb=x_sb)
        attend(1, L1, x_sb, wo1)
        routed_lora(x_sb)


_INS = ["x", "ctx_4096", "g_xattn", "g_ffn", "L0_xattn_Wq", "L0_xattn_Wk", "L0_xattn_Wv", "L0_xattn_Wo",
        "L0_xattn_q_norm_w", "L0_xattn_k_norm_w", "L0_ffn_weight", "L1_xattn_Wq", "L1_xattn_Wk", "L1_xattn_Wv",
        "L1_xattn_Wo", "L1_ffn_A", "L1_ffn_B", "L1_ffn_Wr", "L1_ffn_br"]


def kernel(**inputs):
    import numpy as _np
    import concourse.bacc as _bacc
    from concourse import mybir as _mybir
    from concourse.bass_utils import run_bass_kernel_spmd as _run

    nc = _bacc.Bacc("TRN2", target_bir_lowering=False, num_devices=1)
    arrays, args = {}, []
    for name in _INS:
        a = _np.ascontiguousarray(inputs[name])
        arrays[f"in_{name}_dram"] = a
        args.append(nc.dram_tensor(f"in_{name}_dram", a.shape, _mybir.dt.from_np(a.dtype), kind="ExternalInput").ap())
    args.append(nc.dram_tensor("out_0_dram", (BATCH, QLEN, HID), _mybir.dt.float32, kind="ExternalOutput").ap())
    flamingo(nc, *args)
    r = _run(nc, [arrays], core_ids=[0])
    return r.results[0]["out_0_dram"]
```
